# Optimizing a Trainium2 kernel written in Bass

```python
import numpy as np
import jax
import jax.numpy as jnp

def _softmax(x, axis=-1):
    return jax.nn.softmax(x, axis=axis)

def _gelu(x):
    return jax.nn.gelu(x, approximate=True)

def _silu(x):
    return jax.nn.silu(x)

def _sigmoid(x):
    return jax.nn.sigmoid(x)

def _layernorm(x, axis=-1, eps=1e-05):
    m = jnp.mean(x, axis=axis, keepdims=True)
    v = jnp.var(x, axis=axis, keepdims=True)
    return (x - m) / jnp.sqrt(v + eps)

def _scatter_add(tgt, idx, src, axis=0):
    return tgt.at[idx].add(src)

def _segment_sum(src, seg, n):
    return jax.ops.segment_sum(src, seg, n)
kernel_name = 'mk_gnn_resnorm_d2_gnn_r8_e5a633'

def setup_inputs(seed: int=0):
    np.random.seed(seed)
    _w = jnp.asarray

    def _rec_inputs():
        import jax
        import jax.numpy as jnp
        _gk = jax.random.key(seed)
        x = -0.0006008 + 1.001 * jax.random.normal(jax.random.fold_in(_gk, 1), (6250, 256), jnp.float32)
        src = jax.random.randint(jax.random.fold_in(_gk, 2), (100000,), 0, 6250, jnp.int32)
        dst = jnp.minimum((6250 * jax.random.uniform(jax.random.fold_in(_gk, 3), (100000,)) ** 2.0).astype(jnp.int32), 49999)
        _o = jnp.argsort(dst, stable=True)
        src = src[_o]
        dst = dst[_o]
        return (x, src, dst)
    x, src, dst = _rec_inputs()

    def _L0_gnn_setup():
        import jax, jax.numpy as jnp
        import numpy as np
        N_NODES = 1250
        N_EDGES = 40000
        D_IN = 256
        D_OUT = 256
        key = jax.random.key(seed)
        k1, k2, k3, k4 = jax.random.split(key, 4)
        x = jax.random.normal(k1, (N_NODES, D_IN), dtype=jnp.float32)
        edge_index = jax.random.randint(k2, (2, N_EDGES), 0, N_NODES, dtype=jnp.int64)
        weight = jax.random.normal(k3, (2 * D_IN, D_OUT), dtype=jnp.float32) / np.sqrt(2 * D_IN)
        bias = jax.random.normal(k4, (D_OUT,), dtype=jnp.float32)
        return {'x': x, 'edge_index': edge_index, 'weight': weight, 'bias': bias}
    _L0_gnn_all = _L0_gnn_setup()
    _L0_gnn_in = {k: v for k, v in _L0_gnn_all.items() if k in ('weight', 'bias')}
    del _L0_gnn_all

    def _L1_gnn_setup():
        import jax, jax.numpy as jnp
        import numpy as np
        N_NODES = 2048
        N_EDGES = 32768
        D_IN = 256
        D = 256
        H = 512
        E = 64
        TOP_K = 2
        CAP = 1024
        BN_EPS = 1e-05

        def _moe_ff(x, Wg, bg, w1, b1, w2, b2):
            N = x.shape[0]
            logits = x @ Wg + bg
            vals, idx = jax.lax.top_k(logits, TOP_K)
            gates = jax.nn.softmax(vals, axis=-1)
            e_flat = idx.reshape(-1)
            g_flat = gates.reshape(-1)
            tok = jnp.arange(N * TOP_K) // TOP_K
            order = jnp.argsort(e_flat)
            e_s, tok_s, g_s = (e_flat[order], tok[order], g_flat[order])
            counts = jnp.bincount(e_flat, length=E)
            offs = jnp.concatenate([jnp.zeros((1,), counts.dtype), jnp.cumsum(counts)[:-1]])
            rank = jnp.arange(N * TOP_K) - offs[e_s]
            valid = rank < CAP
            slot = jnp.where(valid, e_s * CAP + rank, E * CAP)
            buf = jnp.zeros((E * CAP + 1, D), x.dtype).at[slot].set(x[tok_s])
            h = buf[:E * CAP].reshape(E, CAP, D)
            h1 = jax.nn.gelu(jnp.einsum('ecd,edh->ech', h, w1) + b1[:, None, :], approximate=False)
            h2 = jnp.einsum('ech,ehd->ecd', h1, w2) + b2[:, None, :]
            out_buf = h2.reshape(E * CAP, D)
            y_s = jnp.where(valid[:, None], out_buf[jnp.minimum(slot, E * CAP - 1)], 0.0)
            return jnp.zeros((N, D), x.dtype).at[tok_s].add(g_s[:, None] * y_s)

        def _forward(feats, W_gc, b_gc, W_res, b_res, Wg, bg, w1, b1, w2, b2, gamma, beta, src, dst):
            n = feats.shape[0]
            ones = jnp.ones((src.shape[0],), feats.dtype)
            deg_out = jnp.clip(jax.ops.segment_sum(ones, src, num_segments=n), 1.0)
            deg_in = jnp.clip(jax.ops.segment_sum(ones, dst, num_segments=n), 1.0)
            h = feats * jax.lax.rsqrt(deg_out)[:, None]
            m = jax.ops.segment_sum(h[src], dst, num_segments=n) * jax.lax.rsqrt(deg_in)[:, None]
            gc = m @ W_gc + b_gc
            x = gc + (feats @ W_res + b_res)
            core = _moe_ff(x, Wg, bg, w1, b1, w2, b2)
            y = x + core
            mean = jnp.mean(y, axis=0)
            var = jnp.mean((y - mean) ** 2, axis=0)
            return (y - mean) * jax.lax.rsqrt(var + BN_EPS) * gamma + beta
        key = jax.random.key(seed)
        ks = jax.random.split(key, 16)
        s = lambda d: 1.0 / np.sqrt(d)
        inp = {'feats': jax.random.normal(ks[0], (N_NODES, D_IN), jnp.float32), 'W_gc': jax.random.normal(ks[1], (D_IN, D), jnp.float32) * s(D_IN), 'b_gc': jnp.zeros((D,), jnp.float32), 'W_res': jax.random.normal(ks[2], (D_IN, D), jnp.float32) * s(D_IN), 'b_res': jnp.zeros((D,), jnp.float32), 'Wg': jax.random.normal(ks[3], (D, E), jnp.float32) * s(D), 'bg': jnp.zeros((E,), jnp.float32), 'w1': jax.random.normal(ks[4], (E, D, H), jnp.float32) * s(D), 'b1': jnp.zeros((E, H), jnp.float32), 'w2': jax.random.normal(ks[5], (E, H, D), jnp.float32) * s(H), 'b2': jnp.zeros((E, D), jnp.float32), 'gamma': jnp.ones((D,), jnp.float32), 'beta': jnp.zeros((D,), jnp.float32), 'src': jax.random.randint(ks[6], (N_EDGES,), 0, N_NODES), 'dst': jax.random.randint(ks[7], (N_EDGES,), 0, N_NODES)}
        return inp
    _L1_gnn_all = _L1_gnn_setup()
    _L1_gnn_in = {k: v for k, v in _L1_gnn_all.items() if k in ('W_gc', 'b_gc', 'W_res', 'b_res', 'Wg', 'bg', 'w1', 'b1', 'w2', 'b2', 'gamma', 'beta')}
    del _L1_gnn_all
    return {'x': x, 'src': src, 'dst': dst, 'L0_gnn_weight': _L0_gnn_in['weight'], 'L0_gnn_bias': _L0_gnn_in['bias'], 'L1_gnn_W_gc': _L1_gnn_in['W_gc'], 'L1_gnn_b_gc': _L1_gnn_in['b_gc'], 'L1_gnn_W_res': _L1_gnn_in['W_res'], 'L1_gnn_b_res': _L1_gnn_in['b_res'], 'L1_gnn_Wg': _L1_gnn_in['Wg'], 'L1_gnn_bg': _L1_gnn_in['bg'], 'L1_gnn_w1': _L1_gnn_in['w1'], 'L1_gnn_b1': _L1_gnn_in['b1'], 'L1_gnn_w2': _L1_gnn_in['w2'], 'L1_gnn_b2': _L1_gnn_in['b2'], 'L1_gnn_gamma': _L1_gnn_in['gamma'], 'L1_gnn_beta': _L1_gnn_in['beta']}

def reference(x, src, dst, L0_gnn_weight, L0_gnn_bias, L1_gnn_W_gc, L1_gnn_b_gc, L1_gnn_W_res, L1_gnn_b_res, L1_gnn_Wg, L1_gnn_bg, L1_gnn_w1, L1_gnn_b1, L1_gnn_w2, L1_gnn_b2, L1_gnn_gamma, L1_gnn_beta):
    import jax
    import jax.numpy as jnp

    def _L0_gnn_ref(x, edge_index, weight, bias):
        import jax, jax.numpy as jnp
        import numpy as np
        N_NODES = 1250
        N_EDGES = 40000
        D_IN = 256
        D_OUT = 256
        n = x.shape[0]
        src, dst = (edge_index[0], edge_index[1])
        summed = jax.ops.segment_sum(x[src], dst, num_segments=n)
        deg = jax.ops.segment_sum(jnp.ones_like(src, dtype=x.dtype), dst, num_segments=n)
        agg = summed / jnp.maximum(deg, 1.0)[:, None]
        out = jnp.concatenate([x, agg], axis=-1) @ weight
        out = out / jnp.linalg.norm(out, axis=-1, keepdims=True)
        return out + bias

    def _L1_gnn_ref(feats, W_gc, b_gc, W_res, b_res, Wg, bg, w1, b1, w2, b2, gamma, beta, src, dst):
        import jax, jax.numpy as jnp
        import numpy as np
        N_NODES = 2048
        N_EDGES = 32768
        D_IN = 256
        D = 256
        H = 512
        E = 64
        TOP_K = 2
        CAP = 1024
        BN_EPS = 1e-05

        def _moe_ff(x, Wg, bg, w1, b1, w2, b2):
            N = x.shape[0]
            logits = x @ Wg + bg
            vals, idx = jax.lax.top_k(logits, TOP_K)
            gates = jax.nn.softmax(vals, axis=-1)
            e_flat = idx.reshape(-1)
            g_flat = gates.reshape(-1)
            tok = jnp.arange(N * TOP_K) // TOP_K
            order = jnp.argsort(e_flat)
            e_s, tok_s, g_s = (e_flat[order], tok[order], g_flat[order])
            counts = jnp.bincount(e_flat, length=E)
            offs = jnp.concatenate([jnp.zeros((1,), counts.dtype), jnp.cumsum(counts)[:-1]])
            rank = jnp.arange(N * TOP_K) - offs[e_s]
            valid = rank < CAP
            slot = jnp.where(valid, e_s * CAP + rank, E * CAP)
            buf = jnp.zeros((E * CAP + 1, D), x.dtype).at[slot].set(x[tok_s])
            h = buf[:E * CAP].reshape(E, CAP, D)
            h1 = jax.nn.gelu(jnp.einsum('ecd,edh->ech', h, w1) + b1[:, None, :], approximate=False)
            h2 = jnp.einsum('ech,ehd->ecd', h1, w2) + b2[:, None, :]
            out_buf = h2.reshape(E * CAP, D)
            y_s = jnp.where(valid[:, None], out_buf[jnp.minimum(slot, E * CAP - 1)], 0.0)
            return jnp.zeros((N, D), x.dtype).at[tok_s].add(g_s[:, None] * y_s)

        def _forward(feats, W_gc, b_gc, W_res, b_res, Wg, bg, w1, b1, w2, b2, gamma, beta, src, dst):
            n = feats.shape[0]
            ones = jnp.ones((src.shape[0],), feats.dtype)
            deg_out = jnp.clip(jax.ops.segment_sum(ones, src, num_segments=n), 1.0)
            deg_in = jnp.clip(jax.ops.segment_sum(ones, dst, num_segments=n), 1.0)
            h = feats * jax.lax.rsqrt(deg_out)[:, None]
            m = jax.ops.segment_sum(h[src], dst, num_segments=n) * jax.lax.rsqrt(deg_in)[:, None]
            gc = m @ W_gc + b_gc
            x = gc + (feats @ W_res + b_res)
            core = _moe_ff(x, Wg, bg, w1, b1, w2, b2)
            y = x + core
            mean = jnp.mean(y, axis=0)
            var = jnp.mean((y - mean) ** 2, axis=0)
            return (y - mean) * jax.lax.rsqrt(var + BN_EPS) * gamma + beta
        return _forward(feats, W_gc, b_gc, W_res, b_res, Wg, bg, w1, b1, w2, b2, gamma, beta, src, dst)
    edge_index = jnp.stack([src, dst])
    x = _layernorm(x + _L0_gnn_ref(x, edge_index, L0_gnn_weight, L0_gnn_bias), axis=-1)
    x = _layernorm(x + _L1_gnn_ref(x, L1_gnn_W_gc, L1_gnn_b_gc, L1_gnn_W_res, L1_gnn_b_res, L1_gnn_Wg, L1_gnn_bg, L1_gnn_w1, L1_gnn_b1, L1_gnn_w2, L1_gnn_b2, L1_gnn_gamma, L1_gnn_beta, src, dst), axis=-1)
    return x

_drawn_inputs = setup_inputs


def setup_inputs(seed=0):
    import zlib

    import numpy as np

    out = dict(_drawn_inputs(seed))
    spreads = {'L1_gnn_b_gc': (0.0, 0.1),
     'L1_gnn_b_res': (0.0, 0.1),
     'L1_gnn_bg': (0.0, 0.1),
     'L1_gnn_b1': (0.0, 0.292),
     'L1_gnn_b2': (0.0, 0.1),
     'L1_gnn_gamma': (1.0, 0.2),
     'L1_gnn_beta': (0.0, 0.1)}
    factors = {}
    for name, (base, spread) in spreads.items():
        noise = np.random.default_rng([zlib.crc32(name.encode()), seed]).standard_normal(out[name].shape)
        drawn = base * np.exp(spread * noise) if base else spread * noise
        out[name] = jnp.asarray(drawn.astype(out[name].dtype))
    for name, factor in factors.items():
        out[name] = (out[name] * factor).astype(out[name].dtype)
    return out
```

```python
from contextlib import ExitStack

import concourse.bass as bass
from concourse import mybir

F32 = mybir.dt.float32
BF16 = mybir.dt.bfloat16
I32 = mybir.dt.int32
I16 = mybir.dt.int16
U32 = mybir.dt.uint32
ALU = mybir.AluOpType
ACT = mybir.ActivationFunctionType
AX = mybir.AxisListType.X

P = 128
ROW_PAIR = 2 * P
WIN = 64
GROUP = 8
PAIRS = GROUP // 2
PAD = 8191
LN_EPS = 1e-5
BN_EPS = 1e-5
CAP = 1024
OVER = 1 << 20


def ds(start, size):
    return slice(start, start + size) if isinstance(start, int) else bass.ds(start, size)


def wait_count(eng, sem, count):
    if not isinstance(count, int) or count > 0:
        eng.wait_ge(sem, count)


def in_pairs(eng, tiles, body):
    body(0, [0, 1])
    with eng.Fori(1, tiles // 2) as j:
        body(j, [2 * j, 2 * j + 1])
    if tiles % 2:
        body(tiles // 2, [tiles - 1])


def gnn_kernel(nc, x, src, dst, w0, bias0, w_gc, b_gc, w_res, b_res, w_gate, b_gate,
               w1, b1, w2, b2, gamma, beta, out):
    N, D = x.shape
    EDGES = src.shape[0]
    NE, _, H = w1.shape
    DC = D // P
    HC = H // P
    NT = -(-N // P)
    LAST = N - (NT - 1) * P
    NPAIR = -(-EDGES // (2 * GROUP * P)) * 2 * PAIRS
    ET = 2 * NPAIR
    NG = ET // GROUP
    IT = NG // 2
    assert IT == NT and NT % 2 == 1 and D == 2 * P and NE <= P
    FULL = EDGES // ROW_PAIR
    REST = EDGES - FULL * ROW_PAIR
    CH = -(-NPAIR // P)
    LASTROWS = NPAIR - (CH - 1) * P
    ACCW = NT * P + WIN - 16
    assert ACCW >= N + WIN and ACCW >= NT * P
    ASSIGN = 2 * N
    YROWS = -(-ASSIGN // P) * P
    SLOTS = NE * CAP
    MAXBLK = NE + ASSIGN // P
    BL = -(-(MAXBLK + 8) // 8) * 8

    h_d = nc.dram_tensor("h_scratch", (NT * P, D), F32).ap()
    x2_d = nc.dram_tensor("x2_scratch", (NT * P, D), F32).ap()
    y_d = nc.dram_tensor("y_scratch", (YROWS, D), F32).ap()
    slot_d = nc.dram_tensor("slot_scratch", (SLOTS + P, 1), I32).ap()

    with ExitStack() as ctx:
        def sb(name, shape, dt):
            return ctx.enter_context(nc.sbuf_tensor(name, shape, dt))

        def sem(name):
            return ctx.enter_context(nc.semaphore(name))

        acc = sb("acc", [P, DC, ACCW], F32)
        X = sb("X", [P, NT, D], F32)
        Y = sb("Y", [P, NT, D], F32)
        idx_t = sb("idx_t", [P, ET], I32)
        rel_t = sb("rel_t", [P, ET], BF16)
        far_t = sb("far_t", [P, ET], I16)
        lohi_t = sb("lohi_t", [P, 4, ET], BF16)
        win_row = sb("win_row", [1, NPAIR], I32)
        gath = sb("gath", [P, 2, GROUP, D], F32)
        onehot = sb("onehot", [P, 2, GROUP, WIN], F32)
        oh_lo = sb("oh_lo", [P, 2, 2, 4, P], BF16)
        oh_hi = sb("oh_hi", [P, 2, 2, 4, NT], BF16)
        idx_s = sb("idx_s", [P, 2, GROUP], I32)
        xs = sb("xs", [P, D], F32)
        xT = sb("xT", [P, DC, P], F32)
        w0_s = sb("w0_s", [P, 2 * DC, D], F32)
        wgc_s = sb("wgc_s", [P, DC, D], F32)
        wres_s = sb("wres_s", [P, DC, D], F32)
        wg_s = sb("wg_s", [P, DC, NE], F32)
        ident = sb("ident", [P, P], F32)
        iota_w = sb("iota_w", [P, WIN], F32)
        iota_lo = sb("iota_lo", [P, P], BF16)
        iota_hi = sb("iota_hi", [P, NT], BF16)
        bias_s = sb("bias_s", [P, D], F32)
        bias2_s = sb("bias2_s", [P, D], F32)
        zero_s = sb("zero_s", [P, D], F32)
        bg_s = sb("bg_s", [P, NE], F32)
        rdeg = sb("rdeg", [P, 6, NT], F32)
        DEG_IN, DEG_OUT, R_IN, RS_IN, RS_OUT, TMP = range(6)
        flag_s = sb("flag_s", [1, 1], I32)
        small = sb("small", [P, 8], F32)
        ones_f = sb("ones_f", [P, P], F32)
        ids_t = sb("ids_t", [P, NT, 2], I32)
        vals_t = sb("vals_t", [P, NT, 2], F32)
        blk_e = sb("blk_e", [1, BL], I32)
        blk_s = sb("blk_s", [1, BL], I32)
        blk_n = sb("blk_n", [1, 1], I32)

        banks = [ctx.enter_context(nc.psum_tensor(f"bank{i}", [P, 512], F32)) for i in range(8)]
        WINB = banks[0:2]
        HISTB = banks[2:4]
        TB, MB = banks[4], banks[5]

        yflat = Y[:, :, :].rearrange("p t d -> p (t d)")
        cols = CH * ROW_PAIR

        def tab(k):
            return yflat[:, k * cols:(k + 1) * cols]

        srcI, dstI = tab(0).bitcast(I32), tab(1).bitcast(I32)
        srcF, dstF, idxF, relF, farF, tmpF = tab(2), tab(3), tab(4), tab(5), tab(6), tab(7)
        loS, hiS, loD, hiD = tab(8), tab(9), tab(10), tab(11)
        assert 12 * cols <= NT * D
        tables = [idxF, relF, farF, loS, hiS, loD, hiD]
        table_out = [idx_t[:, :], rel_t[:, :], far_t[:, :]] + [lohi_t[:, k, :] for k in range(4)]
        wmin = small[:, 0:CH]

        gflat = gath[:, :, :, :].rearrange("p a k d -> p (a k d)")
        aflat = acc[:, :, :].rearrange("p c n -> p (c n)")
        at = [0]

        def carve(flat, n, pattern=None, dt=F32, **dims):
            a = flat[:, at[0]:at[0] + n]
            at[0] += n
            if dt is not F32:
                a = a.bitcast(dt)
            return a.rearrange(pattern, **dims) if pattern else a

        sums_s = carve(gflat, 2 * D, "p (b c n) -> p b c n", b=2, c=DC)
        h_s = carve(gflat, 2 * D, "p (b d) -> p b d", b=2)
        junk = carve(gflat, 2 * D, "p (b d) -> p b d", b=2)
        stats = carve(gflat, 6 * NT, "p (t s) -> p t s", s=6)
        row_t = carve(gflat, 8 * NT, "p (k t) -> p k t", k=8)
        SS, RN, SUM, DIFF, VAR, RSTD, NMR, T0 = range(8)
        x2_s = h_s
        x2T = junk.rearrange("p b (c n) -> p b c n", c=DC)
        at[0] = 4 * D + 2 * D
        logit = carve(gflat, 2 * NE, "p (t e) -> p t e", t=2)
        top8 = carve(gflat, 16, "p (t e) -> p t e", t=2)
        top8i = carve(gflat, 16, "p (t e) -> p t e", t=2, dt=U32)
        top2f = carve(gflat, 4)
        pick = carve(gflat, 4 * NE, "p (t k e) -> p t k e", t=2, k=2)
        prod = carve(gflat, 4 * NE, "p (t k e) -> p t k e", t=2, k=2)
        both = carve(gflat, NE, "p (t e) -> p t e", t=2, dt=BF16)
        before = carve(gflat, NE // 2, dt=BF16)
        rank = carve(gflat, 4)
        slotf = carve(gflat, 4)
        overf = carve(gflat, 4)
        slot_s = carve(gflat, 4, "p (t k) -> p t k", t=2, dt=I32)
        ids_s = carve(gflat, 4, "p (t k) -> p t k", t=2, dt=I32)
        iota_e = carve(gflat, NE)
        upper = carve(gflat, P // 2, dt=BF16)
        upto = carve(gflat, NE)
        iota_b = carve(gflat, BL)
        cnt = carve(gflat, 8)
        reached = carve(gflat, BL)
        blk_row = carve(gflat, 4 * BL, "p (k b) -> p k b", k=4)
        ones_b = carve(gflat, P // 2, dt=BF16)
        assert at[0] <= 2 * GROUP * D
        at[0] = 0
        w1_s = carve(aflat, 2 * DC * H, "p (b c h) -> p b c h", b=2, c=DC)
        w2_s = carve(aflat, 2 * HC * D, "p (b c d) -> p b c d", b=2, c=HC)
        b2_s = carve(aflat, 2 * D, "p (b d) -> p b d", b=2)
        xg_s = carve(aflat, 2 * D, "p (b d) -> p b d", b=2)
        xgT = carve(aflat, 2 * D, "p (b c n) -> p b c n", b=2, c=DC)
        hT = carve(aflat, 2 * H, "p (b c n) -> p b c n", b=2, c=HC)
        yo_s = carve(aflat, 2 * D, "p (b d) -> p b d", b=2)
        b1r_s = carve(aflat, 2 * P, "p (b n) -> p b n", b=2)
        b1T = carve(aflat, 2 * HC, "p (b c) -> p b c", b=2)
        bid_s = carve(aflat, 2, dt=I32)
        bids_s = carve(aflat, 2, dt=I32)
        gid_s = carve(aflat, 2, dt=I32)
        tmp_s = carve(aflat, 4)
        ya_s = carve(aflat, 2 * D, "p (b d) -> p b d", b=2)
        yb_s = carve(aflat, 2 * D, "p (b d) -> p b d", b=2)
        sq_s = carve(aflat, 2 * D, "p (b d) -> p b d", b=2)
        out_s = carve(aflat, 2 * D, "p (b d) -> p b d", b=2)
        mean_s = carve(aflat, D)
        scale_s = carve(aflat, D)
        bn_s = carve(aflat, 2 * D, "p (b d) -> p b d", b=2)
        assert at[0] <= DC * ACCW

        fill = gath[:, 1, :, :].rearrange("p k d -> p (k d)")[:, 0:(SLOTS + P) // P].bitcast(I32)

        FARW = 448
        NFAR = NT * P // FARW
        assert NFAR * FARW == NT * P and FARW <= 512 and FARW <= GROUP * WIN
        at[0] = GROUP * D
        iota_far = carve(gflat, FARW)
        far_dst = carve(gflat, 1)
        far_idx = carve(gflat, 1, dt=I32)
        far_rows = gath[:, 0, 0, :]
        far_onehot = onehot[:, 0, :, :].rearrange("p k w -> p (k w)")[:, 0:FARW]

        edges_in = sem("edges_in")
        pads_set = sem("pads_set")
        const_set = sem("const_set")
        weights_in = sem("weights_in")
        dve_step = sem("dve_step")
        tabs_made = sem("tabs_made")
        tabs_turned = sem("tabs_turned")
        tabs_done = sem("tabs_done")
        wmin_turned = sem("wmin_turned")
        win_set = sem("win_set")
        table_fill = sem("table_fill")
        spacer = sem("spacer")
        groups_done = sem("groups_done")
        idx_ready = sem("idx_ready")
        onehot_ready = sem("onehot_ready")
        hist_ready = sem("hist_ready")
        hist_done = sem("hist_done")
        acc_step = sem("acc_step")
        gath_full = [sem(f"gath_full{k}") for k in range(2 * GROUP)]
        xs_full = sem("xs_full")
        x_turned = sem("x_turned")
        xT_ready = sem("xT_ready")
        prep_mm = sem("prep_mm")
        prep_done = sem("prep_done")
        xs1_ready = sem("xs1_ready")
        bias1_ready = sem("bias1_ready")
        bias1_in = sem("bias1_in")
        hist_read = sem("hist_read")
        sqrt_done = sem("sqrt_done")
        sums_final = sem("sums_final")
        far_const = sem("far_const")
        far_taken = [sem(f"far_taken{k}") for k in range(2)]
        far_gath = [sem(f"far_gath{k}") for k in range(2)]
        far_ready = [sem(f"far_ready{k}") for k in range(2)]
        far_mm = [sem(f"far_mm{k}") for k in range(2)]
        far_step = [sem(f"far_step{k}") for k in range(2)]
        fill_set = sem("fill_set")
        slots_cleared = sem("slots_cleared")
        y_cleared = sem("y_cleared")
        deg_ready = sem("deg_ready")
        sums_staged = sem("sums_staged")
        sums_mm = sem("sums_mm")
        sums_used = sem("sums_used")
        squares = sem("squares")
        raw_ready = sem("raw_ready")
        stats_done = sem("stats_done")
        x1_ready = sem("x1_ready")
        h_ready = sem("h_ready")
        h_stored = [sem(f"h_stored{b}") for b in range(2)]
        rsqrt_asked = sem("rsqrt_asked")
        x2_ready = sem("x2_ready")
        x2_kept = sem("x2_kept")
        x2_stored = [sem(f"x2_stored{b}") for b in range(2)]
        x2_turned = sem("x2_turned")
        x2T_ready = sem("x2T_ready")
        logit_mm = sem("logit_mm")
        both_ready = sem("both_ready")
        rank_mm = sem("rank_mm")
        slots_ready = sem("slots_ready")
        route_step = sem("route_step")
        slots_stored = [sem(f"slots_stored{k}") for k in range(4)]
        route_const = sem("route_const")
        blk_mm = sem("blk_mm")
        blk_step = sem("blk_step")
        blocks_ready = sem("blocks_ready")
        bid_full = [sem(f"bid_full{b}") for b in range(2)]
        bids_full = [sem(f"bids_full{b}") for b in range(2)]
        w_full = [sem(f"w_full{b}") for b in range(2)]
        gid_step = sem("gid_step")
        xg_full = [sem(f"xg_full{b}") for b in range(2)]
        xg_turned = sem("xg_turned")
        xgT_ready = sem("xgT_ready")
        b1_turned = sem("b1_turned")
        b1T_ready = sem("b1T_ready")
        mm1_done = sem("mm1_done")
        gelu_done = sem("gelu_done")
        mm2_done = sem("mm2_done")
        yo_ready = sem("yo_ready")
        yo_stored = [sem(f"yo_stored{b}") for b in range(2)]
        experts_done = sem("experts_done")
        y_full = [sem(f"y_full{b}") for b in range(2)]
        yb_scaled = sem("yb_scaled")
        ya_added = sem("ya_added")
        yb_added = sem("yb_added")
        mean_mm = sem("mean_mm")
        mean_ready = sem("mean_ready")
        centred = sem("centred")
        sq_ready = sem("sq_ready")
        var_mm = sem("var_mm")
        last_in = sem("last_in")
        beta_added = sem("beta_added")
        scale_ready = sem("scale_ready")
        scaled = sem("scaled")
        summed = sem("summed")
        stats2 = sem("stats2")
        out_ready = sem("out_ready")
        out_stored = [sem(f"out_stored{b}") for b in range(2)]

        def spaced_wait(eng, s, count):
            if isinstance(count, int):
                wait_count(eng, s, count)
            else:
                eng.wait_ge(s, count)
                eng.sem_inc(spacer, 1)

        def bcast(vec, n=P):
            return vec.rearrange("(a n) -> a n", a=1).to_broadcast([n, vec.shape[0]])

        block = ctx.enter_context(nc.Block())

        @block.sync
        def _(sp):
            edge_loads = 0
            for vec, t in ((src, srcI), (dst, dstI)):
                tv = t.rearrange("p (c e) -> p c e", c=CH)
                sp.dma_start(tv[:, 0:CH - 1, :], vec[0:(CH - 1) * P * ROW_PAIR].rearrange(
                    "(c p e) -> p c e", p=P, e=ROW_PAIR)).then_inc(edges_in, 16)
                edge_loads += 1
            sp.wait_ge(pads_set, 1)
            n_full = FULL - (CH - 1) * P
            for vec, t in ((src, srcI), (dst, dstI)):
                tv = t.rearrange("p (c e) -> p c e", c=CH)
                sp.dma_start(tv[0:n_full, CH - 1, :], vec[(CH - 1) * P * ROW_PAIR:FULL * ROW_PAIR]
                             .rearrange("(p e) -> p e", e=ROW_PAIR)).then_inc(edges_in, 16)
                sp.dma_start(tv[n_full:n_full + 1, CH - 1, 0:REST],
                             vec[FULL * ROW_PAIR:EDGES].rearrange("(p e) -> p e", p=1)
                             ).then_inc(edges_in, 16)
                edge_loads += 2
            sp.dma_start(w0_s[:, :, :], w0.rearrange("(c p) n -> p c n", p=P)).then_inc(weights_in, 16)
            sp.dma_start(bias_s[:, :], bcast(bias0)).then_inc(weights_in, 16)
            sp.dma_start(wgc_s[:, :, :], w_gc.rearrange("(c p) n -> p c n", p=P)).then_inc(weights_in, 16)
            sp.dma_start(wres_s[:, :, :], w_res.rearrange("(c p) n -> p c n", p=P)).then_inc(weights_in, 16)
            sp.dma_start(wg_s[:, :, :], w_gate.rearrange("(c p) n -> p c n", p=P)).then_inc(weights_in, 16)
            sp.dma_start(bias2_s[:, :], bcast(b_res)).then_inc(weights_in, 16)
            sp.dma_start(bg_s[:, :], bcast(b_gate)).then_inc(weights_in, 16)

            sp.wait_ge(fill_set, 2)
            sp.dma_start(slot_d.rearrange("(p s) a -> p (s a)", p=P), fill).then_inc(slots_cleared, 16)

            def load_x(i, rows=P):
                wait_count(sp, prep_done, 1 * i)
                sp.dma_start(xs[0:rows, :], x[ds(P * i, rows), :]).then_inc(xs_full, 16)

            load_x(0)
            with sp.Fori(1, NT - 1) as i:
                load_x(i)
            load_x(NT - 1, LAST)

            sp.wait_ge(prep_done, NT)
            sp.dma_start(bias_s[:, :], bcast(b_gc)).then_inc(bias1_in, 16)

            def store_h(_, tiles):
                for b, i in enumerate(tiles):
                    sp.wait_ge(h_ready, i + 1)
                    sp.dma_start(h_d[ds(P * i, P), :], h_s[:, b, :]).then_inc(h_stored[b], 16)
            in_pairs(sp, NT, store_h)
            for b in range(2):
                sp.wait_ge(h_stored[b], 16 * ((NT + 1 - b) // 2))

            def store_x2(_, tiles):
                for b, i in enumerate(tiles):
                    sp.wait_ge(x2_ready, i + 1)
                    sp.dma_start(x2_d[ds(P * i, P), :], x2_s[:, b, :]).then_inc(x2_stored[b], 16)
            in_pairs(sp, NT, store_x2)
            for b in range(2):
                sp.wait_ge(x2_stored[b], 16 * ((NT + 1 - b) // 2))

            sp.wait_ge(blocks_ready, 1)
            pairs = sp.value_load(blk_n[0:1, 0:1], min_val=2, max_val=(BL - 8) // 2)
            n_pair = (NT + 1) // 2
            for k in range(4):
                sp.wait_ge(slots_stored[k], 16 * (n_pair if k < 2 else n_pair - 1))

            def load_rows(blk, b, where, full):
                first = sp.value_load(blk_s[0:1, ds(blk, 1)], min_val=0, max_val=SLOTS)
                sp.dma_start(where[:, b:b + 1], slot_d[ds(first, P), :]).then_inc(full[b], 16)

            load_rows(0, 0, bid_s, bid_full)
            load_rows(1, 1, bid_s, bid_full)

            def load_blocks(j):
                for b in range(2):
                    blk = 2 * j + b
                    spaced_wait(sp, gid_step, 3 * (blk + 1))
                    load_rows(blk + 2, b, bid_s, bid_full)
                    e = sp.value_load(blk_e[0:1, ds(blk, 1)], min_val=0, max_val=NE - 1)
                    wait_count(sp, mm2_done, blk - 1)
                    wait_count(sp, yo_ready, blk - 1)
                    sp.dma_start(w1_s[:, b, :, :], w1[ds(e, 1), :, :].rearrange(
                        "a (c p) h -> p (a c) h", p=P)).then_inc(w_full[b], 16)
                    sp.dma_start(b1r_s[0:HC, b, :], b1[ds(e, 1), :].rearrange(
                        "a (c p) -> (a c) p", p=P)).then_inc(w_full[b], 16)
                    sp.dma_start(w2_s[:, b, :, :], w2[ds(e, 1), :, :].rearrange(
                        "a (c p) d -> p (a c) d", p=P)).then_inc(w_full[b], 16)
                    sp.dma_start(b2_s[:, b, :], b2[ds(e, 1), :].to_broadcast([P, D])).then_inc(w_full[b], 16)
                    spaced_wait(sp, yo_stored[b], 16 * j)
                    load_rows(blk, b, bids_s, bids_full)
            load_blocks(0)
            with sp.Fori(1, pairs) as j:
                load_blocks(j)
            for b in range(2):
                sp.wait_ge(yo_stored[b], 16 * pairs)

            sp.wait_ge(y_cleared, 16)
            sp.dma_start(bias2_s[:, :], bcast(gamma)).then_inc(last_in, 16)
            sp.dma_start(zero_s[:, :], bcast(beta)).then_inc(last_in, 16)

            def load_y(_, tiles):
                for b, i in enumerate(tiles):
                    rows = LAST if isinstance(i, int) and i == NT - 1 else P
                    wait_count(sp, yb_added, i - 1)
                    sp.dma_start(ya_s[0:rows, b, :], y_d[ds(P * i, rows), :]).then_inc(y_full[b], 16)
                    sp.dma_start(yb_s[0:rows, b, :], y_d[ds(N + P * i, rows), :]).then_inc(y_full[b], 16)
            in_pairs(sp, NT, load_y)

            def store_out(_, tiles):
                for b, i in enumerate(tiles):
                    rows = LAST if isinstance(i, int) and i == NT - 1 else P
                    sp.wait_ge(out_ready, i + 1)
                    sp.dma_start(out[ds(P * i, rows), :], out_s[0:rows, b, :]).then_inc(out_stored[b], 16)
            in_pairs(sp, NT, store_out)
            for b in range(2):
                sp.wait_ge(out_stored[b], 16 * ((NT + 1 - b) // 2))

        @block.gpsimd
        def _(pool):
            for t in (srcI, dstI):
                pad = pool.memset(t.rearrange("p (c e) -> p c e", c=CH)[:, CH - 1, :], PAD)
            pad.then_inc(pads_set, 1)
            pool.memset(ident[:, :], 0.0).then_inc(const_set, 1)
            pool.memset(ones_f[:, :], 1.0).then_inc(const_set, 1)
            pool.iota(iota_w[:, :], pattern=[[1, WIN]], base=0, channel_multiplier=0,
                      allow_small_or_imprecise_dtypes=True).then_inc(const_set, 1)
            pool.iota(iota_lo[:, :], pattern=[[1, P]], base=0, channel_multiplier=0,
                      allow_small_or_imprecise_dtypes=True).then_inc(const_set, 1)
            pool.iota(iota_hi[:, :], pattern=[[P, NT]], base=0, channel_multiplier=0,
                      allow_small_or_imprecise_dtypes=True).then_inc(const_set, 1)
            pool.wait_ge(const_set, 1)
            pool.affine_select(out=ident[:, :], in_=ident[:, :], compare_op=ALU.not_equal, fill=1.0,
                               base=0, pattern=[[-1, P]], channel_multiplier=1).then_inc(const_set, 1)

            pool.memset(fill, ASSIGN).then_inc(fill_set, 1)
            pool.memset(zero_s[:, :], 0.0).then_inc(fill_set, 1)
            pool.iota(ids_t[:, :, :], pattern=[[P, NT], [N, 2]], base=0, channel_multiplier=1
                      ).then_inc(const_set, 1)
            pool.wait_ge(slots_cleared, 16)

            def gather(table, g, step, half):
                spaced_wait(pool, idx_ready, g + 1)
                for k in range(GROUP):
                    pool.indirect_dma_start(
                        out=gath[:, half, k, :], out_offset=None, in_=table,
                        in_offset=bass.IndirectOffsetOnAxis(ap=idx_s[:, half, k:k + 1], axis=0),
                    ).then_inc(gath_full[half * GROUP + k], 16)

            def layer(L, table):
                def step(i):
                    for half in range(2):
                        gather(table, NG * L + 2 * i + half, IT * L + i, half)
                step(0)
                with pool.Fori(1, IT) as i:
                    step(i)

            def far_gathers(L, table):
                pool.wait_ge(acc_step, PAIRS * NG * (L + 1) + 1 + L)
                beyond = pool.value_load(flag_s[0:1, 0:1], min_val=0, max_val=ET * P)
                with pool.If(beyond > 0):
                    pool.iota(iota_far, pattern=[[1, FARW]], base=0, channel_multiplier=0,
                              allow_small_or_imprecise_dtypes=True).then_inc(far_const, 1)
                    with pool.Fori(0, ET) as t:
                        spaced_wait(pool, far_taken[L], t + 1)
                        pool.indirect_dma_start(
                            out=far_rows, out_offset=None, in_=table,
                            in_offset=bass.IndirectOffsetOnAxis(ap=far_idx, axis=0)).then_inc(far_gath[L], 16)

            layer(0, x[:, :])
            far_gathers(0, x[:, :])

            def stage(_, tiles):
                for b, i in enumerate(tiles):
                    spaced_wait(pool, sums_mm, i - 1)
                    pool.tensor_copy(sums_s[:, b, :, :], acc[:, :, ds(P * i, P)]).then_inc(sums_staged, 1)
            pool.wait_ge(sums_final, 1)
            in_pairs(pool, NT, stage)
            pool.wait_ge(sums_staged, NT)
            pool.memset(acc[:, :, :], 0.0).then_inc(acc_step, 1)

            for b in range(2):
                pool.wait_ge(h_stored[b], 16 * ((NT + 1 - b) // 2))
            layer(1, h_d)
            far_gathers(1, h_d)

            pool.wait_ge(sums_final, 2)
            pool.iota(iota_e, pattern=[[1, NE]], base=0, channel_multiplier=0,
                      allow_small_or_imprecise_dtypes=True).then_inc(route_const, 1)
            pool.iota(iota_b, pattern=[[1, BL]], base=0, channel_multiplier=0,
                      allow_small_or_imprecise_dtypes=True).then_inc(route_const, 1)
            pool.memset(before, 0.0).then_inc(route_const, 1)
            pool.memset(both, 0.0).then_inc(route_const, 1)
            pool.memset(upper, 1.0).then_inc(route_const, 1)
            pool.memset(ones_b, 1.0).then_inc(route_const, 1)
            pool.memset(upto, 1.0).then_inc(route_const, 1)
            pool.wait_ge(route_const, 7)
            pool.affine_select(out=upper, in_=upper, compare_op=ALU.is_gt, fill=0.0, base=0,
                               pattern=[[1, P]], channel_multiplier=-1).then_inc(route_const, 1)
            pool.affine_select(out=upto, in_=upto, compare_op=ALU.is_ge, fill=0.0, base=0,
                               pattern=[[1, NE]], channel_multiplier=-1).then_inc(route_const, 1)

            def store_slots(pair, tiles):
                spaced_wait(pool, slots_ready, pair + 1)
                for t, i in enumerate(tiles):
                    rows = LAST if isinstance(i, int) and i == NT - 1 else P
                    for k in range(2):
                        pool.indirect_dma_start(
                            out=slot_d, in_=ids_s[0:rows, t, k:k + 1], in_offset=None,
                            out_offset=bass.IndirectOffsetOnAxis(ap=slot_s[0:rows, t, k:k + 1], axis=0),
                            bounds_check=SLOTS - 1, oob_is_err=False).then_inc(slots_stored[2 * t + k], 16)
            in_pairs(pool, NT, store_slots)

            pool.wait_ge(blocks_ready, 1)
            for b in range(2):
                pool.wait_ge(x2_stored[b], 16 * ((NT + 1 - b) // 2))
            pairs = pool.value_load(blk_n[0:1, 0:1], min_val=2, max_val=(BL - 8) // 2)
            pool.wait_ge(y_cleared, 16)

            def gather_rows(blk, b):
                spaced_wait(pool, gid_step, 3 * (blk + 1))
                pool.indirect_dma_start(
                    out=xg_s[:, b, :], out_offset=None, in_=x2_d,
                    in_offset=bass.IndirectOffsetOnAxis(ap=gid_s[:, b:b + 1], axis=0)).then_inc(xg_full[b], 16)

            gather_rows(0, 0)
            gather_rows(1, 1)

            def blocks(j):
                for b in range(2):
                    spaced_wait(pool, xg_turned, 2 * j + b + 1)
                    gather_rows(2 * j + b + 2, b)
                    spaced_wait(pool, bids_full[b], 16 * (j + 1))
                    spaced_wait(pool, yo_ready, 2 * j + b + 1)
                    pool.indirect_dma_start(
                        out=y_d, in_=yo_s[:, b, :], in_offset=None,
                        out_offset=bass.IndirectOffsetOnAxis(ap=bids_s[:, b:b + 1], axis=0),
                        bounds_check=ASSIGN - 1, oob_is_err=False).then_inc(yo_stored[b], 16)
            blocks(0)
            with pool.Fori(1, pairs) as j:
                blocks(j)

            def add_yb(_, tiles):
                for b, i in enumerate(tiles):
                    pool.wait_ge(ya_added, i + 1)
                    spaced_wait(pool, yb_scaled, i + 1)
                    pool.tensor_tensor(Y[:, ds(i, 1), :], Y[:, ds(i, 1), :], yb_s[:, b:b + 1, :], ALU.add
                                       ).then_inc(yb_added, 1)
            in_pairs(pool, NT, add_yb)
            pool.wait_ge(last_in, 32)

            def add_beta(_, tiles):
                for b, i in enumerate(tiles):
                    pool.tensor_tensor(X[:, ds(i, 1), :], X[:, ds(i, 1), :], zero_s[:, :].unsqueeze(1), ALU.add
                                       ).then_inc(beta_added, 1)
            in_pairs(pool, NT, add_beta)
            pool.wait_ge(scale_ready, 1)

            def scale_y(_, tiles):
                for b, i in enumerate(tiles):
                    pool.tensor_tensor(Y[:, ds(i, 1), :], Y[:, ds(i, 1), :], scale_s.unsqueeze(1), ALU.mult
                                       ).then_inc(scaled, 1)
            in_pairs(pool, NT, scale_y)

        @block.scalar
        def _(act):
            n = 0
            for k, (_, o) in enumerate(zip(tables, table_out)):
                for c in range(CH):
                    m = P if c < CH - 1 else LASTROWS
                    act.wait_ge(tabs_turned, n + 1)
                    act.activation(o[:, c * ROW_PAIR:c * ROW_PAIR + 2 * m].rearrange("p (q h) -> p q h", h=2),
                                   banks[4 + n % 4][:, 0:2 * P].rearrange("p (h q) -> p q h", h=2)[:, 0:m, :],
                                   ACT.Copy).then_inc(tabs_done, 1)
                    n += 1

            def stage_idx(L, i):
                for half in range(2):
                    g = NG * L + 2 * i + half
                    spaced_wait(act, groups_done, g - 1)
                    act.activation(idx_s[:, half, :], idx_t[:, ds(2 * GROUP * i + GROUP * half, GROUP)],
                                   ACT.Copy).then_inc(idx_ready, 1)

            act.wait_ge(tabs_done, n)

            def step0(i):
                stage_idx(0, i)
                act.wait_ge(x_turned, i + 1)
                act.activation(xT[:, :, :], TB[:, 0:D].rearrange("p (c n) -> p c n", c=DC),
                               ACT.Copy).then_inc(xT_ready, 1)
            act.wait_ge(fill_set, 2)
            act.dma_start(y_d.rearrange("(p r) d -> p r d", p=P),
                          zero_s[:, :].unsqueeze(1).to_broadcast([P, YROWS // P, D])).then_inc(y_cleared, 16)
            step0(0)
            with act.Fori(1, IT) as i:
                step0(i)

            act.wait_ge(deg_ready, 1)
            act.activation(rdeg[:, RS_IN, :], rdeg[:, R_IN, :], ACT.Sqrt)
            act.activation(rdeg[:, RS_OUT, :], rdeg[:, TMP, :], ACT.Sqrt).then_inc(sqrt_done, 1)

            def square(_, tiles):
                for b, i in enumerate(tiles):
                    spaced_wait(act, squares, i - 1)
                    spaced_wait(act, sums_used, i + 1)
                    act.activation(junk[:, b, :], Y[:, ds(i, 1), :].rearrange("p a d -> p (a d)"), ACT.Square,
                                   accum_out=row_t[:, SS, ds(i, 1)]).then_inc(squares, 1)
            in_pairs(act, NT, square)
            act.wait_ge(squares, NT)
            act.activation(row_t[:, RN, :], row_t[:, SS, :], ACT.Sqrt).then_inc(sqrt_done, 1)
            act.wait_ge(rsqrt_asked, 1)
            act.activation(row_t[:, RSTD, :], row_t[:, VAR, :], ACT.Sqrt).then_inc(sqrt_done, 1)

            def scale_h(_, tiles):
                for b, i in enumerate(tiles):
                    spaced_wait(act, h_stored[b], 16 * ((i - b) // 2) if isinstance(i, int) else 16 * _)
                    spaced_wait(act, x1_ready, i + 1)
                    act.activation(h_s[:, b, :], X[:, ds(i, 1), :].rearrange("p a d -> p (a d)"), ACT.Copy,
                                   scale=rdeg[:, RS_OUT, ds(i, 1)]).then_inc(h_ready, 1)
            in_pairs(act, NT, scale_h)

            def step1(i):
                stage_idx(1, i)
                spaced_wait(act, x_turned, NT + i)
                act.activation(xs[:, :], X[:, ds(i, 1), :].rearrange("p a d -> p (a d)"), ACT.Copy
                               ).then_inc(xs1_ready, 1)
                act.wait_ge(x_turned, NT + i + 1)
                act.activation(xT[:, :, :], TB[:, 0:D].rearrange("p (c n) -> p c n", c=DC),
                               ACT.Copy).then_inc(xT_ready, 1)
            step1(0)
            with act.Fori(1, IT) as i:
                step1(i)

            def stage_x2(_, tiles):
                for b, i in enumerate(tiles):
                    spaced_wait(act, sums_mm, NT + i - 1)
                    act.activation(sums_s[:, b, :, :], acc[:, :, ds(P * i, P)], ACT.Copy).then_inc(sums_staged, 1)
                for b, i in enumerate(tiles):
                    spaced_wait(act, x2_ready, i + 1)
                    act.activation(Y[:, ds(i, 1), :].rearrange("p a d -> p (a d)"), x2_s[:, b, :], ACT.Copy
                                   ).then_inc(x2_kept, 1)
                    act.wait_ge(x2_turned, i + 1)
                    act.activation(x2T[:, b, :, :], banks[2 + b][:, 0:D].rearrange("p (c n) -> p c n", c=DC),
                                   ACT.Copy).then_inc(x2T_ready, 1)
            act.wait_ge(sums_final, 2)
            in_pairs(act, NT, stage_x2)
            act.wait_ge(rsqrt_asked, 2)
            act.activation(vals_t[:, :, 1:2], vals_t[:, :, 1:2], ACT.Exp).then_inc(sqrt_done, 1)

            act.wait_ge(blocks_ready, 1)
            pairs = act.value_load(blk_n[0:1, 0:1], min_val=2, max_val=(BL - 8) // 2)

            def gelus(j):
                for b in range(2):
                    blk = 2 * j + b
                    act.wait_ge(b1T_ready, blk + 1)
                    wait_count(act, mm2_done, blk - 1)
                    for c in range(HC):
                        act.wait_ge(mm1_done, HC * blk + c + 1)
                        act.activation(hT[:, b, c, :], banks[2 + c][:, 0:P], ACT.Gelu,
                                       bias=b1T[:, b, c:c + 1]).then_inc(gelu_done, 1)
            gelus(0)
            with act.Fori(1, pairs) as j:
                gelus(j)

            def scale_yb(p, tiles):
                for b, i in enumerate(tiles):
                    spaced_wait(act, y_full[b], 32 * (p + 1))
                    act.activation(yb_s[:, b, :], yb_s[:, b, :], ACT.Copy,
                                   scale=vals_t[:, ds(i, 1), 1:2].rearrange("p a b -> p (a b)")
                                   ).then_inc(yb_scaled, 1)
            in_pairs(act, NT, scale_yb)

            def square_y(_, tiles):
                for b, i in enumerate(tiles):
                    spaced_wait(act, var_mm, i - 1)
                    spaced_wait(act, centred, i + 1)
                    act.activation(sq_s[:, b, :], Y[:, ds(i, 1), :].rearrange("p a d -> p (a d)"), ACT.Square
                                   ).then_inc(sq_ready, 1)
            in_pairs(act, NT, square_y)
            act.wait_ge(rsqrt_asked, 3)
            act.activation(bn_s[:, 1, :], bn_s[:, 0, :], ACT.Sqrt).then_inc(sqrt_done, 1)
            act.wait_ge(rsqrt_asked, 4)
            act.activation(row_t[:, RSTD, :], row_t[:, VAR, :], ACT.Sqrt).then_inc(sqrt_done, 1)

        @block.tensor
        def _(pe):
            pe.wait_ge(const_set, 6)
            n = 0
            for k, t in enumerate(tables):
                for c in range(CH):
                    m = P if c < CH - 1 else LASTROWS
                    pe.wait_ge(tabs_made, k + 1)
                    if n >= 4:
                        pe.wait_ge(tabs_done, n - 3)
                    for h in range(2):
                        last = pe.transpose(banks[4 + n % 4][:, h * P:h * P + m],
                                            t[0:m, c * ROW_PAIR + h * P:c * ROW_PAIR + (h + 1) * P],
                                            ident[0:m, 0:m])
                    last.then_inc(tabs_turned, 1)
                    n += 1
            pe.wait_ge(tabs_made, len(tables) + 1)
            for c in range(CH):
                pe.transpose(banks[0][0:1, c * P:(c + 1) * P], wmin[:, c:c + 1], ident[:, :])
            pe.matmul(banks[1][0:1, 0:1], small[:, 5:6], ones_f[:, 0:1], start=True, stop=True
                      ).then_inc(wmin_turned, 1)
            pe.wait_ge(win_set, 1)
            pe.wait_ge(tabs_done, n)
            pe.wait_ge(weights_in, 7 * 16)

            def sums(L, i, half):
                g = NG * L + 2 * i + half
                pe.wait_ge(onehot_ready, g + 1)
                wait_count(pe, acc_step, PAIRS * (g - 1) + 1 + L if not isinstance(g, int) or g > 1 else 0)
                for q in range(PAIRS):
                    for k in (2 * q, 2 * q + 1):
                        pe.wait_ge(gath_full[half * GROUP + k], 16 * (IT * L + i + 1))
                    for c in range(DC):
                        for k in (2 * q, 2 * q + 1):
                            last = pe.matmul(WINB[half][:, q * P + c * WIN:q * P + (c + 1) * WIN],
                                             gath[:, half, k, c * P:(c + 1) * P], onehot[:, half, k, :],
                                             start=(k == 2 * q), stop=(k == 2 * q + 1))
                    if q == PAIRS - 1:
                        last.then_inc(groups_done, 1)
                if L == 0:
                    for b in range(2):
                        pe.wait_ge(hist_ready, 2 * g + b + 1)
                        for t in range(4):
                            for s in range(2):
                                last = pe.matmul(HISTB[s][:, 0:NT], oh_lo[:, b, s, t, :], oh_hi[:, b, s, t, :],
                                                 start=isinstance(g, int) and g + b + t == 0,
                                                 stop=isinstance(g, int) and g == NG - 1 and b + t == 4)
                        last.then_inc(hist_done, 1)

            def prep(L, i, w, sem_xs, unit):
                pe.wait_ge(sem_xs, unit * (i + 1))
                for c in range(DC):
                    last = pe.transpose(TB[:, c * P:(c + 1) * P], xs[:, c * P:(c + 1) * P], ident[:, :])
                last.then_inc(x_turned, 1)
                pe.wait_ge(xT_ready, NT * L + i + 1)
                wait_count(pe, prep_done, NT * L + i)
                for c in range(DC):
                    last = pe.matmul(MB[:, 0:D], xT[:, c, :], w[:, c, :], start=(c == 0), stop=(c == DC - 1))
                last.then_inc(prep_mm, 1)

            def step0(i):
                sums(0, i, 0)
                prep(0, i, w0_s, xs_full, 16)
                sums(0, i, 1)
            step0(0)
            with pe.Fori(1, IT - 1) as i:
                step0(i)
            step0(IT - 1)

            def far_sums(L):
                pe.wait_ge(acc_step, PAIRS * NG * (L + 1) + 1 + L)
                beyond = pe.value_load(flag_s[0:1, 0:1], min_val=0, max_val=ET * P)
                with pe.If(beyond > 0):
                    with pe.Fori(0, ET) as t:
                        spaced_wait(pe, far_gath[L], 16 * (t + 1))
                        with pe.Fori(0, NFAR) as w:
                            pe.wait_ge(far_ready[L], NFAR * t + w + 1)
                            for c in range(DC):
                                last = pe.matmul(WINB[c][:, 0:FARW], far_rows[:, c * P:(c + 1) * P], far_onehot,
                                                 start=True, stop=True)
                            last.then_inc(far_mm[L], 1)

            def product(L, w, c0):
                def body(_, tiles):
                    for b, i in enumerate(tiles):
                        pe.wait_ge(sums_staged, NT * L + i + 1)
                        wait_count(pe, sums_used, NT * L + i - 1)
                        for c in range(DC):
                            last = pe.matmul(banks[b][:, 0:D], sums_s[:, b, c, :], w[:, c0 + c, :],
                                             start=(c == 0), stop=(c == DC - 1))
                        last.then_inc(sums_mm, 1)
                return body
            far_sums(0)
            pe.wait_ge(sums_final, 1)
            in_pairs(pe, NT, product(0, w0_s, DC))

            def step1(i):
                sums(1, i, 0)
                prep(1, i, wres_s, xs1_ready, 1)
                sums(1, i, 1)
            pe.wait_ge(acc_step, PAIRS * NG + 2)
            pe.wait_ge(sums_used, NT)
            step1(0)
            with pe.Fori(1, IT) as i:
                step1(i)

            far_sums(1)
            pe.wait_ge(sums_final, 2)
            pe.wait_ge(route_const, 9)
            agg = product(1, wgc_s, 0)

            def route(pair, tiles):
                agg(pair, tiles)
                for b, i in enumerate(tiles):
                    pe.wait_ge(x2_ready, i + 1)
                    for c in range(DC):
                        last = pe.transpose(banks[2 + b][:, c * P:(c + 1) * P], x2_s[:, b, c * P:(c + 1) * P],
                                            ident[:, :])
                    last.then_inc(x2_turned, 1)
                for b, i in enumerate(tiles):
                    pe.wait_ge(x2T_ready, i + 1)
                    for c in range(DC):
                        last = pe.matmul(banks[4][:, b * NE:(b + 1) * NE], x2T[:, b, c, :], wg_s[:, c, :],
                                         start=(c == 0), stop=(c == DC - 1))
                last.then_inc(logit_mm, 1)
                pe.wait_ge(both_ready, pair + 1)
                for b, i in enumerate(tiles):
                    o = banks[5][:, b * NE:(b + 1) * NE]
                    pe.matmul(o, ones_b, before, start=True, stop=False)
                    if b:
                        pe.matmul(o, ones_b, both[:, 0, :], start=False, stop=False)
                    last = pe.matmul(o, upper, both[:, b, :], start=False, stop=True)
                last.then_inc(rank_mm, 1)
            in_pairs(pe, NT, route)

            pe.wait_ge(blk_step, 1)
            pe.matmul(banks[4][0:NE, 0:1], before, ones_b[:, 0:1], start=True, stop=True).then_inc(blk_mm, 1)
            pe.wait_ge(blk_step, 2)
            pe.matmul(banks[5][0:NE, 0:1], upto[0:NE, :], cnt[0:NE, 2:3], start=True, stop=True
                      ).then_inc(blk_mm, 1)
            pe.wait_ge(blk_step, 3)
            pe.matmul(banks[4][0:1, 0:BL], ones_f[0:NE, 0:1], reached[0:NE, :], start=True, stop=True)
            pe.matmul(banks[5][0:1, 0:BL], cnt[0:NE, 2:3], reached[0:NE, :], start=True, stop=True)
            pe.matmul(banks[2][0:1, 0:1], ones_f[0:NE, 0:1], cnt[0:NE, 2:3], start=True, stop=True
                      ).then_inc(blk_mm, 1)

            pe.wait_ge(blocks_ready, 1)
            pairs = pe.value_load(blk_n[0:1, 0:1], min_val=2, max_val=(BL - 8) // 2)

            def turn(j, b, blk):
                pe.wait_ge(xg_full[b], 16 * (j + 1))
                wait_count(pe, xgT_ready, blk - 1)
                wait_count(pe, b1T_ready, blk - 1)
                for c in range(DC):
                    last = pe.transpose(banks[b][:, c * P:(c + 1) * P], xg_s[:, b, c * P:(c + 1) * P], ident[:, :])
                last.then_inc(xg_turned, 1)

            turn(0, 0, 0)

            def experts(j):
                for b in range(2):
                    blk = 2 * j + b
                    pe.wait_ge(w_full[b], 64 * (j + 1))
                    spaced_wait(pe, xgT_ready, blk + 1)
                    pe.transpose(banks[b][:, D:D + HC], b1r_s[0:HC, b, :], ident[0:HC, 0:HC]).then_inc(b1_turned, 1)
                    for c in range(HC):
                        wait_count(pe, gelu_done, HC * (blk - 1) + c + 1 if not isinstance(blk, int) or blk > 0 else 0)
                        for d in range(DC):
                            last = pe.matmul(banks[2 + c][:, 0:P], w1_s[:, b, d, c * P:(c + 1) * P],
                                             xgT[:, b, d, :], start=(d == 0), stop=(d == DC - 1))
                        last.then_inc(mm1_done, 1)
                    turn(j + b, 1 - b, blk + 1)
                    wait_count(pe, yo_ready, blk - 1)
                    for c in range(HC):
                        pe.wait_ge(gelu_done, HC * blk + c + 1)
                        last = pe.matmul(banks[6 + b][:, 0:D], hT[:, b, c, :], w2_s[:, b, c, :],
                                         start=(c == 0), stop=(c == HC - 1))
                    last.then_inc(mm2_done, 1)
            experts(0)
            with pe.Fori(1, pairs) as j:
                experts(j)

            def col_sums(bank, data, ready, done):
                def body(_, tiles):
                    for b, i in enumerate(tiles):
                        rows = LAST if isinstance(i, int) and i == NT - 1 else P
                        pe.wait_ge(ready, i + 1)
                        pe.matmul(bank[:, 0:D], ones_f[0:rows, :], data(b, i)[0:rows, :],
                                  start=isinstance(i, int) and i == 0, stop=isinstance(i, int) and i == NT - 1
                                  ).then_inc(done, 1)
                return body
            in_pairs(pe, NT, col_sums(banks[0], lambda b, i: Y[:, ds(i, 1), :].rearrange("p a d -> p (a d)"),
                                      yb_added, mean_mm))
            in_pairs(pe, NT, col_sums(banks[1], lambda b, i: sq_s[:, b, :], sq_ready, var_mm))

        @block.vector
        def _(dve):
            steps = [0]

            def link(ins):
                steps[0] += 1
                ins.then_inc(dve_step, 1)
                dve.wait_ge(dve_step, steps[0])

            v = nc.vector
            link(v.memset(acc[:, :, :], 0.0))
            dve.wait_ge(pads_set, 1)
            dve.wait_ge(edges_in, 6 * 16)
            v.tensor_scalar(loS.bitcast(I32), srcI, P - 1, None, ALU.bitwise_and)
            v.tensor_scalar(loD.bitcast(I32), dstI, P - 1, None, ALU.bitwise_and)
            v.tensor_copy(srcF, srcI)
            link(v.tensor_copy(dstF, dstI))
            v.tensor_copy(tmpF, loS.bitcast(I32))
            link(v.tensor_copy(relF, loD.bitcast(I32)))
            v.tensor_tensor(hiS, srcF, tmpF, ALU.subtract)
            v.tensor_tensor(hiD, dstF, relF, ALU.subtract)
            v.tensor_copy(loS, tmpF)
            v.tensor_copy(loD, relF)
            link(v.tensor_scalar(idxF, srcF, float(N - 1), None, ALU.min))
            link(v.tensor_reduce(wmin, dstF.rearrange("p (c e) -> p c e", c=CH), AX, ALU.min))
            link(v.tensor_scalar(wmin, wmin, float(N - 1), None, ALU.min))
            for c in range(CH):
                last = v.tensor_scalar(relF[:, c * ROW_PAIR:(c + 1) * ROW_PAIR],
                                       dstF[:, c * ROW_PAIR:(c + 1) * ROW_PAIR], wmin[:, c:c + 1], None,
                                       ALU.subtract)
            link(last)
            link(v.tensor_scalar(tmpF, relF, float(WIN), None, ALU.is_ge))
            link(v.scalar_tensor_tensor(farF, dstF, 1.0, tmpF, ALU.add, ALU.mult))
            link(v.tensor_scalar(farF, farF, -1.0, None, ALU.add))
            link(v.scalar_tensor_tensor(tmpF, dstF, float(N), tmpF, ALU.is_lt, ALU.mult))
            link(v.tensor_reduce(small[:, 5:6], tmpF, AX, ALU.add))
            dve.sem_inc(tabs_made, len(tables) + 1)
            dve.wait_ge(wmin_turned, 1)
            v.tensor_copy(win_row[0:1, :], banks[0][0:1, 0:NPAIR])
            link(v.tensor_copy(flag_s[:, :], banks[1][0:1, 0:1]))
            dve.sem_inc(win_set, 1)
            dve.wait_ge(tabs_done, len(tables) * CH)
            dve.wait_ge(weights_in, 7 * 16)

            def one_hots(L, i, half):
                g = NG * L + 2 * i + half
                wait_count(dve, groups_done, g - 1)
                v.tensor_tensor(onehot[:, half, :, :],
                                iota_w[:, :].unsqueeze(1).to_broadcast([P, GROUP, WIN]),
                                rel_t[:, ds(2 * GROUP * i + GROUP * half, GROUP)].unsqueeze(2)
                                .to_broadcast([P, GROUP, WIN]), ALU.is_equal).then_inc(onehot_ready, 1)

            def degree_one_hots(i, half):
                g = 2 * i + half
                for b in range(2):
                    wait_count(dve, hist_done, 2 * g + b - 1)
                    for s in range(2):
                        for o, io, w, part in ((oh_lo, iota_lo, P, 0), (oh_hi, iota_hi, NT, 1)):
                            last = v.tensor_tensor(
                                o[:, b, s, :, :], io[:, :].unsqueeze(1).to_broadcast([P, 4, w]),
                                lohi_t[:, 2 * s + part, ds(2 * GROUP * i + GROUP * half + 4 * b, 4)]
                                .unsqueeze(2).to_broadcast([P, 4, w]), ALU.is_equal)
                    last.then_inc(hist_ready, 1)

            dve.sem_inc(acc_step, 1)

            def add_windows(L, i, half, last=False):
                g = NG * L + 2 * i + half
                first = [dve.value_load(win_row[0:1, ds(2 * PAIRS * i + PAIRS * half + q, 1)],
                                        min_val=0, max_val=N - 1) for q in range(PAIRS)]
                dve.wait_ge(groups_done, g + 1)
                if not last:
                    one_hots(L, i + 1, half)
                if L == 0 and not (last and half == 1):
                    degree_one_hots(i + half, 1 - half)
                for q in range(PAIRS):
                    dve.wait_ge(acc_step, PAIRS * g + q + 1 + L)
                    a = acc[:, :, bass.ds(first[q], WIN)]
                    v.tensor_tensor(a, a, WINB[half][:, q * P:(q + 1) * P].rearrange(
                        "p (c w) -> p c w", c=DC), ALU.add).then_inc(acc_step, 1)

            one_hots(0, 0, 0)
            degree_one_hots(0, 0)
            one_hots(0, 0, 1)

            def step0(i, last=False):
                add_windows(0, i, 0, last)
                dve.wait_ge(prep_mm, i + 1)
                v.tensor_copy(Y[:, ds(i, 1), :], MB[:, 0:D].unsqueeze(1))
                v.tensor_tensor(X[:, ds(i, 1), :], xs[:, :].unsqueeze(1), bias_s[:, :].unsqueeze(1),
                                ALU.add).then_inc(prep_done, 1)
                add_windows(0, i, 1, last)
            step0(0)
            with dve.Fori(1, IT - 1) as i:
                step0(i)
            step0(IT - 1, True)

            def far_windows(L):
                dve.wait_ge(acc_step, PAIRS * NG * (L + 1) + 1 + L)
                beyond = dve.value_load(flag_s[0:1, 0:1], min_val=0, max_val=ET * P)
                with dve.If(beyond > 0):
                    dve.wait_ge(far_const, L + 1)
                    with dve.Fori(0, ET) as t:
                        v.tensor_copy(far_idx, idx_t[:, bass.ds(t, 1)])
                        v.tensor_copy(far_dst, far_t[:, bass.ds(t, 1)]).then_inc(far_step[L], 1)
                        spaced_wait(dve, far_step[L], (NFAR + 1) * t + 1)
                        dve.sem_inc(far_taken[L], 1)
                        with dve.Fori(0, NFAR) as w:
                            v.tensor_scalar(far_onehot, iota_far, far_dst, None, ALU.is_equal
                                            ).then_inc(far_ready[L], 1)
                            dve.wait_ge(far_mm[L], NFAR * t + w + 1)
                            v.tensor_scalar(far_dst, far_dst, float(-FARW), None, ALU.add)
                            for c in range(DC):
                                a = acc[:, c, bass.ds(FARW * w, FARW)]
                                last = v.tensor_tensor(a, a, WINB[c][:, 0:FARW], ALU.add)
                            last.then_inc(far_step[L], 1)
                            spaced_wait(dve, far_step[L], (NFAR + 1) * t + w + 2)
                dve.sem_inc(sums_final, 1)
            far_windows(0)

            dve.wait_ge(hist_done, 2 * NG)
            v.tensor_scalar(rdeg[:, DEG_IN, :], HISTB[1][:, 0:NT], 1.0, None, ALU.max)
            link(v.tensor_scalar(rdeg[:, DEG_OUT, :], HISTB[0][:, 0:NT], 1.0, None, ALU.max))
            v.reciprocal(rdeg[:, R_IN, :], rdeg[:, DEG_IN, :])
            link(v.reciprocal(rdeg[:, TMP, :], rdeg[:, DEG_OUT, :]))
            dve.sem_inc(deg_ready, 1)

            def combine(_, tiles):
                for b, i in enumerate(tiles):
                    dve.wait_ge(sums_mm, i + 1)
                    yi = Y[:, ds(i, 1), :].rearrange("p a d -> p (a d)")
                    v.scalar_tensor_tensor(yi, banks[b][:, 0:D], rdeg[:, R_IN, ds(i, 1)], yi, ALU.mult, ALU.add
                                           ).then_inc(sums_used, 1)
            in_pairs(dve, NT, combine)
            dve.wait_ge(sqrt_done, 2)
            link(v.reciprocal(row_t[:, RN, :], row_t[:, RN, :]))

            def residual(_, tiles):
                for b, i in enumerate(tiles):
                    xi = X[:, ds(i, 1), :].rearrange("p a d -> p (a d)")
                    v.scalar_tensor_tensor(xi, Y[:, ds(i, 1), :].rearrange("p a d -> p (a d)"),
                                           row_t[:, RN, ds(i, 1)], xi, ALU.mult, ALU.add).then_inc(raw_ready, 1)
                for b, i in enumerate(tiles):
                    spaced_wait(dve, raw_ready, i + 1)
                    v.bn_stats(stats[:, ds(i, 1), :].rearrange("p a s -> p (a s)"),
                               X[:, ds(i, 1), :].rearrange("p a d -> p (a d)")).then_inc(stats_done, 1)
            in_pairs(dve, NT, residual)
            dve.wait_ge(stats_done, NT)

            def row_norm(roots):
                me, ve, mo, vo = (stats[:, :, k] for k in (1, 2, 4, 5))
                v.tensor_tensor(row_t[:, SUM, :], me, mo, ALU.add)
                v.tensor_tensor(row_t[:, VAR, :], ve, vo, ALU.add)
                link(v.tensor_tensor(row_t[:, DIFF, :], me, mo, ALU.subtract))
                link(v.tensor_tensor(row_t[:, DIFF, :], row_t[:, DIFF, :], row_t[:, DIFF, :], ALU.mult))
                link(v.scalar_tensor_tensor(row_t[:, VAR, :], row_t[:, DIFF, :], D / 4.0, row_t[:, VAR, :],
                                            ALU.mult, ALU.add))
                link(v.tensor_scalar(row_t[:, VAR, :], row_t[:, VAR, :], 1.0 / D, LN_EPS, ALU.mult, ALU.add))
                dve.sem_inc(rsqrt_asked, 1)
                dve.wait_ge(sqrt_done, roots)
                link(v.reciprocal(row_t[:, RSTD, :], row_t[:, RSTD, :]))
                link(v.scalar_tensor_tensor(row_t[:, NMR, :], row_t[:, SUM, :], -0.5, row_t[:, RSTD, :],
                                            ALU.mult, ALU.mult))
            row_norm(3)

            def norm_x(_, tiles):
                for b, i in enumerate(tiles):
                    xi = X[:, ds(i, 1), :].rearrange("p a d -> p (a d)")
                    v.tensor_scalar(xi, xi, row_t[:, RSTD, ds(i, 1)], row_t[:, NMR, ds(i, 1)], ALU.mult, ALU.add
                                    ).then_inc(x1_ready, 1)
            in_pairs(dve, NT, norm_x)
            dve.wait_ge(bias1_in, 16)
            link(v.tensor_tensor(bias_s[:, :], bias_s[:, :], bias2_s[:, :], ALU.add))

            def step1(i, last=False):
                add_windows(1, i, 0, last)
                dve.wait_ge(prep_mm, NT + i + 1)
                v.tensor_tensor(Y[:, ds(i, 1), :], MB[:, 0:D].unsqueeze(1), bias_s[:, :].unsqueeze(1),
                                ALU.add).then_inc(prep_done, 1)
                add_windows(1, i, 1, last)
            one_hots(1, 0, 0)
            one_hots(1, 0, 1)
            step1(0)
            with dve.Fori(1, IT - 1) as i:
                step1(i)
            step1(IT - 1, True)

            far_windows(1)

            dve.wait_ge(route_const, 9)
            STEPS = 12

            def route(pair, tiles):
                n = len(tiles)
                done = [0]
                rows = LAST if isinstance(tiles[0], int) and tiles[0] == NT - 1 else P

                def after(ins, spaced=False):
                    done[0] += 1
                    ins.then_inc(route_step, 1)
                    (spaced_wait if spaced else wait_count)(dve, route_step, STEPS * pair + done[0])

                for b, i in enumerate(tiles):
                    dve.wait_ge(sums_mm, NT + i + 1)
                    wait_count(dve, x2_turned, i - 1)
                    wait_count(dve, x2_kept, i - 1)
                    wait_count(dve, x2_stored[b], 16 * pair)
                    v.scalar_tensor_tensor(x2_s[:, b, :], banks[b][:, 0:D], rdeg[:, RS_IN, ds(i, 1)],
                                           Y[:, ds(i, 1), :].rearrange("p a d -> p (a d)"), ALU.mult, ALU.add
                                           ).then_inc(x2_ready, 1)
                dve.wait_ge(x2_ready, tiles[-1] + 1)
                dve.sem_inc(sums_used, n)
                dve.wait_ge(logit_mm, pair + 1)
                after(v.tensor_tensor(logit[:, 0:n, :], banks[4][:, 0:n * NE].rearrange("p (t e) -> p t e", t=n),
                                      bg_s[:, :].unsqueeze(1).to_broadcast([P, n, NE]), ALU.add), spaced=True)
                for t in range(n):
                    last = v.max(top8[:, t, :], logit[:, t, :])
                after(last, spaced=True)
                for t in range(n):
                    last = v.max_index(top8i[:, t, :], top8[:, t, :], logit[:, t, :])
                after(last)
                after(v.tensor_copy(top2f[:, 0:2 * n].rearrange("p (t k) -> p t k", k=2), top8i[:, 0:n, 0:2]))
                after(v.tensor_tensor(pick[:, 0:n, :, :].rearrange("p t k e -> p (t k) e"),
                                      iota_e.unsqueeze(1).to_broadcast([P, 2 * n, NE]),
                                      top2f[:, 0:2 * n].unsqueeze(2).to_broadcast([P, 2 * n, NE]), ALU.is_equal))
                if rows < P:
                    after(v.memset(both[:, 0:n, :], 0.0))
                v.tensor_copy(vals_t[:, ds(tiles[0], n), :], top8[:, 0:n, 0:2])
                after(v.tensor_tensor(both[0:rows, 0:n, :], pick[0:rows, 0:n, 0, :], pick[0:rows, 0:n, 1, :], ALU.add))
                dve.sem_inc(both_ready, 1)
                dve.wait_ge(rank_mm, pair + 1)
                for t in range(n):
                    last = v.tensor_tensor(prod[:, t, :, :], pick[:, t, :, :],
                                           banks[5][:, t * NE:(t + 1) * NE].unsqueeze(1).to_broadcast([P, 2, NE]),
                                           ALU.mult)
                after(last)
                for k in range(4):
                    wait_count(dve, slots_stored[k], 16 * pair)
                after(v.tensor_reduce(rank[:, 0:2 * n], prod[:, 0:n, :, :].rearrange("p t k e -> p (t k) e"), AX, ALU.add))
                v.tensor_copy(ids_s[:, 0:n, :], ids_t[:, ds(tiles[0], n), :])
                v.scalar_tensor_tensor(slotf[:, 0:2 * n], top2f[:, 0:2 * n], float(CAP), rank[:, 0:2 * n],
                                       ALU.mult, ALU.add)
                after(v.tensor_scalar(overf[:, 0:2 * n], rank[:, 0:2 * n], float(CAP), float(OVER), ALU.is_ge, ALU.mult))
                after(v.tensor_tensor(slot_s[:, 0:n, :].rearrange("p t k -> p (t k)"), slotf[:, 0:2 * n],
                                      overf[:, 0:2 * n], ALU.add))
                dve.sem_inc(slots_ready, 1)
                for t in range(n):
                    after(v.tensor_tensor(before, before, both[:, t, :], ALU.add))
                assert rows < P or done[0] == STEPS, done
            in_pairs(dve, NT, route)
            dve.sem_inc(blk_step, 1)

            link(v.tensor_tensor(vals_t[:, :, 1:2], vals_t[:, :, 1:2], vals_t[:, :, 0:1], ALU.subtract))
            dve.sem_inc(rsqrt_asked, 1)
            dve.wait_ge(blk_mm, 1)
            link(v.tensor_scalar(cnt[0:NE, 0:1], banks[4][0:NE, 0:1], float(CAP), float(P - 1), ALU.min, ALU.add))
            link(v.tensor_copy(cnt[0:NE, 1:2].bitcast(I32), cnt[0:NE, 0:1]))
            link(v.tensor_scalar(cnt[0:NE, 1:2].bitcast(I32), cnt[0:NE, 1:2].bitcast(I32), 7, None,
                                 ALU.arith_shift_right))
            link(v.tensor_copy(cnt[0:NE, 2:3], cnt[0:NE, 1:2].bitcast(I32)))
            dve.sem_inc(blk_step, 1)
            dve.wait_ge(blk_mm, 2)
            link(v.tensor_copy(cnt[0:NE, 3:4], banks[5][0:NE, 0:1]))
            link(v.tensor_scalar(reached[0:NE, :], iota_b[0:NE, :], cnt[0:NE, 3:4], None, ALU.is_ge))
            dve.sem_inc(blk_step, 1)
            dve.wait_ge(blk_mm, 3)
            ex, pre = banks[4][0:1, 0:BL], banks[5][0:1, 0:BL]
            v.tensor_scalar(blk_e[:, :], ex, float(NE - 1), None, ALU.min)
            link(v.tensor_scalar(blk_row[0:1, 0, :], ex, float(CAP), None, ALU.mult))
            link(v.tensor_tensor(blk_row[0:1, 1, :], iota_b[0:1, :], pre, ALU.subtract))
            link(v.scalar_tensor_tensor(blk_row[0:1, 2, :], blk_row[0:1, 1, :], float(P), blk_row[0:1, 0, :],
                                        ALU.mult, ALU.add))
            link(v.tensor_scalar(blk_s[:, :], blk_row[0:1, 2, :], float(SLOTS), None, ALU.min))
            link(v.tensor_scalar(cnt[0:1, 4:5], banks[2][0:1, 0:1], 3.0, 1.0, ALU.max, ALU.add))
            link(v.tensor_copy(cnt[0:1, 5:6].bitcast(I32), cnt[0:1, 4:5]))
            link(v.tensor_scalar(blk_n[:, :], cnt[0:1, 5:6].bitcast(I32), 1, None, ALU.arith_shift_right))
            dve.sem_inc(blocks_ready, 1)
            dve.wait_ge(sqrt_done, 4)
            link(v.tensor_scalar(vals_t[:, :, 0:1], vals_t[:, :, 1:2], 1.0, None, ALU.add))
            link(v.reciprocal(vals_t[:, :, 0:1], vals_t[:, :, 0:1]))
            link(v.tensor_tensor(vals_t[:, :, 1:2], vals_t[:, :, 1:2], vals_t[:, :, 0:1], ALU.mult))

            pairs = dve.value_load(blk_n[0:1, 0:1], min_val=2, max_val=(BL - 8) // 2)

            def row_ids(j, b, blk):
                dve.wait_ge(bid_full[b], 16 * (j + 1))
                wait_count(dve, xg_turned, blk - 1)
                v.tensor_scalar(tmp_s[:, 0:1], bid_s[:, b:b + 1], float(N), float(-N), ALU.is_ge, ALU.mult
                                ).then_inc(gid_step, 1)
                dve.wait_ge(gid_step, 3 * blk + 1)
                v.tensor_tensor(tmp_s[:, 1:2], bid_s[:, b:b + 1], tmp_s[:, 0:1], ALU.add).then_inc(gid_step, 1)
                dve.wait_ge(gid_step, 3 * blk + 2)
                v.tensor_scalar(gid_s[:, b:b + 1], tmp_s[:, 1:2], float(N - 1), None, ALU.min).then_inc(gid_step, 1)

            def copy_xT(b, blk):
                dve.wait_ge(xg_turned, blk + 1)
                wait_count(dve, mm1_done, HC * (blk - 1) if not isinstance(blk, int) or blk > 1 else 0)
                v.tensor_copy(xgT[:, b, :, :], banks[b][:, 0:D].rearrange("p (c n) -> p c n", c=DC)
                              ).then_inc(xgT_ready, 1)

            row_ids(0, 0, 0)
            row_ids(0, 1, 1)
            copy_xT(0, 0)

            def blocks(j):
                for b in range(2):
                    blk = 2 * j + b
                    row_ids(j + 1, b, blk + 2)
                    dve.wait_ge(b1_turned, blk + 1)
                    wait_count(dve, gelu_done, HC * (blk - 1) if not isinstance(blk, int) or blk > 1 else 0)
                    v.tensor_copy(b1T[:, b, :], banks[b][:, D:D + HC]).then_inc(b1T_ready, 1)
                    copy_xT(1 - b, blk + 1)
                    dve.wait_ge(mm2_done, blk + 1)
                    wait_count(dve, yo_stored[b], 16 * j)
                    v.tensor_tensor(yo_s[:, b, :], banks[6 + b][:, 0:D], b2_s[:, b, :], ALU.add
                                    ).then_inc(yo_ready, 1)
            blocks(0)
            with dve.Fori(1, pairs) as j:
                blocks(j)

            def add_ya(p, tiles):
                for b, i in enumerate(tiles):
                    dve.wait_ge(y_full[b], 32 * (p + 1))
                    yi = Y[:, ds(i, 1), :].rearrange("p a d -> p (a d)")
                    v.scalar_tensor_tensor(yi, ya_s[:, b, :],
                                           vals_t[:, ds(i, 1), 0:1].rearrange("p a b -> p (a b)"), yi,
                                           ALU.mult, ALU.add).then_inc(ya_added, 1)
            in_pairs(dve, NT, add_ya)

            dve.wait_ge(mean_mm, NT)
            link(v.tensor_scalar(mean_s, banks[0][:, 0:D], 1.0 / N, None, ALU.mult))

            def centre(_, tiles):
                for b, i in enumerate(tiles):
                    v.tensor_tensor(Y[:, ds(i, 1), :], Y[:, ds(i, 1), :], mean_s.unsqueeze(1), ALU.subtract
                                    ).then_inc(centred, 1)
            in_pairs(dve, NT, centre)
            dve.wait_ge(var_mm, NT)
            link(v.tensor_scalar(bn_s[:, 0, :], banks[1][:, 0:D], 1.0 / N, BN_EPS, ALU.mult, ALU.add))
            dve.sem_inc(rsqrt_asked, 1)
            dve.wait_ge(sqrt_done, 5)
            link(v.reciprocal(bn_s[:, 1, :], bn_s[:, 1, :]))
            dve.wait_ge(last_in, 32)
            link(v.tensor_tensor(scale_s, bn_s[:, 1, :], bias2_s[:, :], ALU.mult))
            dve.sem_inc(scale_ready, 1)

            def final_sum(_, tiles):
                for b, i in enumerate(tiles):
                    dve.wait_ge(beta_added, i + 1)
                    dve.wait_ge(scaled, i + 1)
                    v.tensor_tensor(X[:, ds(i, 1), :], X[:, ds(i, 1), :], Y[:, ds(i, 1), :], ALU.add
                                    ).then_inc(summed, 1)
                for b, i in enumerate(tiles):
                    spaced_wait(dve, summed, i + 1)
                    v.bn_stats(stats[:, ds(i, 1), :].rearrange("p a s -> p (a s)"),
                               X[:, ds(i, 1), :].rearrange("p a d -> p (a d)")).then_inc(stats2, 1)
            in_pairs(dve, NT, final_sum)
            dve.wait_ge(stats2, NT)
            row_norm(6)

            def norm_out(p, tiles):
                for b, i in enumerate(tiles):
                    wait_count(dve, out_stored[b], 16 * p)
                    v.tensor_scalar(out_s[:, b, :], X[:, ds(i, 1), :].rearrange("p a d -> p (a d)"),
                                    row_t[:, RSTD, ds(i, 1)], row_t[:, NMR, ds(i, 1)], ALU.mult, ALU.add
                                    ).then_inc(out_ready, 1)
            in_pairs(dve, NT, norm_out)


_INS = ['x', 'src', 'dst', 'L0_gnn_weight', 'L0_gnn_bias', 'L1_gnn_W_gc', 'L1_gnn_b_gc', 'L1_gnn_W_res',
        'L1_gnn_b_res', 'L1_gnn_Wg', 'L1_gnn_bg', 'L1_gnn_w1', 'L1_gnn_b1', 'L1_gnn_w2', 'L1_gnn_b2',
        'L1_gnn_gamma', 'L1_gnn_beta']
_OUTS = [((6250, 256), 'float32')]


def kernel(**inputs):
    import numpy as _np
    import concourse.bacc as _bacc
    from concourse import mybir as _mybir
    from concourse.bass_utils import run_bass_kernel_spmd as _run

    nc = _bacc.Bacc("TRN2", target_bir_lowering=False, num_devices=1)
    arrays, args = {}, []
    for name in _INS:
        a = _np.ascontiguousarray(inputs[name])
        arrays[f"in_{name}_dram"] = a
        args.append(nc.dram_tensor(f"in_{name}_dram", a.shape, _mybir.dt.from_np(a.dtype), kind="ExternalInput").ap())
    for i, (shape, dtype) in enumerate(_OUTS):
        dt = _mybir.dt.from_np(_np.dtype(dtype))
        args.append(nc.dram_tensor(f"out_{i}_dram", shape, dt, kind="ExternalOutput").ap())
    gnn_kernel(nc, *args)
    r = _run(nc, [arrays], core_ids=[0])
    got = tuple(r.results[0][f"out_{i}_dram"] for i in range(len(_OUTS)))
    return got[0]
```

```python
from contextlib import ExitStack

import concourse.bass as bass
from concourse import mybir

F32 = mybir.dt.float32
BF16 = mybir.dt.bfloat16
I32 = mybir.dt.int32
I16 = mybir.dt.int16
U32 = mybir.dt.uint32
ALU = mybir.AluOpType
ACT = mybir.ActivationFunctionType
AX = mybir.AxisListType.X

P = 128
ROW_PAIR = 2 * P
WIN = 64
GROUP = 8
PAIRS = GROUP // 2
SEVEN = 7
PAD = 8191
LN_EPS = 1e-5
BN_EPS = 1e-5
CAP = 1024
OVER = 1 << 20


def ds(start, size):
    return slice(start, start + size) if isinstance(start, int) else bass.ds(start, size)


def wait_count(eng, sem, count):
    if not isinstance(count, int) or count > 0:
        eng.wait_ge(sem, count)


def in_pairs(eng, tiles, body):
    body(0, [0, 1])
    with eng.Fori(1, tiles // 2) as j:
        body(j, [2 * j, 2 * j + 1])
    if tiles % 2:
        body(tiles // 2, [tiles - 1])


def in_sevens(eng, tiles, body):
    n = tiles // SEVEN
    body(0, list(range(SEVEN)))
    with eng.Fori(1, n - 1) as j:
        body(j, [SEVEN * j + b for b in range(SEVEN)])
    body(n - 1, [SEVEN * (n - 1) + b for b in range(SEVEN)])


def gnn_kernel(nc, x, src, dst, w0, bias0, w_gc, b_gc, w_res, b_res, w_gate, b_gate,
               w1, b1, w2, b2, gamma, beta, out):
    N, D = x.shape
    EDGES = src.shape[0]
    NE, _, H = w1.shape
    DC = D // P
    HC = H // P
    NT = -(-N // P)
    LAST = N - (NT - 1) * P
    NPAIR = -(-EDGES // (2 * GROUP * P)) * 2 * PAIRS
    ET = 2 * NPAIR
    NG = ET // GROUP
    IT = NG // 2
    assert IT == NT and NT % 2 == 1 and NT % SEVEN == 0 and D == 2 * P and NE <= P
    FULL = EDGES // ROW_PAIR
    REST = EDGES - FULL * ROW_PAIR
    CH = -(-NPAIR // P)
    LASTROWS = NPAIR - (CH - 1) * P
    ACCW = NT * P + WIN - 16
    assert ACCW >= N + WIN and ACCW >= NT * P
    ASSIGN = 2 * N
    YROWS = 2 * NT * P
    SLOTS = NE * CAP
    MAXBLK = NE + ASSIGN // P
    BL = -(-(MAXBLK + 8) // 8) * 8

    h_d = nc.dram_tensor("h_scratch", (NT * P, D), F32).ap()
    x2_d = nc.dram_tensor("x2_scratch", (NT * P, D), F32).ap()
    y_d = nc.dram_tensor("y_scratch", (YROWS, D), F32).ap()
    slot_d = nc.dram_tensor("slot_scratch", (SLOTS + P, 1), I32).ap()

    with ExitStack() as ctx:
        def sb(name, shape, dt):
            return ctx.enter_context(nc.sbuf_tensor(name, shape, dt))

        def sem(name):
            return ctx.enter_context(nc.semaphore(name))

        acc = sb("acc", [P, DC, ACCW], F32)
        X = sb("X", [P, NT, D], F32)
        Y = sb("Y", [P, NT, D], F32)
        idx_t = sb("idx_t", [P, ET], I32)
        rel_t = sb("rel_t", [P, ET], BF16)
        far_t = sb("far_t", [P, ET], I16)
        lohi_t = sb("lohi_t", [P, 4, ET], BF16)
        win_row = sb("win_row", [1, NPAIR], I32)
        gath = sb("gath", [P, 2, GROUP, D], F32)
        onehot = sb("onehot", [P, 2, GROUP, WIN], F32)
        oh_lo = sb("oh_lo", [P, 2, 2, 4, P], BF16)
        oh_hi = sb("oh_hi", [P, 2, 2, 4, NT], BF16)
        idx_s = sb("idx_s", [P, 2, GROUP], I32)
        xs = sb("xs", [P, D], F32)
        xT = sb("xT", [P, DC, P], F32)
        w0_s = sb("w0_s", [P, 2 * DC, D], F32)
        wgc_s = sb("wgc_s", [P, DC, D], F32)
        wres_s = sb("wres_s", [P, DC, D], F32)
        wg_s = sb("wg_s", [P, DC, NE], F32)
        ident = sb("ident", [P, P], F32)
        iota_w = sb("iota_w", [P, WIN], F32)
        iota_lo = sb("iota_lo", [P, P], BF16)
        iota_hi = sb("iota_hi", [P, NT], BF16)
        bias_s = sb("bias_s", [P, D], F32)
        bias2_s = sb("bias2_s", [P, D], F32)
        zero_s = sb("zero_s", [P, D], F32)
        bg_s = sb("bg_s", [P, NE], F32)
        rdeg = sb("rdeg", [P, 6, NT], F32)
        DEG_IN, DEG_OUT, R_IN, RS_IN, RS_OUT, TMP = range(6)
        flag_s = sb("flag_s", [1, 1], I32)
        small = sb("small", [P, 8], F32)
        ones_f = sb("ones_f", [P, P], F32)
        ids_t = sb("ids_t", [P, NT, 2], I32)
        vals_t = sb("vals_t", [P, NT, 2], F32)
        blk_e = sb("blk_e", [1, BL], I32)
        blk_s = sb("blk_s", [1, BL], I32)
        blk_new = sb("blk_new", [1, BL], I32)
        blk_n = sb("blk_n", [1, 1], I32)

        banks = [ctx.enter_context(nc.psum_tensor(f"bank{i}", [P, 512], F32)) for i in range(8)]
        WINB = banks[0:2]
        HISTB = banks[2:4]
        TB, MB = banks[4], banks[5]

        yflat = Y[:, :, :].rearrange("p t d -> p (t d)")
        cols = CH * ROW_PAIR

        def tab(k):
            return yflat[:, k * cols:(k + 1) * cols]

        srcI, dstI = tab(0).bitcast(I32), tab(1).bitcast(I32)
        srcF, dstF, idxF, relF, farF, tmpF = tab(2), tab(3), tab(4), tab(5), tab(6), tab(7)
        loS, hiS, loD, hiD = tab(8), tab(9), tab(10), tab(11)
        assert 12 * cols <= NT * D
        tables = [idxF, relF, farF, loS, hiS, loD, hiD]
        table_out = [idx_t[:, :], rel_t[:, :], far_t[:, :]] + [lohi_t[:, k, :] for k in range(4)]
        wmin = small[:, 0:CH]

        gflat = gath[:, :, :, :].rearrange("p a k d -> p (a k d)")
        aflat = acc[:, :, :].rearrange("p c n -> p (c n)")
        at = [0]

        def carve(flat, n, pattern=None, dt=F32, **dims):
            a = flat[:, at[0]:at[0] + n]
            at[0] += n
            if dt is not F32:
                a = a.bitcast(dt)
            return a.rearrange(pattern, **dims) if pattern else a

        sums_s = carve(gflat, 2 * D, "p (b c n) -> p b c n", b=2, c=DC)
        x2_s = carve(gflat, 2 * D, "p (b d) -> p b d", b=2)
        junk = carve(gflat, 2 * D, "p (b d) -> p b d", b=2)
        stats = carve(gflat, 6 * NT, "p (t s) -> p t s", s=6)
        row_t = carve(gflat, 8 * NT, "p (k t) -> p k t", k=8)
        SS, RN, SUM, DIFF, VAR, RSTD, NMR, T0 = range(8)
        h_s = carve(gflat, SEVEN * D, "p (b d) -> p b d", b=SEVEN)
        assert at[0] <= 2 * GROUP * D
        x2T = junk.rearrange("p b (c n) -> p b c n", c=DC)
        at[0] = 4 * D + 2 * D
        logit = carve(gflat, 2 * NE, "p (t e) -> p t e", t=2)
        top8 = carve(gflat, 16, "p (t e) -> p t e", t=2)
        top8i = carve(gflat, 16, "p (t e) -> p t e", t=2, dt=U32)
        top2f = carve(gflat, 4)
        pick = carve(gflat, 4 * NE, "p (t k e) -> p t k e", t=2, k=2)
        prod = carve(gflat, 4 * NE, "p (t k e) -> p t k e", t=2, k=2)
        both = carve(gflat, NE, "p (t e) -> p t e", t=2, dt=BF16)
        before = carve(gflat, NE // 2, dt=BF16)
        rank = carve(gflat, 4)
        slotf = carve(gflat, 4)
        overf = carve(gflat, 4)
        slot_s = carve(gflat, 4, "p (t k) -> p t k", t=2, dt=I32)
        ids_s = carve(gflat, 4, "p (t k) -> p t k", t=2, dt=I32)
        iota_e = carve(gflat, NE)
        upper = carve(gflat, P // 2, dt=BF16)
        upto = carve(gflat, NE)
        iota_b = carve(gflat, BL)
        cnt = carve(gflat, 8)
        reached = carve(gflat, BL)
        blk_row = carve(gflat, 4 * BL, "p (k b) -> p k b", k=4)
        ones_b = carve(gflat, P // 2, dt=BF16)
        assert at[0] <= 2 * GROUP * D
        at[0] = 0
        w1_s = carve(aflat, 2 * DC * H, "p (b c h) -> p b c h", b=2, c=DC)
        w2_s = carve(aflat, 2 * HC * D, "p (b c d) -> p b c d", b=2, c=HC)
        b2_s = carve(aflat, 2 * D, "p (b d) -> p b d", b=2)
        xg_s = carve(aflat, 2 * D, "p (b d) -> p b d", b=2)
        xgT = carve(aflat, 2 * D, "p (b c n) -> p b c n", b=2, c=DC)
        hT = carve(aflat, 2 * H, "p (b c n) -> p b c n", b=2, c=HC)
        yo_s = carve(aflat, 2 * D, "p (b d) -> p b d", b=2)
        b1r_s = carve(aflat, 2 * P, "p (b n) -> p b n", b=2)
        b1T = carve(aflat, 2 * HC, "p (b c) -> p b c", b=2)
        bids_all = carve(aflat, BL, dt=I32)
        bids_s = carve(aflat, 2, dt=I32)
        gid_s = carve(aflat, 2, dt=I32)
        tmp_s = carve(aflat, 4)
        ya_s = carve(aflat, SEVEN * D, "p (b d) -> p b d", b=SEVEN)
        yb_s = carve(aflat, SEVEN * D, "p (b d) -> p b d", b=SEVEN)
        sq_s, out_s = ya_s, yb_s
        mean_s = carve(aflat, D)
        scale_s = carve(aflat, D)
        bn_s = carve(aflat, 2 * D, "p (b d) -> p b d", b=2)
        assert at[0] <= DC * ACCW

        fill = gath[:, 1, :, :].rearrange("p k d -> p (k d)")[:, 0:(SLOTS + P) // P].bitcast(I32)

        FARW = 448
        NFAR = NT * P // FARW
        assert NFAR * FARW == NT * P and FARW <= 512 and FARW <= GROUP * WIN
        at[0] = GROUP * D
        iota_far = carve(gflat, FARW)
        far_dst = carve(gflat, 1)
        far_idx = carve(gflat, 1, dt=I32)
        far_rows = gath[:, 0, 0, :]
        far_onehot = onehot[:, 0, :, :].rearrange("p k w -> p (k w)")[:, 0:FARW]

        edges_in = sem("edges_in")
        pads_set = sem("pads_set")
        const_set = sem("const_set")
        weights_in = sem("weights_in")
        dve_step = sem("dve_step")
        tabs_made = sem("tabs_made")
        tabs_turned = sem("tabs_turned")
        tabs_done = sem("tabs_done")
        wmin_turned = sem("wmin_turned")
        win_set = sem("win_set")
        table_fill = sem("table_fill")
        spacer = sem("spacer")
        groups_done = sem("groups_done")
        idx_ready = sem("idx_ready")
        onehot_ready = sem("onehot_ready")
        hist_ready = sem("hist_ready")
        hist_done = sem("hist_done")
        acc_step = sem("acc_step")
        gath_full = [sem(f"gath_full{k}") for k in range(2 * GROUP)]
        xs_full = sem("xs_full")
        x_turned = sem("x_turned")
        xT_ready = sem("xT_ready")
        prep_mm = sem("prep_mm")
        prep_done = sem("prep_done")
        xs1_ready = sem("xs1_ready")
        bias1_ready = sem("bias1_ready")
        bias1_in = sem("bias1_in")
        hist_read = sem("hist_read")
        sqrt_done = sem("sqrt_done")
        sums_final = sem("sums_final")
        far_const = sem("far_const")
        far_taken = [sem(f"far_taken{k}") for k in range(2)]
        far_gath = [sem(f"far_gath{k}") for k in range(2)]
        far_ready = [sem(f"far_ready{k}") for k in range(2)]
        far_mm = [sem(f"far_mm{k}") for k in range(2)]
        far_step = [sem(f"far_step{k}") for k in range(2)]
        fill_set = sem("fill_set")
        slots_cleared = sem("slots_cleared")
        y_cleared = sem("y_cleared")
        deg_ready = sem("deg_ready")
        sums_staged = [sem(f"sums_staged{b}") for b in range(2)]
        sums_mm = sem("sums_mm")
        sums_used = sem("sums_used")
        squares = sem("squares")
        raw_ready = sem("raw_ready")
        stats_done = sem("stats_done")
        x1_ready = sem("x1_ready")
        h_ready = sem("h_ready")
        h_stored = [sem(f"h_stored{b}") for b in range(SEVEN)]
        rsqrt_asked = sem("rsqrt_asked")
        x2_ready = sem("x2_ready")
        x2_kept = sem("x2_kept")
        x2_stored = [sem(f"x2_stored{b}") for b in range(2)]
        x2_turned = sem("x2_turned")
        x2T_ready = sem("x2T_ready")
        logit_mm = sem("logit_mm")
        both_ready = sem("both_ready")
        rank_mm = sem("rank_mm")
        slots_ready = sem("slots_ready")
        route_step = sem("route_step")
        slots_stored = [sem(f"slots_stored{k}") for k in range(4)]
        route_const = sem("route_const")
        blk_mm = sem("blk_mm")
        blk_step = sem("blk_step")
        blocks_ready = sem("blocks_ready")
        bid_full = [sem(f"bid_full{b}") for b in range(2)]
        w1_full = [sem(f"w1_full{b}") for b in range(2)]
        w2_full = [sem(f"w2_full{b}") for b in range(2)]
        gid_step = sem("gid_step")
        xg_full = [sem(f"xg_full{b}") for b in range(2)]
        xg_turned = sem("xg_turned")
        xgT_ready = sem("xgT_ready")
        b1_turned = sem("b1_turned")
        b1T_ready = sem("b1T_ready")
        mm1_done = sem("mm1_done")
        gelu_done = sem("gelu_done")
        mm2_done = sem("mm2_done")
        yo_ready = sem("yo_ready")
        yo_stored = [sem(f"yo_stored{b}") for b in range(2)]
        experts_done = sem("experts_done")
        y_full = [sem(f"y_full{b}") for b in range(SEVEN)]
        ya_added = sem("ya_added")
        yb_added = sem("yb_added")
        mean_mm = sem("mean_mm")
        mean_ready = sem("mean_ready")
        centred = sem("centred")
        sq_ready = sem("sq_ready")
        var_mm = sem("var_mm")
        last_in = sem("last_in")
        beta_added = sem("beta_added")
        scale_ready = sem("scale_ready")
        scaled = sem("scaled")
        summed = sem("summed")
        stats2 = sem("stats2")
        out_ready = sem("out_ready")
        out_stored = [sem(f"out_stored{b}") for b in range(SEVEN)]

        def spaced_wait(eng, s, count):
            if isinstance(count, int):
                wait_count(eng, s, count)
            else:
                eng.wait_ge(s, count)
                eng.sem_inc(spacer, 1)

        def bcast(vec, n=P):
            return vec.rearrange("(a n) -> a n", a=1).to_broadcast([n, vec.shape[0]])

        def load_w2(eng, e, b, cond=None):
            eng.dma_start(w2_s[:, b, :, :], w2[ds(e, 1), :, :].rearrange(
                "a (c p) d -> p (a c) d", p=P), cond=cond).then_inc(w2_full[b], 16)
            eng.dma_start(b2_s[:, b, :], b2[ds(e, 1), :].to_broadcast([P, D]), cond=cond
                         ).then_inc(w2_full[b], 16)

        def weights_of(eng, blk):
            e = eng.value_load(blk_e[0:1, ds(blk, 1)], min_val=0, max_val=NE - 1)
            return e, eng.value_load(blk_new[0:1, ds(blk, 1)], min_val=0, max_val=1) > 0

        block = ctx.enter_context(nc.Block())

        @block.sync
        def _(sp):
            edge_loads = 0
            for vec, t in ((src, srcI), (dst, dstI)):
                tv = t.rearrange("p (c e) -> p c e", c=CH)
                sp.dma_start(tv[:, 0:CH - 1, :], vec[0:(CH - 1) * P * ROW_PAIR].rearrange(
                    "(c p e) -> p c e", p=P, e=ROW_PAIR)).then_inc(edges_in, 16)
                edge_loads += 1
            sp.wait_ge(pads_set, 1)
            n_full = FULL - (CH - 1) * P
            for vec, t in ((src, srcI), (dst, dstI)):
                tv = t.rearrange("p (c e) -> p c e", c=CH)
                sp.dma_start(tv[0:n_full, CH - 1, :], vec[(CH - 1) * P * ROW_PAIR:FULL * ROW_PAIR]
                             .rearrange("(p e) -> p e", e=ROW_PAIR)).then_inc(edges_in, 16)
                sp.dma_start(tv[n_full:n_full + 1, CH - 1, 0:REST],
                             vec[FULL * ROW_PAIR:EDGES].rearrange("(p e) -> p e", p=1)
                             ).then_inc(edges_in, 16)
                edge_loads += 2
            sp.dma_start(w0_s[:, :, :], w0.rearrange("(c p) n -> p c n", p=P)).then_inc(weights_in, 16)
            sp.dma_start(bias_s[:, :], bcast(bias0)).then_inc(weights_in, 16)
            sp.dma_start(wgc_s[:, :, :], w_gc.rearrange("(c p) n -> p c n", p=P)).then_inc(weights_in, 16)
            sp.dma_start(wres_s[:, :, :], w_res.rearrange("(c p) n -> p c n", p=P)).then_inc(weights_in, 16)
            sp.dma_start(wg_s[:, :, :], w_gate.rearrange("(c p) n -> p c n", p=P)).then_inc(weights_in, 16)
            sp.dma_start(bias2_s[:, :], bcast(b_res)).then_inc(weights_in, 16)
            sp.dma_start(bg_s[:, :], bcast(b_gate)).then_inc(weights_in, 16)

            sp.wait_ge(fill_set, 2)
            sp.dma_start(slot_d.rearrange("(p s) a -> p (s a)", p=P), fill).then_inc(slots_cleared, 16)

            def load_x(i, rows=P):
                wait_count(sp, prep_done, 1 * i)
                sp.dma_start(xs[0:rows, :], x[ds(P * i, rows), :]).then_inc(xs_full, 16)

            load_x(0)
            with sp.Fori(1, NT - 1) as i:
                load_x(i)
            load_x(NT - 1, LAST)

            sp.wait_ge(prep_done, NT)
            sp.dma_start(bias_s[:, :], bcast(b_gc)).then_inc(bias1_in, 16)

            def store_h(_, tiles):
                for b, i in enumerate(tiles):
                    sp.wait_ge(h_ready, i + 1)
                    sp.dma_start(h_d[ds(P * i, P), :], h_s[:, b, :]).then_inc(h_stored[b], 16)
            in_sevens(sp, NT, store_h)
            for b in range(SEVEN):
                sp.wait_ge(h_stored[b], 16 * NT // SEVEN)

            def store_x2(_, tiles):
                for b, i in enumerate(tiles):
                    sp.wait_ge(x2_ready, i + 1)
                    sp.dma_start(x2_d[ds(P * i, P), :], x2_s[:, b, :]).then_inc(x2_stored[b], 16)
            in_pairs(sp, NT, store_x2)
            for b in range(2):
                sp.wait_ge(x2_stored[b], 16 * ((NT + 1 - b) // 2))

            sp.wait_ge(blocks_ready, 1)
            pairs = sp.value_load(blk_n[0:1, 0:1], min_val=2, max_val=(BL - 8) // 2)
            n_pair = (NT + 1) // 2
            for k in range(4):
                sp.wait_ge(slots_stored[k], 16 * (n_pair if k < 2 else n_pair - 1))

            def load_ids(blk, b):
                first = sp.value_load(blk_s[0:1, ds(blk, 1)], min_val=0, max_val=SLOTS)
                sp.dma_start(bids_all[:, ds(blk, 1)], slot_d[ds(first, P), :]).then_inc(bid_full[b], 16)

            def load_w1(e, b, cond=None):
                sp.dma_start(w1_s[:, b, :, :], w1[ds(e, 1), :, :].rearrange(
                    "a (c p) h -> p (a c) h", p=P), cond=cond).then_inc(w1_full[b], 16)
                sp.dma_start(b1r_s[0:HC, b, :], b1[ds(e, 1), :].rearrange(
                    "a (c p) -> (a c) p", p=P), cond=cond).then_inc(w1_full[b], 16)

            load_ids(0, 0)
            load_ids(1, 1)
            for b in range(2):
                e = sp.value_load(blk_e[0:1, b:b + 1], min_val=0, max_val=NE - 1)
                load_w1(e, b)
                load_w2(sp, e, b)
            for blk in (2, 3):
                sp.wait_ge(gid_step, 3 * (blk - 1))
                load_ids(blk, blk % 2)
            e, fresh = weights_of(sp, 2)
            sp.wait_ge(mm1_done, HC)
            load_w1(e, 0, fresh)

            with sp.Fori(0, pairs) as j:
                for b in range(2):
                    blk = 2 * j + b
                    spaced_wait(sp, gid_step, 3 * (blk + 3))
                    load_ids(blk + 4, b)
                    e, fresh = weights_of(sp, blk + 3)
                    spaced_wait(sp, mm1_done, HC * (blk + 2))
                    load_w1(e, 1 - b, fresh)
            for b in range(2):
                spaced_wait(sp, yo_stored[b], 16 * pairs)
                spaced_wait(sp, bid_full[b], 16 * (pairs + 2))
                spaced_wait(sp, w1_full[b], 32 * (pairs + 2 - b))
                spaced_wait(sp, w2_full[b], 32 * (pairs + 1))

            sp.wait_ge(y_cleared, 16 * NT)
            sp.dma_start(bias2_s[:, :], bcast(gamma)).then_inc(last_in, 16)
            sp.dma_start(zero_s[:, :], bcast(beta)).then_inc(last_in, 16)

            def load_y(_, tiles):
                for b, i in enumerate(tiles):
                    rows = LAST if isinstance(i, int) and i == NT - 1 else P
                    wait_count(sp, yb_added, i + 1 - SEVEN)
                    sp.dma_start(ya_s[0:rows, b, :], y_d[ds(P * i, rows), :]).then_inc(y_full[b], 16)
                    sp.dma_start(yb_s[0:rows, b, :], y_d[ds(N + P * i, rows), :]).then_inc(y_full[b], 16)
            in_sevens(sp, NT, load_y)

            def store_out(_, tiles):
                for b, i in enumerate(tiles):
                    rows = LAST if isinstance(i, int) and i == NT - 1 else P
                    sp.wait_ge(out_ready, i + 1)
                    sp.dma_start(out[ds(P * i, rows), :], out_s[0:rows, b, :]).then_inc(out_stored[b], 16)
            in_sevens(sp, NT, store_out)
            for b in range(SEVEN):
                sp.wait_ge(out_stored[b], 16 * NT // SEVEN)

        @block.gpsimd
        def _(pool):
            for t in (srcI, dstI):
                pad = pool.memset(t.rearrange("p (c e) -> p c e", c=CH)[:, CH - 1, :], PAD)
            pad.then_inc(pads_set, 1)
            pool.memset(ident[:, :], 0.0).then_inc(const_set, 1)
            pool.memset(ones_f[:, :], 1.0).then_inc(const_set, 1)
            pool.iota(iota_w[:, :], pattern=[[1, WIN]], base=0, channel_multiplier=0,
                      allow_small_or_imprecise_dtypes=True).then_inc(const_set, 1)
            pool.iota(iota_lo[:, :], pattern=[[1, P]], base=0, channel_multiplier=0,
                      allow_small_or_imprecise_dtypes=True).then_inc(const_set, 1)
            pool.iota(iota_hi[:, :], pattern=[[P, NT]], base=0, channel_multiplier=0,
                      allow_small_or_imprecise_dtypes=True).then_inc(const_set, 1)
            pool.wait_ge(const_set, 1)
            pool.affine_select(out=ident[:, :], in_=ident[:, :], compare_op=ALU.not_equal, fill=1.0,
                               base=0, pattern=[[-1, P]], channel_multiplier=1).then_inc(const_set, 1)

            pool.memset(fill, ASSIGN).then_inc(fill_set, 1)
            pool.memset(zero_s[:, :], 0.0).then_inc(fill_set, 1)
            pool.iota(ids_t[:, :, :], pattern=[[P, NT], [N, 2]], base=0, channel_multiplier=1
                      ).then_inc(const_set, 1)
            pool.memset(acc[:, :, :], 0.0).then_inc(acc_step, 1)
            pool.wait_ge(slots_cleared, 16)

            def gather(table, g, step, half):
                spaced_wait(pool, idx_ready, g + 1)
                for k in range(GROUP):
                    pool.indirect_dma_start(
                        out=gath[:, half, k, :], out_offset=None, in_=table,
                        in_offset=bass.IndirectOffsetOnAxis(ap=idx_s[:, half, k:k + 1], axis=0),
                    ).then_inc(gath_full[half * GROUP + k], 16)

            def layer(L, table):
                def step(i):
                    for half in range(2):
                        gather(table, NG * L + 2 * i + half, IT * L + i, half)
                step(0)
                with pool.Fori(1, IT) as i:
                    step(i)

            def far_gathers(L, table):
                pool.wait_ge(acc_step, PAIRS * NG * (L + 1) + 1 + L)
                beyond = pool.value_load(flag_s[0:1, 0:1], min_val=0, max_val=ET * P)
                with pool.If(beyond > 0):
                    pool.iota(iota_far, pattern=[[1, FARW]], base=0, channel_multiplier=0,
                              allow_small_or_imprecise_dtypes=True).then_inc(far_const, 1)
                    with pool.Fori(0, ET) as t:
                        spaced_wait(pool, far_taken[L], t + 1)
                        pool.indirect_dma_start(
                            out=far_rows, out_offset=None, in_=table,
                            in_offset=bass.IndirectOffsetOnAxis(ap=far_idx, axis=0)).then_inc(far_gath[L], 16)

            layer(0, x[:, :])
            far_gathers(0, x[:, :])

            def stage(_, tiles):
                if len(tiles) == 2:
                    spaced_wait(pool, sums_mm, tiles[1] - 1)
                    pool.tensor_copy(sums_s[:, 1, :, :], acc[:, :, ds(P * tiles[1], P)]).then_inc(sums_staged[1], 1)
            pool.wait_ge(sums_final, 1)
            in_pairs(pool, NT, stage)
            for b in range(2):
                pool.wait_ge(sums_staged[b], (NT + 1 - b) // 2)
            pool.memset(acc[:, :, :], 0.0).then_inc(acc_step, 1)

            for b in range(SEVEN):
                pool.wait_ge(h_stored[b], 16 * NT // SEVEN)
            layer(1, h_d)
            far_gathers(1, h_d)

            pool.wait_ge(sums_final, 2)
            pool.iota(iota_e, pattern=[[1, NE]], base=0, channel_multiplier=0,
                      allow_small_or_imprecise_dtypes=True).then_inc(route_const, 1)
            pool.iota(iota_b, pattern=[[1, BL]], base=0, channel_multiplier=0,
                      allow_small_or_imprecise_dtypes=True).then_inc(route_const, 1)
            pool.memset(before, 0.0).then_inc(route_const, 1)
            pool.memset(both, 0.0).then_inc(route_const, 1)
            pool.memset(upper, 1.0).then_inc(route_const, 1)
            pool.memset(ones_b, 1.0).then_inc(route_const, 1)
            pool.memset(upto, 1.0).then_inc(route_const, 1)
            pool.wait_ge(route_const, 7)
            pool.affine_select(out=upper, in_=upper, compare_op=ALU.is_gt, fill=0.0, base=0,
                               pattern=[[1, P]], channel_multiplier=-1).then_inc(route_const, 1)
            pool.affine_select(out=upto, in_=upto, compare_op=ALU.is_ge, fill=0.0, base=0,
                               pattern=[[1, NE]], channel_multiplier=-1).then_inc(route_const, 1)

            def store_slots(pair, tiles):
                spaced_wait(pool, slots_ready, pair + 1)
                for t, i in enumerate(tiles):
                    rows = LAST if isinstance(i, int) and i == NT - 1 else P
                    for k in range(2):
                        pool.indirect_dma_start(
                            out=slot_d, in_=ids_s[0:rows, t, k:k + 1], in_offset=None,
                            out_offset=bass.IndirectOffsetOnAxis(ap=slot_s[0:rows, t, k:k + 1], axis=0),
                            bounds_check=SLOTS - 1, oob_is_err=False).then_inc(slots_stored[2 * t + k], 16)
            in_pairs(pool, NT, store_slots)

            pool.wait_ge(blocks_ready, 1)
            for b in range(2):
                pool.wait_ge(x2_stored[b], 16 * ((NT + 1 - b) // 2))
            pairs = pool.value_load(blk_n[0:1, 0:1], min_val=2, max_val=(BL - 8) // 2)
            pool.wait_ge(y_cleared, 16 * NT)

            def gather_rows(blk, b):
                spaced_wait(pool, gid_step, 3 * (blk + 1))
                pool.indirect_dma_start(
                    out=xg_s[:, b, :], out_offset=None, in_=x2_d,
                    in_offset=bass.IndirectOffsetOnAxis(ap=gid_s[:, b:b + 1], axis=0)).then_inc(xg_full[b], 16)

            for b in range(2):
                gather_rows(b, b)
            pool.wait_ge(xg_turned, 1)
            gather_rows(2, 0)

            def blocks(j):
                for b in range(2):
                    blk = 2 * j + b
                    spaced_wait(pool, xg_turned, blk + 2)
                    gather_rows(blk + 3, 1 - b)
                    spaced_wait(pool, yo_ready, blk + 1)
                    pool.indirect_dma_start(
                        out=y_d, in_=yo_s[:, b, :], in_offset=None,
                        out_offset=bass.IndirectOffsetOnAxis(ap=bids_s[:, b:b + 1], axis=0),
                        bounds_check=ASSIGN - 1, oob_is_err=False).then_inc(yo_stored[b], 16)
            with pool.Fori(0, pairs) as j:
                blocks(j)

            pool.wait_ge(last_in, 32)

            def add_beta(_, tiles):
                for b, i in enumerate(tiles):
                    pool.tensor_tensor(X[:, ds(i, 1), :], X[:, ds(i, 1), :], zero_s[:, :].unsqueeze(1), ALU.add
                                       ).then_inc(beta_added, 1)
            in_pairs(pool, NT, add_beta)
            pool.wait_ge(scale_ready, 1)

            def scale_y(_, tiles):
                for b, i in enumerate(tiles):
                    pool.tensor_tensor(Y[:, ds(i, 1), :], Y[:, ds(i, 1), :], scale_s.unsqueeze(1), ALU.mult
                                       ).then_inc(scaled, 1)
            in_pairs(pool, NT, scale_y)

        @block.scalar
        def _(act):
            n = 0
            for k, (_, o) in enumerate(zip(tables, table_out)):
                for c in range(CH):
                    m = P if c < CH - 1 else LASTROWS
                    act.wait_ge(tabs_turned, n + 1)
                    act.activation(o[:, c * ROW_PAIR:c * ROW_PAIR + 2 * m].rearrange("p (q h) -> p q h", h=2),
                                   banks[4 + n % 4][:, 0:2 * P].rearrange("p (h q) -> p q h", h=2)[:, 0:m, :],
                                   ACT.Copy).then_inc(tabs_done, 1)
                    n += 1

            def stage_idx(L, i):
                for half in range(2):
                    g = NG * L + 2 * i + half
                    spaced_wait(act, groups_done, g - 1)
                    act.activation(idx_s[:, half, :], idx_t[:, ds(2 * GROUP * i + GROUP * half, GROUP)],
                                   ACT.Copy).then_inc(idx_ready, 1)

            act.wait_ge(tabs_done, n)

            def step0(i):
                stage_idx(0, i)
                act.dma_start(y_d[ds(2 * P * i, 2 * P), :].rearrange("(p r) d -> p r d", p=P),
                              zero_s[:, :].unsqueeze(1).to_broadcast([P, 2, D])).then_inc(y_cleared, 16)
                act.wait_ge(x_turned, i + 1)
                act.activation(xT[:, :, :], TB[:, 0:D].rearrange("p (c n) -> p c n", c=DC),
                               ACT.Copy).then_inc(xT_ready, 1)
            act.wait_ge(fill_set, 2)
            step0(0)
            with act.Fori(1, IT) as i:
                step0(i)

            act.wait_ge(deg_ready, 1)
            act.activation(rdeg[:, RS_IN, :], rdeg[:, R_IN, :], ACT.Sqrt)
            act.activation(rdeg[:, RS_OUT, :], rdeg[:, TMP, :], ACT.Sqrt).then_inc(sqrt_done, 1)
            act.wait_ge(sums_final, 1)

            def square(_, tiles):
                spaced_wait(act, sums_mm, tiles[0] - 1)
                act.activation(sums_s[:, 0, :, :], acc[:, :, ds(P * tiles[0], P)], ACT.Copy
                               ).then_inc(sums_staged[0], 1)
                for b, i in enumerate(tiles):
                    spaced_wait(act, squares, i - 1)
                    spaced_wait(act, sums_used, i + 1)
                    act.activation(junk[:, b, :], Y[:, ds(i, 1), :].rearrange("p a d -> p (a d)"), ACT.Square,
                                   accum_out=row_t[:, SS, ds(i, 1)]).then_inc(squares, 1)
            in_pairs(act, NT, square)
            act.wait_ge(squares, NT)
            act.activation(row_t[:, RN, :], row_t[:, SS, :], ACT.Sqrt).then_inc(sqrt_done, 1)
            act.wait_ge(rsqrt_asked, 1)
            act.activation(row_t[:, RSTD, :], row_t[:, VAR, :], ACT.Sqrt).then_inc(sqrt_done, 1)

            def scale_h(group, tiles):
                for b, i in enumerate(tiles):
                    spaced_wait(act, h_stored[b], 16 * group)
                    spaced_wait(act, x1_ready, i + 1)
                    act.activation(h_s[:, b, :], X[:, ds(i, 1), :].rearrange("p a d -> p (a d)"), ACT.Copy,
                                   scale=rdeg[:, RS_OUT, ds(i, 1)]).then_inc(h_ready, 1)
            in_sevens(act, NT, scale_h)

            def step1(i):
                stage_idx(1, i)
                spaced_wait(act, x_turned, NT + i)
                act.activation(xs[:, :], X[:, ds(i, 1), :].rearrange("p a d -> p (a d)"), ACT.Copy
                               ).then_inc(xs1_ready, 1)
                act.wait_ge(x_turned, NT + i + 1)
                act.activation(xT[:, :, :], TB[:, 0:D].rearrange("p (c n) -> p c n", c=DC),
                               ACT.Copy).then_inc(xT_ready, 1)
            step1(0)
            with act.Fori(1, IT) as i:
                step1(i)

            def stage_x2(_, tiles):
                for b, i in enumerate(tiles):
                    spaced_wait(act, sums_mm, NT + i - 1)
                    act.activation(sums_s[:, b, :, :], acc[:, :, ds(P * i, P)], ACT.Copy
                                   ).then_inc(sums_staged[b], 1)
                for b, i in enumerate(tiles):
                    spaced_wait(act, x2_ready, i + 1)
                    act.activation(Y[:, ds(i, 1), :].rearrange("p a d -> p (a d)"), x2_s[:, b, :], ACT.Copy
                                   ).then_inc(x2_kept, 1)
                    act.wait_ge(x2_turned, i + 1)
                    act.activation(x2T[:, b, :, :], banks[2 + b][:, 0:D].rearrange("p (c n) -> p c n", c=DC),
                                   ACT.Copy).then_inc(x2T_ready, 1)
            act.wait_ge(sums_final, 2)
            in_pairs(act, NT, stage_x2)
            act.wait_ge(rsqrt_asked, 2)
            act.activation(vals_t[:, :, 1:2], vals_t[:, :, 1:2], ACT.Exp).then_inc(sqrt_done, 1)

            act.wait_ge(blocks_ready, 1)
            pairs = act.value_load(blk_n[0:1, 0:1], min_val=2, max_val=(BL - 8) // 2)

            def gelus(blk, b):
                act.wait_ge(b1T_ready, blk + 1)
                wait_count(act, mm2_done, blk - 1)
                for c in range(HC):
                    act.wait_ge(mm1_done, HC * blk + c + 1)
                    act.activation(hT[:, b, c, :], banks[2 + c][:, 0:P], ACT.Gelu,
                                   bias=b1T[:, b, c:c + 1]).then_inc(gelu_done, 1)
            gelus(0, 0)
            def hidden(j):
                for b in range(2):
                    blk = 2 * j + b
                    gelus(blk + 1, 1 - b)
                    e, fresh = weights_of(act, blk + 2)
                    spaced_wait(act, yo_ready, blk + 1)
                    load_w2(act, e, b, fresh)
            hidden(0)
            with act.Fori(1, pairs) as j:
                hidden(j)

            def square_y(_, tiles):
                for b, i in enumerate(tiles):
                    spaced_wait(act, var_mm, i + 1 - SEVEN)
                    spaced_wait(act, centred, i + 1)
                    act.activation(sq_s[:, b, :], Y[:, ds(i, 1), :].rearrange("p a d -> p (a d)"), ACT.Square
                                   ).then_inc(sq_ready, 1)
            in_sevens(act, NT, square_y)
            act.wait_ge(rsqrt_asked, 3)
            act.activation(bn_s[:, 1, :], bn_s[:, 0, :], ACT.Sqrt).then_inc(sqrt_done, 1)
            act.wait_ge(rsqrt_asked, 4)
            act.activation(row_t[:, RSTD, :], row_t[:, VAR, :], ACT.Sqrt).then_inc(sqrt_done, 1)

        @block.tensor
        def _(pe):
            pe.wait_ge(const_set, 6)
            n = 0
            for k, t in enumerate(tables):
                for c in range(CH):
                    m = P if c < CH - 1 else LASTROWS
                    pe.wait_ge(tabs_made, k + 1)
                    if n >= 4:
                        pe.wait_ge(tabs_done, n - 3)
                    for h in range(2):
                        last = pe.transpose(banks[4 + n % 4][:, h * P:h * P + m],
                                            t[0:m, c * ROW_PAIR + h * P:c * ROW_PAIR + (h + 1) * P],
                                            ident[0:m, 0:m])
                    last.then_inc(tabs_turned, 1)
                    n += 1
            pe.wait_ge(tabs_made, len(tables) + 1)
            for c in range(CH):
                pe.transpose(banks[0][0:1, c * P:(c + 1) * P], wmin[:, c:c + 1], ident[:, :])
            pe.matmul(banks[1][0:1, 0:1], small[:, 5:6], ones_f[:, 0:1], start=True, stop=True
                      ).then_inc(wmin_turned, 1)
            pe.wait_ge(win_set, 1)
            pe.wait_ge(tabs_done, n)
            pe.wait_ge(weights_in, 7 * 16)

            def sums(L, i, half):
                g = NG * L + 2 * i + half
                pe.wait_ge(onehot_ready, g + 1)
                wait_count(pe, acc_step, PAIRS * (g - 1) + 1 + L if not isinstance(g, int) or g > 1 else 0)
                for q in range(PAIRS):
                    for k in (2 * q, 2 * q + 1):
                        pe.wait_ge(gath_full[half * GROUP + k], 16 * (IT * L + i + 1))
                    for c in range(DC):
                        for k in (2 * q, 2 * q + 1):
                            last = pe.matmul(WINB[half][:, q * P + c * WIN:q * P + (c + 1) * WIN],
                                             gath[:, half, k, c * P:(c + 1) * P], onehot[:, half, k, :],
                                             start=(k == 2 * q), stop=(k == 2 * q + 1))
                    if q == PAIRS - 1:
                        last.then_inc(groups_done, 1)
                if L == 0:
                    for b in range(2):
                        pe.wait_ge(hist_ready, 2 * g + b + 1)
                        for t in range(4):
                            for s in range(2):
                                last = pe.matmul(HISTB[s][:, 0:NT], oh_lo[:, b, s, t, :], oh_hi[:, b, s, t, :],
                                                 start=isinstance(g, int) and g + b + t == 0,
                                                 stop=isinstance(g, int) and g == NG - 1 and b + t == 4)
                        last.then_inc(hist_done, 1)

            def prep(L, i, w, sem_xs, unit):
                pe.wait_ge(sem_xs, unit * (i + 1))
                for c in range(DC):
                    last = pe.transpose(TB[:, c * P:(c + 1) * P], xs[:, c * P:(c + 1) * P], ident[:, :])
                last.then_inc(x_turned, 1)
                pe.wait_ge(xT_ready, NT * L + i + 1)
                wait_count(pe, prep_done, NT * L + i)
                for c in range(DC):
                    last = pe.matmul(MB[:, 0:D], xT[:, c, :], w[:, c, :], start=(c == 0), stop=(c == DC - 1))
                last.then_inc(prep_mm, 1)

            def step0(i):
                sums(0, i, 0)
                prep(0, i, w0_s, xs_full, 16)
                sums(0, i, 1)
            step0(0)
            with pe.Fori(1, IT - 1) as i:
                step0(i)
            step0(IT - 1)

            def far_sums(L):
                pe.wait_ge(acc_step, PAIRS * NG * (L + 1) + 1 + L)
                beyond = pe.value_load(flag_s[0:1, 0:1], min_val=0, max_val=ET * P)
                with pe.If(beyond > 0):
                    with pe.Fori(0, ET) as t:
                        spaced_wait(pe, far_gath[L], 16 * (t + 1))
                        with pe.Fori(0, NFAR) as w:
                            pe.wait_ge(far_ready[L], NFAR * t + w + 1)
                            for c in range(DC):
                                last = pe.matmul(WINB[c][:, 0:FARW], far_rows[:, c * P:(c + 1) * P], far_onehot,
                                                 start=True, stop=True)
                            last.then_inc(far_mm[L], 1)

            def product(L, w, c0):
                def body(pair, tiles):
                    for b, i in enumerate(tiles):
                        pe.wait_ge(sums_staged[b], L * ((NT + 1 - b) // 2) + pair + 1)
                        wait_count(pe, sums_used, NT * L + i - 1)
                        for c in range(DC):
                            last = pe.matmul(banks[b][:, 0:D], sums_s[:, b, c, :], w[:, c0 + c, :],
                                             start=(c == 0), stop=(c == DC - 1))
                        last.then_inc(sums_mm, 1)
                return body
            far_sums(0)
            pe.wait_ge(sums_final, 1)
            in_pairs(pe, NT, product(0, w0_s, DC))

            def step1(i):
                sums(1, i, 0)
                prep(1, i, wres_s, xs1_ready, 1)
                sums(1, i, 1)
            pe.wait_ge(acc_step, PAIRS * NG + 2)
            pe.wait_ge(sums_used, NT)
            step1(0)
            with pe.Fori(1, IT) as i:
                step1(i)

            far_sums(1)
            pe.wait_ge(sums_final, 2)
            pe.wait_ge(route_const, 9)
            agg = product(1, wgc_s, 0)

            def route(pair, tiles):
                agg(pair, tiles)
                for b, i in enumerate(tiles):
                    pe.wait_ge(x2_ready, i + 1)
                    for c in range(DC):
                        last = pe.transpose(banks[2 + b][:, c * P:(c + 1) * P], x2_s[:, b, c * P:(c + 1) * P],
                                            ident[:, :])
                    last.then_inc(x2_turned, 1)
                for b, i in enumerate(tiles):
                    pe.wait_ge(x2T_ready, i + 1)
                    for c in range(DC):
                        last = pe.matmul(banks[4][:, b * NE:(b + 1) * NE], x2T[:, b, c, :], wg_s[:, c, :],
                                         start=(c == 0), stop=(c == DC - 1))
                last.then_inc(logit_mm, 1)
                pe.wait_ge(both_ready, pair + 1)
                for b, i in enumerate(tiles):
                    o = banks[5][:, b * NE:(b + 1) * NE]
                    pe.matmul(o, ones_b, before, start=True, stop=False)
                    if b:
                        pe.matmul(o, ones_b, both[:, 0, :], start=False, stop=False)
                    last = pe.matmul(o, upper, both[:, b, :], start=False, stop=True)
                last.then_inc(rank_mm, 1)
            in_pairs(pe, NT, route)

            pe.wait_ge(blk_step, 1)
            pe.matmul(banks[4][0:NE, 0:1], before, ones_b[:, 0:1], start=True, stop=True).then_inc(blk_mm, 1)
            pe.wait_ge(blk_step, 2)
            pe.matmul(banks[5][0:NE, 0:1], upto[0:NE, :], cnt[0:NE, 2:3], start=True, stop=True
                      ).then_inc(blk_mm, 1)
            pe.wait_ge(blk_step, 3)
            pe.matmul(banks[4][0:1, 0:BL], ones_f[0:NE, 0:1], reached[0:NE, :], start=True, stop=True)
            pe.matmul(banks[5][0:1, 0:BL], cnt[0:NE, 2:3], reached[0:NE, :], start=True, stop=True)
            pe.matmul(banks[2][0:1, 0:1], ones_f[0:NE, 0:1], cnt[0:NE, 2:3], start=True, stop=True
                      ).then_inc(blk_mm, 1)

            pe.wait_ge(blocks_ready, 1)
            pairs = pe.value_load(blk_n[0:1, 0:1], min_val=2, max_val=(BL - 8) // 2)

            def turn(blk, n_before, b):
                pe.wait_ge(xg_full[b], 16 * (n_before + 1))
                wait_count(pe, xgT_ready, blk - 1)
                wait_count(pe, b1T_ready, blk - 1)
                for c in range(DC):
                    last = pe.transpose(banks[b][:, c * P:(c + 1) * P], xg_s[:, b, c * P:(c + 1) * P], ident[:, :])
                last.then_inc(xg_turned, 1)

            def product1(blk, n_before, b):
                pe.wait_ge(w1_full[b], 32 * (n_before + 1))
                spaced_wait(pe, xgT_ready, blk + 1)
                pe.transpose(banks[b][:, D:D + HC], b1r_s[0:HC, b, :], ident[0:HC, 0:HC]).then_inc(b1_turned, 1)
                for c in range(HC):
                    wait_count(pe, gelu_done, HC * (blk - 1) + c + 1 if not isinstance(blk, int) or blk > 0 else 0)
                    for d in range(DC):
                        last = pe.matmul(banks[2 + c][:, 0:P], w1_s[:, b, d, c * P:(c + 1) * P],
                                         xgT[:, b, d, :], start=(d == 0), stop=(d == DC - 1))
                    last.then_inc(mm1_done, 1)

            def product2(blk, n_before, b):
                wait_count(pe, yo_ready, blk - 1)
                pe.wait_ge(w2_full[b], 32 * (n_before + 1))
                for c in range(HC):
                    pe.wait_ge(gelu_done, HC * blk + c + 1)
                    last = pe.matmul(banks[6 + b][:, 0:D], hT[:, b, c, :], w2_s[:, b, c, :],
                                     start=(c == 0), stop=(c == HC - 1))
                    if c == HC // 2 - 1:
                        turn(blk + 2, n_before + 1, b)
                last.then_inc(mm2_done, 1)

            turn(0, 0, 0)
            turn(1, 0, 1)
            product1(0, 0, 0)

            def experts(j):
                for b in range(2):
                    blk = 2 * j + b
                    product1(blk + 1, j + b, 1 - b)
                    product2(blk, j, b)
            experts(0)
            with pe.Fori(1, pairs) as j:
                experts(j)

            def col_sums(bank, data, ready, done):
                def body(_, tiles):
                    for b, i in enumerate(tiles):
                        rows = LAST if isinstance(i, int) and i == NT - 1 else P
                        pe.wait_ge(ready, i + 1)
                        pe.matmul(bank[:, 0:D], ones_f[0:rows, :], data(b, i)[0:rows, :],
                                  start=isinstance(i, int) and i == 0, stop=isinstance(i, int) and i == NT - 1
                                  ).then_inc(done, 1)
                return body
            in_sevens(pe, NT, col_sums(banks[0], lambda b, i: Y[:, ds(i, 1), :].rearrange("p a d -> p (a d)"),
                                       yb_added, mean_mm))
            in_sevens(pe, NT, col_sums(banks[1], lambda b, i: sq_s[:, b, :], sq_ready, var_mm))

        @block.vector
        def _(dve):
            steps = [0]

            def link(ins):
                steps[0] += 1
                ins.then_inc(dve_step, 1)
                dve.wait_ge(dve_step, steps[0])

            v = nc.vector
            dve.wait_ge(pads_set, 1)
            dve.wait_ge(edges_in, 6 * 16)
            v.tensor_scalar(loS.bitcast(I32), srcI, P - 1, None, ALU.bitwise_and)
            v.tensor_scalar(loD.bitcast(I32), dstI, P - 1, None, ALU.bitwise_and)
            v.tensor_copy(srcF, srcI)
            link(v.tensor_copy(dstF, dstI))
            v.tensor_copy(tmpF, loS.bitcast(I32))
            link(v.tensor_copy(relF, loD.bitcast(I32)))
            v.tensor_tensor(hiS, srcF, tmpF, ALU.subtract)
            v.tensor_tensor(hiD, dstF, relF, ALU.subtract)
            v.tensor_copy(loS, tmpF)
            v.tensor_copy(loD, relF)
            link(v.tensor_scalar(idxF, srcF, float(N - 1), None, ALU.min))
            link(v.tensor_reduce(wmin, dstF.rearrange("p (c e) -> p c e", c=CH), AX, ALU.min))
            link(v.tensor_scalar(wmin, wmin, float(N - 1), None, ALU.min))
            for c in range(CH):
                last = v.tensor_scalar(relF[:, c * ROW_PAIR:(c + 1) * ROW_PAIR],
                                       dstF[:, c * ROW_PAIR:(c + 1) * ROW_PAIR], wmin[:, c:c + 1], None,
                                       ALU.subtract)
            link(last)
            link(v.tensor_scalar(tmpF, relF, float(WIN), None, ALU.is_ge))
            link(v.scalar_tensor_tensor(farF, dstF, 1.0, tmpF, ALU.add, ALU.mult))
            link(v.tensor_scalar(farF, farF, -1.0, None, ALU.add))
            link(v.scalar_tensor_tensor(tmpF, dstF, float(N), tmpF, ALU.is_lt, ALU.mult))
            link(v.tensor_reduce(small[:, 5:6], tmpF, AX, ALU.add))
            dve.sem_inc(tabs_made, len(tables) + 1)
            dve.wait_ge(wmin_turned, 1)
            v.tensor_copy(win_row[0:1, :], banks[0][0:1, 0:NPAIR])
            link(v.tensor_copy(flag_s[:, :], banks[1][0:1, 0:1]))
            dve.sem_inc(win_set, 1)
            dve.wait_ge(tabs_done, len(tables) * CH)
            dve.wait_ge(weights_in, 7 * 16)

            def one_hots(L, i, half):
                g = NG * L + 2 * i + half
                wait_count(dve, groups_done, g - 1)
                v.tensor_tensor(onehot[:, half, :, :],
                                iota_w[:, :].unsqueeze(1).to_broadcast([P, GROUP, WIN]),
                                rel_t[:, ds(2 * GROUP * i + GROUP * half, GROUP)].unsqueeze(2)
                                .to_broadcast([P, GROUP, WIN]), ALU.is_equal).then_inc(onehot_ready, 1)

            def degree_one_hots(i, half):
                g = 2 * i + half
                for b in range(2):
                    wait_count(dve, hist_done, 2 * g + b - 1)
                    for s in range(2):
                        for o, io, w, part in ((oh_lo, iota_lo, P, 0), (oh_hi, iota_hi, NT, 1)):
                            last = v.tensor_tensor(
                                o[:, b, s, :, :], io[:, :].unsqueeze(1).to_broadcast([P, 4, w]),
                                lohi_t[:, 2 * s + part, ds(2 * GROUP * i + GROUP * half + 4 * b, 4)]
                                .unsqueeze(2).to_broadcast([P, 4, w]), ALU.is_equal)
                    last.then_inc(hist_ready, 1)


            def add_windows(L, i, half, last=False):
                g = NG * L + 2 * i + half
                first = [dve.value_load(win_row[0:1, ds(2 * PAIRS * i + PAIRS * half + q, 1)],
                                        min_val=0, max_val=N - 1) for q in range(PAIRS)]
                dve.wait_ge(groups_done, g + 1)
                if not last:
                    one_hots(L, i + 1, half)
                if L == 0 and not (last and half == 1):
                    degree_one_hots(i + half, 1 - half)
                for q in range(PAIRS):
                    dve.wait_ge(acc_step, PAIRS * g + q + 1 + L)
                    a = acc[:, :, bass.ds(first[q], WIN)]
                    v.tensor_tensor(a, a, WINB[half][:, q * P:(q + 1) * P].rearrange(
                        "p (c w) -> p c w", c=DC), ALU.add).then_inc(acc_step, 1)

            one_hots(0, 0, 0)
            degree_one_hots(0, 0)
            one_hots(0, 0, 1)

            def step0(i, last=False):
                add_windows(0, i, 0, last)
                dve.wait_ge(prep_mm, i + 1)
                v.tensor_copy(Y[:, ds(i, 1), :], MB[:, 0:D].unsqueeze(1))
                v.tensor_tensor(X[:, ds(i, 1), :], xs[:, :].unsqueeze(1), bias_s[:, :].unsqueeze(1),
                                ALU.add).then_inc(prep_done, 1)
                add_windows(0, i, 1, last)
            step0(0)
            with dve.Fori(1, IT - 1) as i:
                step0(i)
            step0(IT - 1, True)

            def far_windows(L):
                dve.wait_ge(acc_step, PAIRS * NG * (L + 1) + 1 + L)
                beyond = dve.value_load(flag_s[0:1, 0:1], min_val=0, max_val=ET * P)
                with dve.If(beyond > 0):
                    dve.wait_ge(far_const, L + 1)
                    with dve.Fori(0, ET) as t:
                        v.tensor_copy(far_idx, idx_t[:, bass.ds(t, 1)])
                        v.tensor_copy(far_dst, far_t[:, bass.ds(t, 1)]).then_inc(far_step[L], 1)
                        spaced_wait(dve, far_step[L], (NFAR + 1) * t + 1)
                        dve.sem_inc(far_taken[L], 1)
                        with dve.Fori(0, NFAR) as w:
                            v.tensor_scalar(far_onehot, iota_far, far_dst, None, ALU.is_equal
                                            ).then_inc(far_ready[L], 1)
                            dve.wait_ge(far_mm[L], NFAR * t + w + 1)
                            v.tensor_scalar(far_dst, far_dst, float(-FARW), None, ALU.add)
                            for c in range(DC):
                                a = acc[:, c, bass.ds(FARW * w, FARW)]
                                last = v.tensor_tensor(a, a, WINB[c][:, 0:FARW], ALU.add)
                            last.then_inc(far_step[L], 1)
                            spaced_wait(dve, far_step[L], (NFAR + 1) * t + w + 2)
                dve.sem_inc(sums_final, 1)
            far_windows(0)

            dve.wait_ge(hist_done, 2 * NG)
            v.tensor_scalar(rdeg[:, DEG_IN, :], HISTB[1][:, 0:NT], 1.0, None, ALU.max)
            link(v.tensor_scalar(rdeg[:, DEG_OUT, :], HISTB[0][:, 0:NT], 1.0, None, ALU.max))
            v.reciprocal(rdeg[:, R_IN, :], rdeg[:, DEG_IN, :])
            link(v.reciprocal(rdeg[:, TMP, :], rdeg[:, DEG_OUT, :]))
            dve.sem_inc(deg_ready, 1)

            def combine(_, tiles):
                for b, i in enumerate(tiles):
                    dve.wait_ge(sums_mm, i + 1)
                    yi = Y[:, ds(i, 1), :].rearrange("p a d -> p (a d)")
                    v.scalar_tensor_tensor(yi, banks[b][:, 0:D], rdeg[:, R_IN, ds(i, 1)], yi, ALU.mult, ALU.add
                                           ).then_inc(sums_used, 1)
            in_pairs(dve, NT, combine)
            dve.wait_ge(sqrt_done, 2)
            link(v.reciprocal(row_t[:, RN, :], row_t[:, RN, :]))

            def residual(_, tiles):
                for b, i in enumerate(tiles):
                    xi = X[:, ds(i, 1), :].rearrange("p a d -> p (a d)")
                    v.scalar_tensor_tensor(xi, Y[:, ds(i, 1), :].rearrange("p a d -> p (a d)"),
                                           row_t[:, RN, ds(i, 1)], xi, ALU.mult, ALU.add).then_inc(raw_ready, 1)
                for b, i in enumerate(tiles):
                    spaced_wait(dve, raw_ready, i + 1)
                    v.bn_stats(stats[:, ds(i, 1), :].rearrange("p a s -> p (a s)"),
                               X[:, ds(i, 1), :].rearrange("p a d -> p (a d)")).then_inc(stats_done, 1)
            in_pairs(dve, NT, residual)
            dve.wait_ge(stats_done, NT)

            def row_norm(roots):
                me, ve, mo, vo = (stats[:, :, k] for k in (1, 2, 4, 5))
                v.tensor_tensor(row_t[:, SUM, :], me, mo, ALU.add)
                v.tensor_tensor(row_t[:, VAR, :], ve, vo, ALU.add)
                link(v.tensor_tensor(row_t[:, DIFF, :], me, mo, ALU.subtract))
                link(v.tensor_tensor(row_t[:, DIFF, :], row_t[:, DIFF, :], row_t[:, DIFF, :], ALU.mult))
                link(v.scalar_tensor_tensor(row_t[:, VAR, :], row_t[:, DIFF, :], D / 4.0, row_t[:, VAR, :],
                                            ALU.mult, ALU.add))
                link(v.tensor_scalar(row_t[:, VAR, :], row_t[:, VAR, :], 1.0 / D, LN_EPS, ALU.mult, ALU.add))
                dve.sem_inc(rsqrt_asked, 1)
                dve.wait_ge(sqrt_done, roots)
                link(v.reciprocal(row_t[:, RSTD, :], row_t[:, RSTD, :]))
                link(v.scalar_tensor_tensor(row_t[:, NMR, :], row_t[:, SUM, :], -0.5, row_t[:, RSTD, :],
                                            ALU.mult, ALU.mult))
            row_norm(3)

            def norm_x(_, tiles):
                for b, i in enumerate(tiles):
                    xi = X[:, ds(i, 1), :].rearrange("p a d -> p (a d)")
                    v.tensor_scalar(xi, xi, row_t[:, RSTD, ds(i, 1)], row_t[:, NMR, ds(i, 1)], ALU.mult, ALU.add
                                    ).then_inc(x1_ready, 1)
            in_pairs(dve, NT, norm_x)
            dve.wait_ge(bias1_in, 16)
            link(v.tensor_tensor(bias_s[:, :], bias_s[:, :], bias2_s[:, :], ALU.add))

            def step1(i, last=False):
                add_windows(1, i, 0, last)
                dve.wait_ge(prep_mm, NT + i + 1)
                v.tensor_tensor(Y[:, ds(i, 1), :], MB[:, 0:D].unsqueeze(1), bias_s[:, :].unsqueeze(1),
                                ALU.add).then_inc(prep_done, 1)
                add_windows(1, i, 1, last)
            one_hots(1, 0, 0)
            one_hots(1, 0, 1)
            step1(0)
            with dve.Fori(1, IT - 1) as i:
                step1(i)
            step1(IT - 1, True)

            far_windows(1)

            dve.wait_ge(route_const, 9)
            STEPS = 12

            def route(pair, tiles):
                n = len(tiles)
                done = [0]
                rows = LAST if isinstance(tiles[0], int) and tiles[0] == NT - 1 else P

                def after(ins, spaced=False):
                    done[0] += 1
                    ins.then_inc(route_step, 1)
                    (spaced_wait if spaced else wait_count)(dve, route_step, STEPS * pair + done[0])

                for b, i in enumerate(tiles):
                    dve.wait_ge(sums_mm, NT + i + 1)
                    wait_count(dve, x2_turned, i - 1)
                    wait_count(dve, x2_kept, i - 1)
                    wait_count(dve, x2_stored[b], 16 * pair)
                    v.scalar_tensor_tensor(x2_s[:, b, :], banks[b][:, 0:D], rdeg[:, RS_IN, ds(i, 1)],
                                           Y[:, ds(i, 1), :].rearrange("p a d -> p (a d)"), ALU.mult, ALU.add
                                           ).then_inc(x2_ready, 1)
                dve.wait_ge(x2_ready, tiles[-1] + 1)
                dve.sem_inc(sums_used, n)
                dve.wait_ge(logit_mm, pair + 1)
                after(v.tensor_tensor(logit[:, 0:n, :], banks[4][:, 0:n * NE].rearrange("p (t e) -> p t e", t=n),
                                      bg_s[:, :].unsqueeze(1).to_broadcast([P, n, NE]), ALU.add), spaced=True)
                for t in range(n):
                    last = v.max(top8[:, t, :], logit[:, t, :])
                after(last, spaced=True)
                for t in range(n):
                    last = v.max_index(top8i[:, t, :], top8[:, t, :], logit[:, t, :])
                after(last)
                after(v.tensor_copy(top2f[:, 0:2 * n].rearrange("p (t k) -> p t k", k=2), top8i[:, 0:n, 0:2]))
                after(v.tensor_tensor(pick[:, 0:n, :, :].rearrange("p t k e -> p (t k) e"),
                                      iota_e.unsqueeze(1).to_broadcast([P, 2 * n, NE]),
                                      top2f[:, 0:2 * n].unsqueeze(2).to_broadcast([P, 2 * n, NE]), ALU.is_equal))
                if rows < P:
                    after(v.memset(both[:, 0:n, :], 0.0))
                v.tensor_copy(vals_t[:, ds(tiles[0], n), :], top8[:, 0:n, 0:2])
                after(v.tensor_tensor(both[0:rows, 0:n, :], pick[0:rows, 0:n, 0, :], pick[0:rows, 0:n, 1, :], ALU.add))
                dve.sem_inc(both_ready, 1)
                dve.wait_ge(rank_mm, pair + 1)
                for t in range(n):
                    last = v.tensor_tensor(prod[:, t, :, :], pick[:, t, :, :],
                                           banks[5][:, t * NE:(t + 1) * NE].unsqueeze(1).to_broadcast([P, 2, NE]),
                                           ALU.mult)
                after(last)
                for k in range(4):
                    wait_count(dve, slots_stored[k], 16 * pair)
                after(v.tensor_reduce(rank[:, 0:2 * n], prod[:, 0:n, :, :].rearrange("p t k e -> p (t k) e"), AX, ALU.add))
                v.tensor_copy(ids_s[:, 0:n, :], ids_t[:, ds(tiles[0], n), :])
                v.scalar_tensor_tensor(slotf[:, 0:2 * n], top2f[:, 0:2 * n], float(CAP), rank[:, 0:2 * n],
                                       ALU.mult, ALU.add)
                after(v.tensor_scalar(overf[:, 0:2 * n], rank[:, 0:2 * n], float(CAP), float(OVER), ALU.is_ge, ALU.mult))
                after(v.tensor_tensor(slot_s[:, 0:n, :].rearrange("p t k -> p (t k)"), slotf[:, 0:2 * n],
                                      overf[:, 0:2 * n], ALU.add))
                dve.sem_inc(slots_ready, 1)
                for t in range(n):
                    after(v.tensor_tensor(before, before, both[:, t, :], ALU.add))
                assert rows < P or done[0] == STEPS, done
            in_pairs(dve, NT, route)
            dve.sem_inc(blk_step, 1)

            link(v.tensor_tensor(vals_t[:, :, 1:2], vals_t[:, :, 1:2], vals_t[:, :, 0:1], ALU.subtract))
            dve.sem_inc(rsqrt_asked, 1)
            dve.wait_ge(blk_mm, 1)
            link(v.tensor_scalar(cnt[0:NE, 0:1], banks[4][0:NE, 0:1], float(CAP), float(P - 1), ALU.min, ALU.add))
            link(v.tensor_copy(cnt[0:NE, 1:2].bitcast(I32), cnt[0:NE, 0:1]))
            link(v.tensor_scalar(cnt[0:NE, 1:2].bitcast(I32), cnt[0:NE, 1:2].bitcast(I32), 7, None,
                                 ALU.arith_shift_right))
            link(v.tensor_copy(cnt[0:NE, 2:3], cnt[0:NE, 1:2].bitcast(I32)))
            dve.sem_inc(blk_step, 1)
            dve.wait_ge(blk_mm, 2)
            link(v.tensor_copy(cnt[0:NE, 3:4], banks[5][0:NE, 0:1]))
            link(v.tensor_scalar(reached[0:NE, :], iota_b[0:NE, :], cnt[0:NE, 3:4], None, ALU.is_ge))
            dve.sem_inc(blk_step, 1)
            dve.wait_ge(blk_mm, 3)
            ex, pre = banks[4][0:1, 0:BL], banks[5][0:1, 0:BL]
            v.tensor_scalar(blk_e[:, :], ex, float(NE - 1), None, ALU.min)
            link(v.tensor_scalar(blk_row[0:1, 0, :], ex, float(CAP), None, ALU.mult))
            link(v.tensor_tensor(blk_row[0:1, 1, :], iota_b[0:1, :], pre, ALU.subtract))
            link(v.scalar_tensor_tensor(blk_row[0:1, 2, :], blk_row[0:1, 1, :], float(P), blk_row[0:1, 0, :],
                                        ALU.mult, ALU.add))
            link(v.tensor_scalar(blk_s[:, :], blk_row[0:1, 2, :], float(SLOTS), None, ALU.min))
            v.tensor_copy(blk_row[0:1, 3, :], ex)
            link(v.tensor_copy(cnt[0:1, 6:7], banks[2][0:1, 0:1]))
            link(v.tensor_tensor(blk_row[0:1, 1, 2:BL], blk_row[0:1, 3, 2:BL], blk_row[0:1, 3, 0:BL - 2],
                                 ALU.not_equal))
            link(v.tensor_scalar(blk_row[0:1, 0, :], iota_b[0:1, :], cnt[0:1, 6:7], None, ALU.is_lt))
            link(v.tensor_tensor(blk_new[:, 2:BL], blk_row[0:1, 1, 2:BL], blk_row[0:1, 0, 2:BL], ALU.mult))
            link(v.tensor_scalar(cnt[0:1, 4:5], banks[2][0:1, 0:1], 3.0, 1.0, ALU.max, ALU.add))
            link(v.tensor_copy(cnt[0:1, 5:6].bitcast(I32), cnt[0:1, 4:5]))
            link(v.tensor_scalar(blk_n[:, :], cnt[0:1, 5:6].bitcast(I32), 1, None, ALU.arith_shift_right))
            dve.sem_inc(blocks_ready, 1)
            dve.wait_ge(sqrt_done, 4)
            link(v.tensor_scalar(vals_t[:, :, 0:1], vals_t[:, :, 1:2], 1.0, None, ALU.add))
            link(v.reciprocal(vals_t[:, :, 0:1], vals_t[:, :, 0:1]))
            link(v.tensor_tensor(vals_t[:, :, 1:2], vals_t[:, :, 1:2], vals_t[:, :, 0:1], ALU.mult))

            pairs = dve.value_load(blk_n[0:1, 0:1], min_val=2, max_val=(BL - 8) // 2)

            def row_ids(blk, n_before, b):
                dve.wait_ge(bid_full[b], 16 * (n_before + 1))
                spaced_wait(dve, xg_turned, blk - 1)
                v.tensor_scalar(tmp_s[:, 0:1], bids_all[:, ds(blk, 1)], float(N), float(-N), ALU.is_ge, ALU.mult
                                ).then_inc(gid_step, 1)
                spaced_wait(dve, gid_step, 3 * blk + 1)
                v.tensor_tensor(tmp_s[:, 1:2], bids_all[:, ds(blk, 1)], tmp_s[:, 0:1], ALU.add).then_inc(gid_step, 1)
                dve.wait_ge(gid_step, 3 * blk + 2)
                v.tensor_scalar(gid_s[:, b:b + 1], tmp_s[:, 1:2], float(N - 1), None, ALU.min).then_inc(gid_step, 1)

            def copy_xT(blk, b):
                dve.wait_ge(xg_turned, blk + 1)
                wait_count(dve, mm1_done, HC * (blk - 1) if not isinstance(blk, int) or blk > 1 else 0)
                v.tensor_copy(xgT[:, b, :, :], banks[b][:, 0:D].rearrange("p (c n) -> p c n", c=DC)
                              ).then_inc(xgT_ready, 1)

            def copy_b1(blk, b):
                dve.wait_ge(b1_turned, blk + 1)
                wait_count(dve, gelu_done, HC * (blk - 1) if not isinstance(blk, int) or blk > 1 else 0)
                v.tensor_copy(b1T[:, b, :], banks[b][:, D:D + HC]).then_inc(b1T_ready, 1)

            def blocks(j):
                for b in range(2):
                    blk = 2 * j + b
                    row_ids(blk + 3, j + 1 + b, 1 - b)
                    copy_b1(blk + 1, 1 - b)
                    copy_xT(blk + 2, b)
                    spaced_wait(dve, yo_stored[b], 16 * j)
                    v.tensor_copy(bids_s[:, b:b + 1], bids_all[:, ds(blk, 1)])
                    dve.wait_ge(mm2_done, blk + 1)
                    v.tensor_tensor(yo_s[:, b, :], banks[6 + b][:, 0:D], b2_s[:, b, :], ALU.add
                                    ).then_inc(yo_ready, 1)

            row_ids(0, 0, 0)
            row_ids(1, 0, 1)
            copy_xT(0, 0)
            copy_xT(1, 1)
            row_ids(2, 1, 0)
            copy_b1(0, 0)
            blocks(0)
            with dve.Fori(1, pairs) as j:
                blocks(j)

            def add_experts(p, tiles):
                for b, i in enumerate(tiles):
                    dve.wait_ge(y_full[b], 32 * (p + 1))
                    yi = Y[:, ds(i, 1), :].rearrange("p a d -> p (a d)")
                    v.scalar_tensor_tensor(yi, ya_s[:, b, :],
                                           vals_t[:, ds(i, 1), 0:1].rearrange("p a b -> p (a b)"), yi,
                                           ALU.mult, ALU.add).then_inc(ya_added, 1)
                for b, i in enumerate(tiles):
                    yi = Y[:, ds(i, 1), :].rearrange("p a d -> p (a d)")
                    dve.wait_ge(ya_added, i + 1)
                    v.scalar_tensor_tensor(yi, yb_s[:, b, :],
                                           vals_t[:, ds(i, 1), 1:2].rearrange("p a b -> p (a b)"), yi,
                                           ALU.mult, ALU.add).then_inc(yb_added, 1)
            in_sevens(dve, NT, add_experts)

            dve.wait_ge(mean_mm, NT)
            link(v.tensor_scalar(mean_s, banks[0][:, 0:D], 1.0 / N, None, ALU.mult))

            def centre(_, tiles):
                for b, i in enumerate(tiles):
                    v.tensor_tensor(Y[:, ds(i, 1), :], Y[:, ds(i, 1), :], mean_s.unsqueeze(1), ALU.subtract
                                    ).then_inc(centred, 1)
            in_pairs(dve, NT, centre)
            dve.wait_ge(var_mm, NT)
            link(v.tensor_scalar(bn_s[:, 0, :], banks[1][:, 0:D], 1.0 / N, BN_EPS, ALU.mult, ALU.add))
            dve.sem_inc(rsqrt_asked, 1)
            dve.wait_ge(sqrt_done, 5)
            link(v.reciprocal(bn_s[:, 1, :], bn_s[:, 1, :]))
            dve.wait_ge(last_in, 32)
            link(v.tensor_tensor(scale_s, bn_s[:, 1, :], bias2_s[:, :], ALU.mult))
            dve.sem_inc(scale_ready, 1)

            def final_sum(_, tiles):
                for b, i in enumerate(tiles):
                    dve.wait_ge(beta_added, i + 1)
                    dve.wait_ge(scaled, i + 1)
                    v.tensor_tensor(X[:, ds(i, 1), :], X[:, ds(i, 1), :], Y[:, ds(i, 1), :], ALU.add
                                    ).then_inc(summed, 1)
                for b, i in enumerate(tiles):
                    spaced_wait(dve, summed, i + 1)
                    v.bn_stats(stats[:, ds(i, 1), :].rearrange("p a s -> p (a s)"),
                               X[:, ds(i, 1), :].rearrange("p a d -> p (a d)")).then_inc(stats2, 1)
            in_pairs(dve, NT, final_sum)
            dve.wait_ge(stats2, NT)
            row_norm(6)

            def norm_out(p, tiles):
                for b, i in enumerate(tiles):
                    wait_count(dve, out_stored[b], 16 * p)
                    v.tensor_scalar(out_s[:, b, :], X[:, ds(i, 1), :].rearrange("p a d -> p (a d)"),
                                    row_t[:, RSTD, ds(i, 1)], row_t[:, NMR, ds(i, 1)], ALU.mult, ALU.add
                                    ).then_inc(out_ready, 1)
            in_sevens(dve, NT, norm_out)


_INS = ['x', 'src', 'dst', 'L0_gnn_weight', 'L0_gnn_bias', 'L1_gnn_W_gc', 'L1_gnn_b_gc', 'L1_gnn_W_res',
        'L1_gnn_b_res', 'L1_gnn_Wg', 'L1_gnn_bg', 'L1_gnn_w1', 'L1_gnn_b1', 'L1_gnn_w2', 'L1_gnn_b2',
        'L1_gnn_gamma', 'L1_gnn_beta']
_OUTS = [((6250, 256), 'float32')]


def kernel(**inputs):
    import numpy as _np
    import concourse.bacc as _bacc
    from concourse import mybir as _mybir
    from concourse.bass_utils import run_bass_kernel_spmd as _run

    nc = _bacc.Bacc("TRN2", target_bir_lowering=False, num_devices=1)
    arrays, args = {}, []
    for name in _INS:
        a = _np.ascontiguousarray(inputs[name])
        arrays[f"in_{name}_dram"] = a
        args.append(nc.dram_tensor(f"in_{name}_dram", a.shape, _mybir.dt.from_np(a.dtype), kind="ExternalInput").ap())
    for i, (shape, dtype) in enumerate(_OUTS):
        dt = _mybir.dt.from_np(_np.dtype(dtype))
        args.append(nc.dram_tensor(f"out_{i}_dram", shape, dt, kind="ExternalOutput").ap())
    gnn_kernel(nc, *args)
    r = _run(nc, [arrays], core_ids=[0])
    got = tuple(r.results[0][f"out_{i}_dram"] for i in range(len(_OUTS)))
    return got[0]
```

```python
from contextlib import ExitStack

import concourse.bass as bass
from concourse import mybir

F32 = mybir.dt.float32
BF16 = mybir.dt.bfloat16
I32 = mybir.dt.int32
I16 = mybir.dt.int16
U32 = mybir.dt.uint32
ALU = mybir.AluOpType
ACT = mybir.ActivationFunctionType
AX = mybir.AxisListType.X

P = 128
ROW_PAIR = 2 * P
WIN = 64
GROUP = 8
PAIRS = GROUP // 2
BY_POOL = 6
SEVEN = 7
PAD = 8191
LN_EPS = 1e-5
BN_EPS = 1e-5
CAP = 1024
OVER = 1 << 20


def ds(start, size):
    return slice(start, start + size) if isinstance(start, int) else bass.ds(start, size)


def wait_count(eng, sem, count):
    if not isinstance(count, int) or count > 0:
        eng.wait_ge(sem, count)


def in_pairs(eng, tiles, body):
    body(0, [0, 1])
    with eng.Fori(1, tiles // 2) as j:
        body(j, [2 * j, 2 * j + 1])
    if tiles % 2:
        body(tiles // 2, [tiles - 1])


def in_sevens(eng, tiles, body):
    n = tiles // SEVEN
    body(0, list(range(SEVEN)))
    with eng.Fori(1, n - 1) as j:
        body(j, [SEVEN * j + b for b in range(SEVEN)])
    body(n - 1, [SEVEN * (n - 1) + b for b in range(SEVEN)])


def gnn_kernel(nc, x, src, dst, w0, bias0, w_gc, b_gc, w_res, b_res, w_gate, b_gate,
               w1, b1, w2, b2, gamma, beta, out):
    N, D = x.shape
    EDGES = src.shape[0]
    NE, _, H = w1.shape
    DC = D // P
    HC = H // P
    NT = -(-N // P)
    LAST = N - (NT - 1) * P
    NPAIR = -(-EDGES // (2 * GROUP * P)) * 2 * PAIRS
    ET = 2 * NPAIR
    NG = ET // GROUP
    IT = NG // 2
    assert IT == NT and NT % 2 == 1 and NT % SEVEN == 0 and D == 2 * P and NE <= P
    FULL = EDGES // ROW_PAIR
    REST = EDGES - FULL * ROW_PAIR
    NG7 = NT // SEVEN
    CH = -(-NPAIR // P)
    LASTROWS = NPAIR - (CH - 1) * P
    ACCW = NT * P + WIN - 16
    assert ACCW >= N + WIN and ACCW >= NT * P
    ASSIGN = 2 * N
    YROWS = 2 * NT * P
    SLOTS = NE * CAP
    MAXBLK = NE + ASSIGN // P
    BL = -(-(MAXBLK + 8) // 8) * 8

    h_d = nc.dram_tensor("h_scratch", (NT * P, D), F32).ap()
    x2_d = nc.dram_tensor("x2_scratch", (NT * P, D), F32).ap()
    y_d = nc.dram_tensor("y_scratch", (YROWS, D), F32).ap()
    slot_d = nc.dram_tensor("slot_scratch", (SLOTS + P, 1), I32).ap()

    with ExitStack() as ctx:
        def sb(name, shape, dt):
            return ctx.enter_context(nc.sbuf_tensor(name, shape, dt))

        def sem(name):
            return ctx.enter_context(nc.semaphore(name))

        acc = sb("acc", [P, DC, ACCW], F32)
        X = sb("X", [P, NT, D], F32)
        Y = sb("Y", [P, NT, D], F32)
        idx_t = sb("idx_t", [P, ET], I32)
        rel_t = sb("rel_t", [P, ET], BF16)
        far_t = sb("far_t", [P, ET], I16)
        lohi_t = sb("lohi_t", [P, 4, ET], BF16)
        win_row = sb("win_row", [1, NPAIR], I32)
        gath = sb("gath", [P, 2, GROUP, D], F32)
        onehot = sb("onehot", [P, 2, GROUP, WIN], F32)
        oh_lo = sb("oh_lo", [P, 2, 2, 4, P], BF16)
        oh_hi = sb("oh_hi", [P, 2, 2, 4, NT], BF16)
        idx_s = sb("idx_s", [P, 2, GROUP], I32)
        xs = sb("xs", [P, D], F32)
        xT = sb("xT", [P, DC, P], F32)
        w0_s = sb("w0_s", [P, 2 * DC, D], F32)
        wgc_s = sb("wgc_s", [P, DC, D], F32)
        wres_s = sb("wres_s", [P, DC, D], F32)
        wg_s = sb("wg_s", [P, DC, NE], F32)
        ident = sb("ident", [P, P], F32)
        iota_w = sb("iota_w", [P, WIN], F32)
        iota_lo = sb("iota_lo", [P, P], BF16)
        iota_hi = sb("iota_hi", [P, NT], BF16)
        bias_s = sb("bias_s", [P, D], F32)
        bias2_s = sb("bias2_s", [P, D], F32)
        zero_s = sb("zero_s", [P, D], F32)
        bg_s = sb("bg_s", [P, NE], F32)
        rdeg = sb("rdeg", [P, 6, NT], F32)
        DEG_IN, DEG_OUT, R_IN, RS_IN, RS_OUT, TMP = range(6)
        flag_s = sb("flag_s", [1, 1], I32)
        small = sb("small", [P, 8], F32)
        ones_f = sb("ones_f", [P, P], F32)
        ids_t = sb("ids_t", [P, NT, 2], I32)
        vals_t = sb("vals_t", [P, NT, 2], F32)
        blk_e = sb("blk_e", [1, BL], I32)
        blk_s = sb("blk_s", [1, BL], I32)
        blk_new = sb("blk_new", [1, BL], I32)
        blk_n = sb("blk_n", [1, 1], I32)

        banks = [ctx.enter_context(nc.psum_tensor(f"bank{i}", [P, 512], F32)) for i in range(8)]
        WINB = banks[0:2]
        HISTB = banks[2:4]
        TB, MB = banks[4], banks[5]

        yflat = Y[:, :, :].rearrange("p t d -> p (t d)")
        cols = CH * ROW_PAIR

        def tab(k):
            return yflat[:, k * cols:(k + 1) * cols]

        srcI, dstI = tab(0).bitcast(I32), tab(1).bitcast(I32)
        srcF, dstF, idxF, relF, farF, tmpF = tab(2), tab(3), tab(4), tab(5), tab(6), tab(7)
        loS, hiS, loD, hiD = tab(8), tab(9), tab(10), tab(11)
        assert 12 * cols <= NT * D
        tables = [idxF, relF, farF, loS, hiS, loD, hiD]
        table_out = [idx_t[:, :], rel_t[:, :], far_t[:, :]] + [lohi_t[:, k, :] for k in range(4)]
        wmin = small[:, 0:CH]

        gflat = gath[:, :, :, :].rearrange("p a k d -> p (a k d)")
        aflat = acc[:, :, :].rearrange("p c n -> p (c n)")
        at = [0]

        def carve(flat, n, pattern=None, dt=F32, **dims):
            a = flat[:, at[0]:at[0] + n]
            at[0] += n
            if dt is not F32:
                a = a.bitcast(dt)
            return a.rearrange(pattern, **dims) if pattern else a

        sums_s = carve(gflat, 2 * D, "p (b c n) -> p b c n", b=2, c=DC)
        x2_s = carve(gflat, 2 * D, "p (b d) -> p b d", b=2)
        junk = carve(gflat, 2 * D, "p (b d) -> p b d", b=2)
        stats = carve(gflat, 6 * NT, "p (t s) -> p t s", s=6)
        row_t = carve(gflat, 7 * NT, "p (k t) -> p k t", k=7)
        SS, RN, SUM, DIFF, VAR, RSTD, NMR = range(7)
        assert at[0] <= 2 * GROUP * D
        x2T = junk.rearrange("p b (c n) -> p b c n", c=DC)
        at[0] = 4 * D + 2 * D
        G = SEVEN
        logit = carve(gflat, G * NE, "p (t e) -> p t e", t=G)
        top8 = carve(gflat, 8 * G, "p (t e) -> p t e", t=G)
        top8i = carve(gflat, 8 * G, "p (t e) -> p t e", t=G, dt=U32)
        top2f = carve(gflat, 2 * G)
        both = carve(gflat, G * NE // 2, "p (t e) -> p t e", t=G, dt=BF16)
        before = carve(gflat, NE // 2, dt=BF16)
        both_sum = carve(gflat, NE)
        rank = carve(gflat, 2 * G)
        slotf = carve(gflat, 2 * G)
        overf = carve(gflat, 2 * G)
        slot_s = carve(gflat, 4 * G, "p (b t k) -> p b t k", b=2, t=G, dt=I32)
        ids_s = carve(gflat, 4 * G, "p (b t k) -> p b t k", b=2, t=G, dt=I32)
        pick = oh_lo[:, :, :, :, :].rearrange("p a s t n -> p (a s t n)").bitcast(F32)[:, 0:2 * G * NE] \
            .rearrange("p (t k e) -> p t k e", t=G, k=2)
        prod = onehot[:, :, :, :].rearrange("p a k w -> p (a k w)")[:, 0:2 * G * NE] \
            .rearrange("p (t k e) -> p t k e", t=G, k=2)
        iota_e = carve(gflat, NE)
        upper = carve(gflat, P // 2, dt=BF16)
        upto = carve(gflat, NE)
        iota_b = carve(gflat, BL)
        cnt = carve(gflat, 8)
        reached = carve(gflat, BL)
        blk_row = carve(gflat, 4 * BL, "p (k b) -> p k b", k=4)
        ones_b = carve(gflat, P // 2, dt=BF16)
        assert at[0] <= 2 * GROUP * D
        at[0] = 0
        w1_s = carve(aflat, 2 * DC * H, "p (b c h) -> p b c h", b=2, c=DC)
        w2_s = carve(aflat, 2 * HC * D, "p (b c d) -> p b c d", b=2, c=HC)
        b2_s = carve(aflat, 2 * D, "p (b d) -> p b d", b=2)
        xg_s = carve(aflat, 2 * D, "p (b d) -> p b d", b=2)
        xgT = carve(aflat, 2 * D, "p (b c n) -> p b c n", b=2, c=DC)
        hT = carve(aflat, 2 * H, "p (b c n) -> p b c n", b=2, c=HC)
        yo_s = carve(aflat, 2 * D, "p (b d) -> p b d", b=2)
        b1r_s = carve(aflat, 2 * P, "p (b n) -> p b n", b=2)
        b1T = carve(aflat, 2 * HC, "p (b c) -> p b c", b=2)
        bids_all = carve(aflat, BL, dt=I32)
        bids_s = carve(aflat, 2, dt=I32)
        gid_s = carve(aflat, 2, dt=I32)
        tmp_s = carve(aflat, 4)
        ya_s = carve(aflat, SEVEN * D, "p (b d) -> p b d", b=SEVEN)
        yb_s = carve(aflat, SEVEN * D, "p (b d) -> p b d", b=SEVEN)
        sq_s = ya_s
        mean_s = carve(aflat, D)
        scale_s = carve(aflat, D)
        bn_s = carve(aflat, 2 * D, "p (b d) -> p b d", b=2)
        assert at[0] <= DC * ACCW

        fill = gath[:, 1, :, :].rearrange("p k d -> p (k d)")[:, 0:(SLOTS + P) // P].bitcast(I32)

        FARW = 448
        NFAR = NT * P // FARW
        assert NFAR * FARW == NT * P and FARW <= 512 and FARW <= GROUP * WIN
        at[0] = GROUP * D
        iota_far = carve(gflat, FARW)
        far_dst = carve(gflat, 1)
        far_idx = carve(gflat, 1, dt=I32)
        far_rows = gath[:, 0, 0, :]
        far_onehot = onehot[:, 0, :, :].rearrange("p k w -> p (k w)")[:, 0:FARW]

        edges_in = sem("edges_in")
        pads_set = sem("pads_set")
        const_set = sem("const_set")
        weights_in = sem("weights_in")
        dve_step = sem("dve_step")
        tabs_made = sem("tabs_made")
        tabs_turned = sem("tabs_turned")
        tabs_done = sem("tabs_done")
        wmin_turned = sem("wmin_turned")
        win_set = sem("win_set")
        spacer = sem("spacer")
        groups_done = sem("groups_done")
        idx_ready = sem("idx_ready")
        onehot_ready = sem("onehot_ready")
        hist_ready = sem("hist_ready")
        hist_done = sem("hist_done")
        acc_step = sem("acc_step")
        gath_full = [sem(f"gath_full{k}") for k in range(2 * GROUP)]
        x_in = sem("x_in")
        x_turned = sem("x_turned")
        xT_ready = sem("xT_ready")
        prep_mm = sem("prep_mm")
        prep_done = sem("prep_done")
        xs_ready = sem("xs_ready")
        bias1_in = sem("bias1_in")
        sqrt_done = sem("sqrt_done")
        norms_done = sem("norms_done")
        norms_ready = sem("norms_ready")
        sums_final = sem("sums_final")
        far_const = sem("far_const")
        far_taken = [sem(f"far_taken{k}") for k in range(2)]
        far_gath = [sem(f"far_gath{k}") for k in range(2)]
        far_ready = [sem(f"far_ready{k}") for k in range(2)]
        far_mm = [sem(f"far_mm{k}") for k in range(2)]
        far_step = [sem(f"far_step{k}") for k in range(2)]
        fill_set = sem("fill_set")
        slots_cleared = sem("slots_cleared")
        y_cleared = sem("y_cleared")
        deg_ready = sem("deg_ready")
        sums_staged = [sem(f"sums_staged{b}") for b in range(2)]
        sums_mm = sem("sums_mm")
        sums_used = sem("sums_used")
        squares = sem("squares")
        raw_ready = sem("raw_ready")
        stats_done = sem("stats_done")
        x1_ready = sem("x1_ready")
        h_ready = sem("h_ready")
        h_stored = [sem(f"h_stored{k}") for k in range(4)]
        rsqrt_asked = sem("rsqrt_asked")
        x2_ready = sem("x2_ready")
        x2_kept = sem("x2_kept")
        x2_stored = sem("x2_stored")
        x2_turned = sem("x2_turned")
        x2T_ready = sem("x2T_ready")
        logit_mm = sem("logit_mm")
        both_ready = sem("both_ready")
        rank_mm = sem("rank_mm")
        slots_ready = sem("slots_ready")
        route_step = sem("route_step")
        slots_stored = [sem(f"slots_stored{b}") for b in range(2)]
        route_const = sem("route_const")
        blk_mm = sem("blk_mm")
        blk_step = sem("blk_step")
        blocks_ready = sem("blocks_ready")
        bid_full = [sem(f"bid_full{b}") for b in range(2)]
        w1_full = [sem(f"w1_full{b}") for b in range(2)]
        w2_full = [sem(f"w2_full{b}") for b in range(2)]
        gid_step = sem("gid_step")
        xg_full = [sem(f"xg_full{b}") for b in range(2)]
        xg_turned = sem("xg_turned")
        xgT_ready = sem("xgT_ready")
        b1_turned = sem("b1_turned")
        b1T_ready = sem("b1T_ready")
        mm1_done = sem("mm1_done")
        gelu_done = sem("gelu_done")
        mm2_done = sem("mm2_done")
        yo_ready = sem("yo_ready")
        yo_stored = [sem(f"yo_stored{b}") for b in range(2)]
        y_full = [sem(f"y_full{k}") for k in range(4)]
        ya_added = sem("ya_added")
        yb_added = sem("yb_added")
        mean_mm = sem("mean_mm")
        centred = sem("centred")
        sq_ready = sem("sq_ready")
        var_mm = sem("var_mm")
        last_in = sem("last_in")
        beta_added = sem("beta_added")
        scale_ready = sem("scale_ready")
        scaled = sem("scaled")
        own_scaled = sem("own_scaled")
        summed = sem("summed")
        stats2 = sem("stats2")
        out_ready = sem("out_ready")
        out_stored = [sem(f"out_stored{k}") for k in range(4)]

        def spaced_wait(eng, s, count):
            if isinstance(count, int):
                wait_count(eng, s, count)
            else:
                eng.wait_ge(s, count)
                eng.sem_inc(spacer, 1)

        def parts(tiles):
            if isinstance(tiles[-1], int) and tiles[-1] == NT - 1:
                return [(0, 2, P, 0), (2, 2, P, 1), (4, 2, P, 2), (6, 1, LAST, 3)]
            return [(0, 2, P, 0), (2, 2, P, 1), (4, 3, P, 2)]

        def tile_rows(d, first, n, rows):
            return d[ds(first, n * rows), :].rearrange("(t p) d -> p t d", p=rows)

        def bcast(vec, n=P):
            return vec.rearrange("(a n) -> a n", a=1).to_broadcast([n, vec.shape[0]])

        def load_w2(eng, e, b, cond=None):
            eng.dma_start(w2_s[:, b, :, :], w2[ds(e, 1), :, :].rearrange(
                "a (c p) d -> p (a c) d", p=P), cond=cond).then_inc(w2_full[b], 16)
            eng.dma_start(b2_s[:, b, :], b2[ds(e, 1), :].to_broadcast([P, D]), cond=cond
                         ).then_inc(w2_full[b], 16)

        def weights_of(eng, blk):
            e = eng.value_load(blk_e[0:1, ds(blk, 1)], min_val=0, max_val=NE - 1)
            return e, eng.value_load(blk_new[0:1, ds(blk, 1)], min_val=0, max_val=1) > 0

        block = ctx.enter_context(nc.Block())

        @block.sync
        def _(sp):
            for vec, t in ((src, srcI), (dst, dstI)):
                tv = t.rearrange("p (c e) -> p c e", c=CH)
                sp.dma_start(tv[:, 0:CH - 1, :], vec[0:(CH - 1) * P * ROW_PAIR].rearrange(
                    "(c p e) -> p c e", p=P, e=ROW_PAIR)).then_inc(edges_in, 16)
            sp.wait_ge(pads_set, 2)
            n_full = FULL - (CH - 1) * P
            for vec, t in ((src, srcI), (dst, dstI)):
                tv = t.rearrange("p (c e) -> p c e", c=CH)
                sp.dma_start(tv[0:n_full, CH - 1, :], vec[(CH - 1) * P * ROW_PAIR:FULL * ROW_PAIR]
                             .rearrange("(p e) -> p e", e=ROW_PAIR)).then_inc(edges_in, 16)
                sp.dma_start(tv[n_full:n_full + 1, CH - 1, 0:REST],
                             vec[FULL * ROW_PAIR:EDGES].rearrange("(p e) -> p e", p=1)
                             ).then_inc(edges_in, 16)
            sp.dma_start(w0_s[:, :, :], w0.rearrange("(c p) n -> p c n", p=P)).then_inc(weights_in, 16)
            sp.dma_start(bias_s[:, :], bcast(bias0)).then_inc(weights_in, 16)
            sp.dma_start(wgc_s[:, :, :], w_gc.rearrange("(c p) n -> p c n", p=P)).then_inc(weights_in, 16)
            sp.dma_start(wres_s[:, :, :], w_res.rearrange("(c p) n -> p c n", p=P)).then_inc(weights_in, 16)
            sp.dma_start(wg_s[:, :, :], w_gate.rearrange("(c p) n -> p c n", p=P)).then_inc(weights_in, 16)
            sp.dma_start(bias2_s[:, :], bcast(b_res)).then_inc(weights_in, 16)
            sp.dma_start(bg_s[:, :], bcast(b_gate)).then_inc(weights_in, 16)

            sp.wait_ge(fill_set, 2)
            sp.dma_start(slot_d.rearrange("(p s) a -> p (s a)", p=P), fill).then_inc(slots_cleared, 16)

            def load_x(i, rows=P):
                wait_count(sp, x_in, 16 * i)
                sp.dma_start(X[0:rows, ds(i, 1), :].rearrange("p a d -> p (a d)"), x[ds(P * i, rows), :]
                             ).then_inc(x_in, 16)

            load_x(0)
            with sp.Fori(1, NT - 1) as i:
                load_x(i)
            load_x(NT - 1, LAST)

            sp.wait_ge(prep_done, NT)
            sp.dma_start(bias_s[:, :], bcast(b_gc)).then_inc(bias1_in, 16)

            def store_h(_, tiles):
                for first, n, _, k in parts(tiles):
                    sp.wait_ge(h_ready, tiles[first] + n)
                    sp.dma_start(tile_rows(h_d, P * tiles[first], n, P), Y[:, ds(tiles[first], n), :]
                                 ).then_inc(h_stored[k], 16)
            in_sevens(sp, NT, store_h)

            def store_x2(_, tiles):
                for b, i in enumerate(tiles):
                    sp.wait_ge(x2_kept, i + 1)
                    sp.dma_start(x2_d[ds(P * i, P), :], Y[:, ds(i, 1), :].rearrange("p a d -> p (a d)")
                                 ).then_inc(x2_stored, 16)
            in_pairs(sp, NT, store_x2)

            sp.wait_ge(blocks_ready, 1)
            pairs = sp.value_load(blk_n[0:1, 0:1], min_val=2, max_val=(BL - 8) // 2)
            for b in range(2):
                sp.wait_ge(slots_stored[b], 32 * G * ((NG7 + 1 - b) // 2))

            def load_ids(blk, b):
                first = sp.value_load(blk_s[0:1, ds(blk, 1)], min_val=0, max_val=SLOTS)
                sp.dma_start(bids_all[:, ds(blk, 1)], slot_d[ds(first, P), :]).then_inc(bid_full[b], 16)

            def load_w1(e, b, cond=None):
                sp.dma_start(w1_s[:, b, :, :], w1[ds(e, 1), :, :].rearrange(
                    "a (c p) h -> p (a c) h", p=P), cond=cond).then_inc(w1_full[b], 16)
                sp.dma_start(b1r_s[0:HC, b, :], b1[ds(e, 1), :].rearrange(
                    "a (c p) -> (a c) p", p=P), cond=cond).then_inc(w1_full[b], 16)

            load_ids(0, 0)
            load_ids(1, 1)
            for b in range(2):
                e = sp.value_load(blk_e[0:1, b:b + 1], min_val=0, max_val=NE - 1)
                load_w1(e, b)
                load_w2(sp, e, b)
            sp.wait_ge(y_cleared, 16 * NT)
            sp.dma_start(bias2_s[:, :], bcast(gamma)).then_inc(last_in, 16)
            sp.dma_start(zero_s[:, :], bcast(beta)).then_inc(last_in, 16)

            for blk in (2, 3):
                sp.wait_ge(gid_step, 3 * (blk - 1))
                load_ids(blk, blk % 2)
            e, fresh = weights_of(sp, 2)
            sp.wait_ge(mm1_done, HC)
            load_w1(e, 0, fresh)

            with sp.Fori(0, pairs) as j:
                for b in range(2):
                    blk = 2 * j + b
                    spaced_wait(sp, gid_step, 3 * (blk + 3))
                    load_ids(blk + 4, b)
                    e, fresh = weights_of(sp, blk + 3)
                    spaced_wait(sp, mm1_done, HC * (blk + 2))
                    load_w1(e, 1 - b, fresh)
            for b in range(2):
                spaced_wait(sp, yo_stored[b], 16 * pairs)
                spaced_wait(sp, bid_full[b], 16 * (pairs + 2))
                spaced_wait(sp, w1_full[b], 32 * (pairs + 2 - b))
                spaced_wait(sp, w2_full[b], 32 * (pairs + 1))

            def load_y(_, tiles):
                for first, n, rows, k in parts(tiles):
                    i = tiles[first]
                    wait_count(sp, yb_added, i + n - SEVEN)
                    for y_s, row in ((ya_s, P * i), (yb_s, N + P * i)):
                        sp.dma_start(y_s[0:rows, first:first + n, :], tile_rows(y_d, row, n, rows)
                                     ).then_inc(y_full[k], 16)
            in_sevens(sp, NT, load_y)

            def store_out(_, tiles):
                for first, n, rows, k in parts(tiles):
                    sp.wait_ge(out_ready, tiles[first] + n)
                    sp.dma_start(tile_rows(out, P * tiles[first], n, rows), X[0:rows, ds(tiles[first], n), :]
                                 ).then_inc(out_stored[k], 16)
            in_sevens(sp, NT, store_out)
            for k in range(4):
                sp.wait_ge(out_stored[k], 16 * (NG7 if k < 3 else 1))

        @block.gpsimd
        def _(pool):
            pool.memset(X[:, NT - 1, :], 1.0).then_inc(pads_set, 1)
            for t in (srcI, dstI):
                pad = pool.memset(t.rearrange("p (c e) -> p c e", c=CH)[:, CH - 1, :], PAD)
            pad.then_inc(pads_set, 1)
            pool.memset(ident[:, :], 0.0).then_inc(const_set, 1)
            pool.memset(ones_f[:, :], 1.0).then_inc(const_set, 1)
            pool.iota(iota_w[:, :], pattern=[[1, WIN]], base=0, channel_multiplier=0,
                      allow_small_or_imprecise_dtypes=True).then_inc(const_set, 1)
            pool.iota(iota_lo[:, :], pattern=[[1, P]], base=0, channel_multiplier=0,
                      allow_small_or_imprecise_dtypes=True).then_inc(const_set, 1)
            pool.iota(iota_hi[:, :], pattern=[[P, NT]], base=0, channel_multiplier=0,
                      allow_small_or_imprecise_dtypes=True).then_inc(const_set, 1)
            pool.wait_ge(const_set, 1)
            pool.affine_select(out=ident[:, :], in_=ident[:, :], compare_op=ALU.not_equal, fill=1.0,
                               base=0, pattern=[[-1, P]], channel_multiplier=1).then_inc(const_set, 1)

            pool.memset(fill, ASSIGN).then_inc(fill_set, 1)
            pool.memset(zero_s[:, :], 0.0).then_inc(fill_set, 1)
            pool.iota(ids_t[:, :, :], pattern=[[P, NT], [N, 2]], base=0, channel_multiplier=1
                      ).then_inc(const_set, 1)
            pool.memset(acc[:, :, :], 0.0).then_inc(acc_step, 1)
            pool.wait_ge(slots_cleared, 16)

            def gather(table, g, half):
                spaced_wait(pool, idx_ready, g + 1)
                for k in range(GROUP):
                    pool.indirect_dma_start(
                        out=gath[:, half, k, :], out_offset=None, in_=table,
                        in_offset=bass.IndirectOffsetOnAxis(ap=idx_s[:, half, k:k + 1], axis=0),
                    ).then_inc(gath_full[half * GROUP + k], 16)

            def layer(L, table):
                def step(i):
                    for half in range(2):
                        gather(table, NG * L + 2 * i + half, half)
                step(0)
                with pool.Fori(1, IT) as i:
                    step(i)

            def far_gathers(L, table):
                pool.wait_ge(acc_step, PAIRS * NG * (L + 1) + 1 + L)
                beyond = pool.value_load(flag_s[0:1, 0:1], min_val=0, max_val=ET * P)
                with pool.If(beyond > 0):
                    pool.iota(iota_far, pattern=[[1, FARW]], base=0, channel_multiplier=0,
                              allow_small_or_imprecise_dtypes=True).then_inc(far_const, 1)
                    with pool.Fori(0, ET) as t:
                        spaced_wait(pool, far_taken[L], t + 1)
                        pool.indirect_dma_start(
                            out=far_rows, out_offset=None, in_=table,
                            in_offset=bass.IndirectOffsetOnAxis(ap=far_idx, axis=0)).then_inc(far_gath[L], 16)

            layer(0, x[:, :])
            far_gathers(0, x[:, :])

            def stage(_, tiles):
                if len(tiles) == 2:
                    spaced_wait(pool, sums_mm, tiles[1] - 1)
                    pool.tensor_copy(sums_s[:, 1, :, :], acc[:, :, ds(P * tiles[1], P)]).then_inc(sums_staged[1], 1)
            pool.wait_ge(sums_final, 1)
            in_pairs(pool, NT, stage)
            for b in range(2):
                pool.wait_ge(sums_staged[b], (NT + 1 - b) // 2)
            pool.memset(acc[:, :, :], 0.0).then_inc(acc_step, 1)

            for k in range(4):
                pool.wait_ge(h_stored[k], 16 * (NG7 if k < 3 else 1))
            layer(1, h_d)
            far_gathers(1, h_d)

            pool.wait_ge(sums_final, 2)
            pool.iota(iota_e, pattern=[[1, NE]], base=0, channel_multiplier=0,
                      allow_small_or_imprecise_dtypes=True).then_inc(route_const, 1)
            pool.iota(iota_b, pattern=[[1, BL]], base=0, channel_multiplier=0,
                      allow_small_or_imprecise_dtypes=True).then_inc(route_const, 1)
            pool.memset(before, 0.0).then_inc(route_const, 1)
            pool.memset(both, 0.0).then_inc(route_const, 1)
            pool.memset(upper, 1.0).then_inc(route_const, 1)
            pool.memset(ones_b, 1.0).then_inc(route_const, 1)
            pool.memset(upto, 1.0).then_inc(route_const, 1)
            pool.wait_ge(route_const, 7)
            pool.affine_select(out=upper, in_=upper, compare_op=ALU.is_gt, fill=0.0, base=0,
                               pattern=[[1, P]], channel_multiplier=-1).then_inc(route_const, 1)
            pool.affine_select(out=upto, in_=upto, compare_op=ALU.is_ge, fill=0.0, base=0,
                               pattern=[[1, NE]], channel_multiplier=-1).then_inc(route_const, 1)

            def store_slots(_, groups):
                for b, g in enumerate(groups):
                    spaced_wait(pool, slots_ready, g + 1)
                    for t in range(G):
                        rows = LAST if isinstance(g, int) and G * g + t == NT - 1 else P
                        for k in range(2):
                            pool.indirect_dma_start(
                                out=slot_d, in_=ids_s[0:rows, b, t, k:k + 1], in_offset=None,
                                out_offset=bass.IndirectOffsetOnAxis(ap=slot_s[0:rows, b, t, k:k + 1], axis=0),
                                bounds_check=SLOTS - 1, oob_is_err=False).then_inc(slots_stored[b], 16)
            in_pairs(pool, NG7, store_slots)

            pool.wait_ge(blocks_ready, 1)
            pool.wait_ge(x2_stored, 16 * NT)
            pairs = pool.value_load(blk_n[0:1, 0:1], min_val=2, max_val=(BL - 8) // 2)
            pool.wait_ge(y_cleared, 16 * NT)

            def gather_rows(blk, b):
                spaced_wait(pool, gid_step, 3 * (blk + 1))
                pool.indirect_dma_start(
                    out=xg_s[:, b, :], out_offset=None, in_=x2_d,
                    in_offset=bass.IndirectOffsetOnAxis(ap=gid_s[:, b:b + 1], axis=0)).then_inc(xg_full[b], 16)

            for b in range(2):
                gather_rows(b, b)
            pool.wait_ge(xg_turned, 1)
            gather_rows(2, 0)

            def blocks(j):
                for b in range(2):
                    blk = 2 * j + b
                    spaced_wait(pool, xg_turned, blk + 2)
                    gather_rows(blk + 3, 1 - b)
                    spaced_wait(pool, yo_ready, blk + 1)
                    pool.indirect_dma_start(
                        out=y_d, in_=yo_s[:, b, :], in_offset=None,
                        out_offset=bass.IndirectOffsetOnAxis(ap=bids_s[:, b:b + 1], axis=0),
                        bounds_check=ASSIGN - 1, oob_is_err=False).then_inc(yo_stored[b], 16)
            with pool.Fori(0, pairs) as j:
                blocks(j)

            pool.wait_ge(last_in, 32)

            def add_beta(_, tiles):
                for b, i in enumerate(tiles):
                    pool.tensor_tensor(X[:, ds(i, 1), :], X[:, ds(i, 1), :], zero_s[:, :].unsqueeze(1), ALU.add
                                       ).then_inc(beta_added, 1)
            in_pairs(pool, NT, add_beta)
            pool.wait_ge(scale_ready, 1)

            def scale_y(_, tiles):
                for i in tiles[:BY_POOL]:
                    pool.tensor_tensor(Y[:, ds(i, 1), :], Y[:, ds(i, 1), :], scale_s.unsqueeze(1), ALU.mult
                                       ).then_inc(scaled, 1)
            in_sevens(pool, NT, scale_y)

        @block.scalar
        def _(act):
            def stage_idx(L, i, half):
                g = NG * L + 2 * i + half
                spaced_wait(act, groups_done, g - 1)
                act.activation(idx_s[:, half, :], idx_t[:, ds(2 * GROUP * i + GROUP * half, GROUP)],
                               ACT.Copy).then_inc(idx_ready, 1)

            n = 0
            for k, o in enumerate(table_out):
                for c in range(CH):
                    m = P if c < CH - 1 else LASTROWS
                    act.wait_ge(tabs_turned, n + 1)
                    act.activation(o[:, c * ROW_PAIR:c * ROW_PAIR + 2 * m].rearrange("p (q h) -> p q h", h=2),
                                   banks[4 + n % 4][:, 0:2 * P].rearrange("p (h q) -> p q h", h=2)[:, 0:m, :],
                                   ACT.Copy).then_inc(tabs_done, 1)
                    n += 1
                if k == 0:
                    act.wait_ge(tabs_done, n)
                    stage_idx(0, 0, 0)
                    stage_idx(0, 0, 1)

            def copy_xs(L, i):
                spaced_wait(act, x_turned, NT * L + i)
                act.activation(xs[:, :], X[:, ds(i, 1), :].rearrange("p a d -> p (a d)"), ACT.Copy
                               ).then_inc(xs_ready, 1)

            act.wait_ge(tabs_done, n)

            def step0(i):
                first = isinstance(i, int) and i == 0
                if not first:
                    stage_idx(0, i, 0)
                act.wait_ge(x_in, 16 * (i + 1))
                copy_xs(0, i)
                if not first:
                    stage_idx(0, i, 1)
                act.dma_start(y_d[ds(2 * P * i, 2 * P), :].rearrange("(p r) d -> p r d", p=P),
                              zero_s[:, :].unsqueeze(1).to_broadcast([P, 2, D])).then_inc(y_cleared, 16)
                act.wait_ge(x_turned, i + 1)
                act.activation(xT[:, :, :], TB[:, 0:D].rearrange("p (c n) -> p c n", c=DC),
                               ACT.Copy).then_inc(xT_ready, 1)
            act.wait_ge(fill_set, 2)
            step0(0)
            with act.Fori(1, IT) as i:
                step0(i)

            act.wait_ge(deg_ready, 1)
            act.activation(rdeg[:, RS_IN, :], rdeg[:, R_IN, :], ACT.Sqrt)
            act.activation(rdeg[:, RS_OUT, :], rdeg[:, TMP, :], ACT.Sqrt).then_inc(sqrt_done, 1)
            act.wait_ge(sums_final, 1)

            def stage_first(i):
                spaced_wait(act, sums_mm, i - 1)
                act.activation(sums_s[:, 0, :, :], acc[:, :, ds(P * i, P)], ACT.Copy
                               ).then_inc(sums_staged[0], 1)

            def square(_, tiles):
                if len(tiles) == 2:
                    stage_first(tiles[0] + 2)
                for b, i in enumerate(tiles):
                    spaced_wait(act, squares, i - 1)
                    spaced_wait(act, sums_used, i + 1)
                    act.activation(junk[:, b, :], Y[:, ds(i, 1), :].rearrange("p a d -> p (a d)"), ACT.Square,
                                   accum_out=row_t[:, SS, ds(i, 1)]).then_inc(squares, 1)

            def squares_and_norms(s, groups):
                n = G * len(groups)
                for q in range(0, n, 2):
                    square(q, [2 * G * s + t for t in (q, q + 1) if t < n])
                spaced_wait(act, squares, 2 * G * s + n)
                act.activation(row_t[:, RN, ds(2 * G * s, n)], row_t[:, SS, ds(2 * G * s, n)], ACT.Sqrt
                               ).then_inc(norms_done, 1)
            stage_first(0)
            in_pairs(act, NG7, squares_and_norms)
            act.wait_ge(rsqrt_asked, 1)
            act.activation(row_t[:, RSTD, :], row_t[:, VAR, :], ACT.Sqrt).then_inc(sqrt_done, 1)

            def scale_h(group, tiles):
                for b, i in enumerate(tiles):
                    spaced_wait(act, x1_ready, i + 1)
                    act.activation(Y[:, ds(i, 1), :].rearrange("p a d -> p (a d)"),
                                   X[:, ds(i, 1), :].rearrange("p a d -> p (a d)"), ACT.Copy,
                                   scale=rdeg[:, RS_OUT, ds(i, 1)]).then_inc(h_ready, 1)
            in_sevens(act, NT, scale_h)

            def step1(i):
                stage_idx(1, i, 0)
                copy_xs(1, i)
                stage_idx(1, i, 1)
                act.wait_ge(x_turned, NT + i + 1)
                act.activation(xT[:, :, :], TB[:, 0:D].rearrange("p (c n) -> p c n", c=DC),
                               ACT.Copy).then_inc(xT_ready, 1)
            step1(0)
            with act.Fori(1, IT) as i:
                step1(i)

            def stage_sums(tiles):
                for b, i in enumerate(tiles):
                    spaced_wait(act, sums_mm, NT + i - 1)
                    act.activation(sums_s[:, b, :, :], acc[:, :, ds(P * i, P)], ACT.Copy
                                   ).then_inc(sums_staged[b], 1)

            def keep_x2(tiles):
                for b, i in enumerate(tiles):
                    act.wait_ge(x2_turned, i + 1)
                    act.activation(x2T[:, b, :, :], banks[2 + b][:, 0:D].rearrange("p (c n) -> p c n", c=DC),
                                   ACT.Copy).then_inc(x2T_ready, 1)
                for b, i in enumerate(tiles):
                    spaced_wait(act, x2_ready, i + 1)
                    act.activation(Y[:, ds(i, 1), :].rearrange("p a d -> p (a d)"), x2_s[:, b, :], ACT.Copy
                                   ).then_inc(x2_kept, 1)
                ahead = [i + 4 for i in tiles]
                stage_sums([i for i in ahead if not isinstance(i, int) or i < NT])
            act.wait_ge(sums_final, 2)
            stage_sums([0, 1])
            stage_sums([2, 3])
            keep_x2([0, 1])
            with act.Fori(1, NT // 2 - 2) as j:
                keep_x2([2 * j, 2 * j + 1])
            for j in (NT // 2 - 2, NT // 2 - 1):
                keep_x2([2 * j, 2 * j + 1])
            keep_x2([NT - 1])
            act.wait_ge(rsqrt_asked, 2)
            act.activation(vals_t[:, :, 1:2], vals_t[:, :, 1:2], ACT.Exp).then_inc(sqrt_done, 1)

            act.wait_ge(blocks_ready, 1)
            pairs = act.value_load(blk_n[0:1, 0:1], min_val=2, max_val=(BL - 8) // 2)

            def gelus(blk, b):
                act.wait_ge(b1T_ready, blk + 1)
                wait_count(act, mm2_done, blk - 1)
                for c in range(HC):
                    act.wait_ge(mm1_done, HC * blk + c + 1)
                    act.activation(hT[:, b, c, :], banks[2 + c][:, 0:P], ACT.Gelu,
                                   bias=b1T[:, b, c:c + 1]).then_inc(gelu_done, 1)
            gelus(0, 0)
            def hidden(j):
                for b in range(2):
                    blk = 2 * j + b
                    gelus(blk + 1, 1 - b)
                    e, fresh = weights_of(act, blk + 2)
                    spaced_wait(act, yo_ready, blk + 1)
                    load_w2(act, e, b, fresh)
            hidden(0)
            with act.Fori(1, pairs) as j:
                hidden(j)

            def square_y(_, tiles):
                for b, i in enumerate(tiles):
                    spaced_wait(act, var_mm, i + 1 - SEVEN)
                    spaced_wait(act, centred, i + 1)
                    act.activation(sq_s[:, b, :], Y[:, ds(i, 1), :].rearrange("p a d -> p (a d)"), ACT.Square
                                   ).then_inc(sq_ready, 1)
            in_sevens(act, NT, square_y)
            act.wait_ge(rsqrt_asked, 3)
            act.activation(bn_s[:, 1, :], bn_s[:, 0, :], ACT.Sqrt).then_inc(sqrt_done, 1)
            act.wait_ge(rsqrt_asked, 4)
            act.activation(row_t[:, RSTD, :], row_t[:, VAR, :], ACT.Sqrt).then_inc(sqrt_done, 1)

        @block.tensor
        def _(pe):
            pe.wait_ge(const_set, 6)
            n = 0
            for k, t in enumerate(tables):
                for c in range(CH):
                    m = P if c < CH - 1 else LASTROWS
                    pe.wait_ge(tabs_made, k + 1)
                    if n >= 4:
                        pe.wait_ge(tabs_done, n - 3)
                    for h in range(2):
                        last = pe.transpose(banks[4 + n % 4][:, h * P:h * P + m],
                                            t[0:m, c * ROW_PAIR + h * P:c * ROW_PAIR + (h + 1) * P],
                                            ident[0:m, 0:m])
                    last.then_inc(tabs_turned, 1)
                    n += 1
            pe.wait_ge(tabs_made, len(tables) + 1)
            for c in range(CH):
                pe.transpose(banks[0][0:1, c * P:(c + 1) * P], wmin[:, c:c + 1], ident[:, :])
            pe.matmul(banks[1][0:1, 0:1], small[:, 5:6], ones_f[:, 0:1], start=True, stop=True
                      ).then_inc(wmin_turned, 1)
            pe.wait_ge(win_set, 1)
            pe.wait_ge(tabs_done, n)
            pe.wait_ge(weights_in, 7 * 16)

            def sums(L, i, half):
                g = NG * L + 2 * i + half
                pe.wait_ge(onehot_ready, g + 1)
                wait_count(pe, acc_step, PAIRS * (g - 1) + 1 + L if not isinstance(g, int) or g > 1 else 0)
                for q in range(PAIRS):
                    for k in (2 * q, 2 * q + 1):
                        pe.wait_ge(gath_full[half * GROUP + k], 16 * (IT * L + i + 1))
                    for c in range(DC):
                        for k in (2 * q, 2 * q + 1):
                            last = pe.matmul(WINB[half][:, q * P + c * WIN:q * P + (c + 1) * WIN],
                                             gath[:, half, k, c * P:(c + 1) * P], onehot[:, half, k, :],
                                             start=(k == 2 * q), stop=(k == 2 * q + 1))
                    if q == PAIRS - 1:
                        last.then_inc(groups_done, 1)
                if L == 0:
                    for b in range(2):
                        pe.wait_ge(hist_ready, 2 * g + b + 1)
                        for t in range(4):
                            for s in range(2):
                                last = pe.matmul(HISTB[s][:, 0:NT], oh_lo[:, b, s, t, :], oh_hi[:, b, s, t, :],
                                                 start=isinstance(g, int) and g + b + t == 0,
                                                 stop=isinstance(g, int) and g == NG - 1 and b + t == 4)
                        last.then_inc(hist_done, 1)

            def turn_x(L, i):
                pe.wait_ge(xs_ready, NT * L + i + 1)
                for c in range(DC):
                    last = pe.transpose(TB[:, c * P:(c + 1) * P], xs[:, c * P:(c + 1) * P], ident[:, :])
                last.then_inc(x_turned, 1)

            def prep(L, i, w):
                pe.wait_ge(xT_ready, NT * L + i + 1)
                wait_count(pe, prep_done, NT * L + i)
                for c in range(DC):
                    last = pe.matmul(MB[:, 0:D], xT[:, c, :], w[:, c, :], start=(c == 0), stop=(c == DC - 1))
                last.then_inc(prep_mm, 1)

            def step0(i):
                turn_x(0, i)
                sums(0, i, 0)
                prep(0, i, w0_s)
                sums(0, i, 1)
            step0(0)
            with pe.Fori(1, IT - 1) as i:
                step0(i)
            step0(IT - 1)

            def far_sums(L):
                pe.wait_ge(acc_step, PAIRS * NG * (L + 1) + 1 + L)
                beyond = pe.value_load(flag_s[0:1, 0:1], min_val=0, max_val=ET * P)
                with pe.If(beyond > 0):
                    with pe.Fori(0, ET) as t:
                        spaced_wait(pe, far_gath[L], 16 * (t + 1))
                        with pe.Fori(0, NFAR) as w:
                            pe.wait_ge(far_ready[L], NFAR * t + w + 1)
                            for c in range(DC):
                                last = pe.matmul(WINB[c][:, 0:FARW], far_rows[:, c * P:(c + 1) * P], far_onehot,
                                                 start=True, stop=True)
                            last.then_inc(far_mm[L], 1)

            def product(L, w, c0):
                def body(pair, tiles):
                    for b, i in enumerate(tiles):
                        pe.wait_ge(sums_staged[b], L * ((NT + 1 - b) // 2) + pair + 1)
                        wait_count(pe, x2_ready if L else sums_used, i - 1)
                        for c in range(DC):
                            last = pe.matmul(banks[b][:, 0:D], sums_s[:, b, c, :], w[:, c0 + c, :],
                                             start=(c == 0), stop=(c == DC - 1))
                        last.then_inc(sums_mm, 1)
                return body
            far_sums(0)
            pe.wait_ge(sums_final, 1)
            in_pairs(pe, NT, product(0, w0_s, DC))

            def step1(i):
                turn_x(1, i)
                sums(1, i, 0)
                prep(1, i, wres_s)
                sums(1, i, 1)
            pe.wait_ge(acc_step, PAIRS * NG + 2)
            pe.wait_ge(sums_used, NT)
            step1(0)
            with pe.Fori(1, IT) as i:
                step1(i)

            far_sums(1)
            pe.wait_ge(sums_final, 2)
            pe.wait_ge(route_const, 9)
            agg = product(1, wgc_s, 0)

            def logits(pair, tiles, local):
                for b, i in enumerate(tiles):
                    pe.wait_ge(x2_ready, i + 1)
                    for c in range(DC):
                        last = pe.transpose(banks[2 + b][:, c * P:(c + 1) * P], x2_s[:, b, c * P:(c + 1) * P],
                                            ident[:, :])
                    last.then_inc(x2_turned, 1)
                ahead = [i + 2 for i in tiles]
                agg(pair + 1, [i for i in ahead if not isinstance(i, int) or i < NT])
                for b, i in enumerate(tiles):
                    pe.wait_ge(x2T_ready, i + 1)
                    half, t = local[b] // G, local[b] % G
                    for c in range(DC):
                        last = pe.matmul(banks[4 + half][:, t * NE:(t + 1) * NE], x2T[:, b, c, :], wg_s[:, c, :],
                                         start=(c == 0), stop=(c == DC - 1))
                    last.then_inc(logit_mm, 1)

            def ranks(g, half):
                pe.wait_ge(both_ready, g + 1)
                wait_count(pe, slots_ready, g - 1)
                o = banks[6 + half][:, 0:G * NE].rearrange("p (t e) -> p t e", t=G)
                pe.matmul(o, ones_b, before.unsqueeze(1).to_broadcast([P, G, NE]), start=True, stop=False)
                for t in range(G - 1):
                    pe.matmul(o[:, t + 1:G, :], ones_b, both[:, t:t + 1, :].to_broadcast([P, G - 1 - t, NE]),
                              start=False, stop=False)
                pe.matmul(o, upper, both[:, :, :], start=False, stop=True).then_inc(rank_mm, 1)

            def route(s, groups):
                n = G * len(groups)
                for q in range(0, n, 2):
                    local = [t for t in (q, q + 1) if t < n]
                    if q == 4 and not (isinstance(s, int) and s == 0):
                        ranks(2 * s - 1, 1)
                    if q == G + 5:
                        ranks(2 * s, 0)
                    logits(G * s + q // 2, [2 * G * s + t for t in local], local)
                if len(groups) == 1:
                    ranks(2 * s, 0)
            agg(0, [0, 1])
            in_pairs(pe, NG7, route)

            pe.wait_ge(blk_step, 1)
            pe.matmul(banks[4][0:NE, 0:1], before, ones_b[:, 0:1], start=True, stop=True).then_inc(blk_mm, 1)
            pe.wait_ge(blk_step, 2)
            pe.matmul(banks[5][0:NE, 0:1], upto[0:NE, :], cnt[0:NE, 2:3], start=True, stop=True
                      ).then_inc(blk_mm, 1)
            pe.wait_ge(blk_step, 3)
            pe.matmul(banks[4][0:1, 0:BL], ones_f[0:NE, 0:1], reached[0:NE, :], start=True, stop=True)
            pe.matmul(banks[5][0:1, 0:BL], cnt[0:NE, 2:3], reached[0:NE, :], start=True, stop=True)
            pe.matmul(banks[2][0:1, 0:1], ones_f[0:NE, 0:1], cnt[0:NE, 2:3], start=True, stop=True
                      ).then_inc(blk_mm, 1)

            pe.wait_ge(blocks_ready, 1)
            pairs = pe.value_load(blk_n[0:1, 0:1], min_val=2, max_val=(BL - 8) // 2)

            def turn(blk, n_before, b):
                pe.wait_ge(xg_full[b], 16 * (n_before + 1))
                wait_count(pe, xgT_ready, blk - 1)
                wait_count(pe, b1T_ready, blk - 1)
                for c in range(DC):
                    last = pe.transpose(banks[b][:, c * P:(c + 1) * P], xg_s[:, b, c * P:(c + 1) * P], ident[:, :])
                last.then_inc(xg_turned, 1)

            def product1(blk, n_before, b):
                pe.wait_ge(w1_full[b], 32 * (n_before + 1))
                spaced_wait(pe, xgT_ready, blk + 1)
                pe.transpose(banks[b][:, D:D + HC], b1r_s[0:HC, b, :], ident[0:HC, 0:HC]).then_inc(b1_turned, 1)
                for c in range(HC):
                    wait_count(pe, gelu_done, HC * (blk - 1) + c + 1 if not isinstance(blk, int) or blk > 0 else 0)
                    for d in range(DC):
                        last = pe.matmul(banks[2 + c][:, 0:P], w1_s[:, b, d, c * P:(c + 1) * P],
                                         xgT[:, b, d, :], start=(d == 0), stop=(d == DC - 1))
                    last.then_inc(mm1_done, 1)

            def product2(blk, n_before, b):
                wait_count(pe, yo_ready, blk - 1)
                pe.wait_ge(w2_full[b], 32 * (n_before + 1))
                for c in range(HC):
                    pe.wait_ge(gelu_done, HC * blk + c + 1)
                    last = pe.matmul(banks[6 + b][:, 0:D], hT[:, b, c, :], w2_s[:, b, c, :],
                                     start=(c == 0), stop=(c == HC - 1))
                    if c == HC // 2 - 1:
                        turn(blk + 2, n_before + 1, b)
                last.then_inc(mm2_done, 1)

            turn(0, 0, 0)
            turn(1, 0, 1)
            product1(0, 0, 0)

            def experts(j):
                for b in range(2):
                    blk = 2 * j + b
                    product1(blk + 1, j + b, 1 - b)
                    product2(blk, j, b)
            experts(0)
            with pe.Fori(1, pairs) as j:
                experts(j)

            def col_sums(bank, data, ready, done):
                def body(_, tiles):
                    for b, i in enumerate(tiles):
                        rows = LAST if isinstance(i, int) and i == NT - 1 else P
                        pe.wait_ge(ready, i + 1)
                        pe.matmul(bank[:, 0:D], ones_f[0:rows, :], data(b, i)[0:rows, :],
                                  start=isinstance(i, int) and i == 0, stop=isinstance(i, int) and i == NT - 1
                                  ).then_inc(done, 1)
                return body
            in_sevens(pe, NT, col_sums(banks[0], lambda b, i: Y[:, ds(i, 1), :].rearrange("p a d -> p (a d)"),
                                       yb_added, mean_mm))
            in_sevens(pe, NT, col_sums(banks[1], lambda b, i: sq_s[:, b, :], sq_ready, var_mm))

        @block.vector
        def _(dve):
            steps = [0]

            def link(ins):
                steps[0] += 1
                ins.then_inc(dve_step, 1)
                dve.wait_ge(dve_step, steps[0])

            v = nc.vector
            dve.wait_ge(pads_set, 2)
            dve.wait_ge(edges_in, 6 * 16)
            link(v.tensor_copy(srcF, srcI))
            link(v.tensor_scalar(idxF, srcF, float(N - 1), None, ALU.min))
            dve.sem_inc(tabs_made, 1)
            v.tensor_scalar(loS.bitcast(I32), srcI, P - 1, None, ALU.bitwise_and)
            v.tensor_scalar(loD.bitcast(I32), dstI, P - 1, None, ALU.bitwise_and)
            link(v.tensor_copy(dstF, dstI))
            v.tensor_copy(tmpF, loS.bitcast(I32))
            link(v.tensor_copy(relF, loD.bitcast(I32)))
            v.tensor_tensor(hiS, srcF, tmpF, ALU.subtract)
            v.tensor_tensor(hiD, dstF, relF, ALU.subtract)
            v.tensor_copy(loS, tmpF)
            link(v.tensor_copy(loD, relF))
            link(v.tensor_reduce(wmin, dstF.rearrange("p (c e) -> p c e", c=CH), AX, ALU.min))
            link(v.tensor_scalar(wmin, wmin, float(N - 1), None, ALU.min))
            for c in range(CH):
                last = v.tensor_scalar(relF[:, c * ROW_PAIR:(c + 1) * ROW_PAIR],
                                       dstF[:, c * ROW_PAIR:(c + 1) * ROW_PAIR], wmin[:, c:c + 1], None,
                                       ALU.subtract)
            link(last)
            link(v.tensor_scalar(tmpF, relF, float(WIN), None, ALU.is_ge))
            link(v.scalar_tensor_tensor(farF, dstF, 1.0, tmpF, ALU.add, ALU.mult))
            link(v.tensor_scalar(farF, farF, -1.0, None, ALU.add))
            link(v.scalar_tensor_tensor(tmpF, dstF, float(N), tmpF, ALU.is_lt, ALU.mult))
            link(v.tensor_reduce(small[:, 5:6], tmpF, AX, ALU.add))
            dve.sem_inc(tabs_made, len(tables))
            dve.wait_ge(wmin_turned, 1)
            v.tensor_copy(win_row[0:1, :], banks[0][0:1, 0:NPAIR])
            link(v.tensor_copy(flag_s[:, :], banks[1][0:1, 0:1]))
            dve.sem_inc(win_set, 1)
            dve.wait_ge(tabs_done, len(tables) * CH)
            dve.wait_ge(weights_in, 7 * 16)

            def one_hots(L, i, half):
                g = NG * L + 2 * i + half
                wait_count(dve, groups_done, g - 1)
                v.tensor_tensor(onehot[:, half, :, :],
                                iota_w[:, :].unsqueeze(1).to_broadcast([P, GROUP, WIN]),
                                rel_t[:, ds(2 * GROUP * i + GROUP * half, GROUP)].unsqueeze(2)
                                .to_broadcast([P, GROUP, WIN]), ALU.is_equal).then_inc(onehot_ready, 1)

            def degree_one_hots(i, half):
                g = 2 * i + half
                for b in range(2):
                    wait_count(dve, hist_done, 2 * g + b - 1)
                    for s in range(2):
                        for o, io, w, part in ((oh_lo, iota_lo, P, 0), (oh_hi, iota_hi, NT, 1)):
                            last = v.tensor_tensor(
                                o[:, b, s, :, :], io[:, :].unsqueeze(1).to_broadcast([P, 4, w]),
                                lohi_t[:, 2 * s + part, ds(2 * GROUP * i + GROUP * half + 4 * b, 4)]
                                .unsqueeze(2).to_broadcast([P, 4, w]), ALU.is_equal)
                    last.then_inc(hist_ready, 1)


            def add_windows(L, i, half, last=False):
                g = NG * L + 2 * i + half
                dve.wait_ge(groups_done, g + 1)
                if not last:
                    one_hots(L, i + 1, half)
                if L == 0 and not (last and half == 1):
                    degree_one_hots(i + half, 1 - half)
                first = [dve.value_load(win_row[0:1, ds(2 * PAIRS * i + PAIRS * half + q, 1)],
                                        min_val=0, max_val=N - 1) for q in range(PAIRS)]
                for q in range(PAIRS):
                    dve.wait_ge(acc_step, PAIRS * g + q + 1 + L)
                    a = acc[:, :, bass.ds(first[q], WIN)]
                    v.tensor_tensor(a, a, WINB[half][:, q * P:(q + 1) * P].rearrange(
                        "p (c w) -> p c w", c=DC), ALU.add).then_inc(acc_step, 1)

            one_hots(0, 0, 0)
            degree_one_hots(0, 0)
            one_hots(0, 0, 1)

            def step0(i, last=False):
                add_windows(0, i, 0, last)
                dve.wait_ge(prep_mm, i + 1)
                v.tensor_copy(Y[:, ds(i, 1), :], MB[:, 0:D].unsqueeze(1))
                v.tensor_tensor(X[:, ds(i, 1), :], X[:, ds(i, 1), :], bias_s[:, :].unsqueeze(1),
                                ALU.add).then_inc(prep_done, 1)
                add_windows(0, i, 1, last)
            step0(0)
            with dve.Fori(1, IT - 1) as i:
                step0(i)
            step0(IT - 1, True)

            def far_windows(L):
                dve.wait_ge(acc_step, PAIRS * NG * (L + 1) + 1 + L)
                beyond = dve.value_load(flag_s[0:1, 0:1], min_val=0, max_val=ET * P)
                with dve.If(beyond > 0):
                    dve.wait_ge(far_const, L + 1)
                    with dve.Fori(0, ET) as t:
                        v.tensor_copy(far_idx, idx_t[:, bass.ds(t, 1)])
                        v.tensor_copy(far_dst, far_t[:, bass.ds(t, 1)]).then_inc(far_step[L], 1)
                        spaced_wait(dve, far_step[L], (NFAR + 1) * t + 1)
                        dve.sem_inc(far_taken[L], 1)
                        with dve.Fori(0, NFAR) as w:
                            v.tensor_scalar(far_onehot, iota_far, far_dst, None, ALU.is_equal
                                            ).then_inc(far_ready[L], 1)
                            dve.wait_ge(far_mm[L], NFAR * t + w + 1)
                            v.tensor_scalar(far_dst, far_dst, float(-FARW), None, ALU.add)
                            for c in range(DC):
                                a = acc[:, c, bass.ds(FARW * w, FARW)]
                                last = v.tensor_tensor(a, a, WINB[c][:, 0:FARW], ALU.add)
                            last.then_inc(far_step[L], 1)
                            spaced_wait(dve, far_step[L], (NFAR + 1) * t + w + 2)
                dve.sem_inc(sums_final, 1)
            far_windows(0)

            dve.wait_ge(hist_done, 2 * NG)
            v.tensor_scalar(rdeg[:, DEG_IN, :], HISTB[1][:, 0:NT], 1.0, None, ALU.max)
            link(v.tensor_scalar(rdeg[:, DEG_OUT, :], HISTB[0][:, 0:NT], 1.0, None, ALU.max))
            v.reciprocal(rdeg[:, R_IN, :], rdeg[:, DEG_IN, :])
            link(v.reciprocal(rdeg[:, TMP, :], rdeg[:, DEG_OUT, :]))
            dve.sem_inc(deg_ready, 1)

            def combine(_, tiles):
                for b, i in enumerate(tiles):
                    dve.wait_ge(sums_mm, i + 1)
                    yi = Y[:, ds(i, 1), :].rearrange("p a d -> p (a d)")
                    v.scalar_tensor_tensor(yi, banks[b][:, 0:D], rdeg[:, R_IN, ds(i, 1)], yi, ALU.mult, ALU.add
                                           ).then_inc(sums_used, 1)
            def residual(tiles):
                for b, i in enumerate(tiles):
                    xi = X[:, ds(i, 1), :].rearrange("p a d -> p (a d)")
                    v.scalar_tensor_tensor(xi, Y[:, ds(i, 1), :].rearrange("p a d -> p (a d)"),
                                           row_t[:, RN, ds(i, 1)], xi, ALU.mult, ALU.add).then_inc(raw_ready, 1)
                for b, i in enumerate(tiles):
                    spaced_wait(dve, raw_ready, i + 1)
                    v.bn_stats(stats[:, ds(i, 1), :].rearrange("p a s -> p (a s)"),
                               X[:, ds(i, 1), :].rearrange("p a d -> p (a d)")).then_inc(stats_done, 1)

            def norms(s, n):
                spaced_wait(dve, norms_done, s + 1)
                rn = row_t[:, RN, ds(2 * G * s, n)]
                v.reciprocal(rn, rn).then_inc(norms_ready, 1)
                spaced_wait(dve, norms_ready, s + 1)

            def combine_and_finish(s, groups):
                n = G * len(groups)
                for q in range(0, n, 2):
                    combine(q, [2 * G * s + t for t in (q, q + 1) if t < n])
                    if not (isinstance(s, int) and s == 0):
                        if q == 0:
                            norms(s - 1, 2 * G)
                        residual([2 * G * (s - 1) + q, 2 * G * (s - 1) + q + 1])
            in_pairs(dve, NG7, combine_and_finish)
            left = NG7 // 2
            for i in range(2 * G * (left - 1) + G + 1, 2 * G * left, 2):
                residual([i, i + 1])
            norms(left, G)
            residual(list(range(2 * G * left, NT)))
            dve.wait_ge(stats_done, NT)

            def row_norm(roots):
                me, ve, mo, vo = (stats[:, :, k] for k in (1, 2, 4, 5))
                v.tensor_tensor(row_t[:, SUM, :], me, mo, ALU.add)
                v.tensor_tensor(row_t[:, VAR, :], ve, vo, ALU.add)
                link(v.tensor_tensor(row_t[:, DIFF, :], me, mo, ALU.subtract))
                link(v.tensor_tensor(row_t[:, DIFF, :], row_t[:, DIFF, :], row_t[:, DIFF, :], ALU.mult))
                link(v.scalar_tensor_tensor(row_t[:, VAR, :], row_t[:, DIFF, :], D / 4.0, row_t[:, VAR, :],
                                            ALU.mult, ALU.add))
                link(v.tensor_scalar(row_t[:, VAR, :], row_t[:, VAR, :], 1.0 / D, LN_EPS, ALU.mult, ALU.add))
                dve.sem_inc(rsqrt_asked, 1)
                dve.wait_ge(sqrt_done, roots)
                link(v.reciprocal(row_t[:, RSTD, :], row_t[:, RSTD, :]))
                link(v.scalar_tensor_tensor(row_t[:, NMR, :], row_t[:, SUM, :], -0.5, row_t[:, RSTD, :],
                                            ALU.mult, ALU.mult))
            row_norm(2)

            def norm_x(_, tiles):
                for b, i in enumerate(tiles):
                    xi = X[:, ds(i, 1), :].rearrange("p a d -> p (a d)")
                    v.tensor_scalar(xi, xi, row_t[:, RSTD, ds(i, 1)], row_t[:, NMR, ds(i, 1)], ALU.mult, ALU.add
                                    ).then_inc(x1_ready, 1)
            in_sevens(dve, NT, norm_x)
            dve.wait_ge(bias1_in, 16)
            link(v.tensor_tensor(bias_s[:, :], bias_s[:, :], bias2_s[:, :], ALU.add))

            def step1(i, last=False):
                add_windows(1, i, 0, last)
                dve.wait_ge(prep_mm, NT + i + 1)
                v.tensor_tensor(Y[:, ds(i, 1), :], MB[:, 0:D].unsqueeze(1), bias_s[:, :].unsqueeze(1),
                                ALU.add).then_inc(prep_done, 1)
                add_windows(1, i, 1, last)
            one_hots(1, 0, 0)
            one_hots(1, 0, 1)
            step1(0)
            with dve.Fori(1, IT - 1) as i:
                step1(i)
            step1(IT - 1, True)

            far_windows(1)

            dve.wait_ge(route_const, 9)
            STEPS = 13

            def make_x2(tiles):
                for b, i in enumerate(tiles):
                    dve.wait_ge(sums_mm, NT + i + 1)
                    wait_count(dve, x2_turned, i - 1)
                    wait_count(dve, x2_kept, i - 1)
                    v.scalar_tensor_tensor(x2_s[:, b, :], banks[b][:, 0:D], rdeg[:, RS_IN, ds(i, 1)],
                                           Y[:, ds(i, 1), :].rearrange("p a d -> p (a d)"), ALU.mult, ALU.add
                                           ).then_inc(x2_ready, 1)

            def step(g, n, ins, spaced=False):
                ins.then_inc(route_step, 1)
                (spaced_wait if spaced else wait_count)(dve, route_step, STEPS * g + n)

            def choose(g, half):
                dve.wait_ge(logit_mm, G * (g + 1))
                step(g, 1, v.tensor_tensor(
                    logit, banks[4 + half][:, 0:G * NE].rearrange("p (t e) -> p t e", t=G),
                    bg_s[:, :].unsqueeze(1).to_broadcast([P, G, NE]), ALU.add), spaced=True)
                for t in range(G):
                    last = v.max(top8[:, t, :], logit[:, t, :])
                step(g, 2, last, spaced=True)
                for t in range(G):
                    last = v.max_index(top8i[:, t, :], top8[:, t, :], logit[:, t, :])
                step(g, 3, last)

            def mark(g):
                step(g, 4, v.tensor_copy(top2f.rearrange("p (t k) -> p t k", k=2), top8i[:, :, 0:2]))
                step(g, 5, v.tensor_tensor(pick.rearrange("p t k e -> p (t k) e"),
                                           iota_e.unsqueeze(1).to_broadcast([P, 2 * G, NE]),
                                           top2f.unsqueeze(2).to_broadcast([P, 2 * G, NE]), ALU.is_equal))
                v.tensor_copy(vals_t[:, ds(G * g, G), :], top8[:, :, 0:2])
                if isinstance(g, int) and g == NG7 - 1:
                    v.tensor_tensor(both[:, 0:G - 1, :], pick[:, 0:G - 1, 0, :], pick[:, 0:G - 1, 1, :], ALU.add)
                    step(g, 6, v.memset(both[:, G - 1, :], 0.0))
                    step(g, 7, v.tensor_tensor(both[0:LAST, G - 1, :], pick[0:LAST, G - 1, 0, :],
                                               pick[0:LAST, G - 1, 1, :], ALU.add))
                else:
                    dve.sem_inc(route_step, 1)
                    step(g, 7, v.tensor_tensor(both, pick[:, :, 0, :], pick[:, :, 1, :], ALU.add))
                dve.sem_inc(both_ready, 1)

            def place(s, g, half):
                dve.wait_ge(rank_mm, g + 1)
                o = banks[6 + half][:, 0:G * NE].rearrange("p (t e) -> p t e", t=G)
                for k in range(2):
                    last = v.tensor_tensor(prod[:, :, k, :], pick[:, :, k, :], o, ALU.mult)
                step(g, 8, last)
                step(g, 9, v.tensor_reduce(rank, prod.rearrange("p t k e -> p (t k) e"), AX, ALU.add))
                v.tensor_reduce(both_sum, both.rearrange("p t e -> p e t"), AX, ALU.add)
                v.scalar_tensor_tensor(slotf, top2f, float(CAP), rank, ALU.mult, ALU.add)
                step(g, 10, v.tensor_scalar(overf, rank, float(CAP), float(OVER), ALU.is_ge, ALU.mult))
                step(g, 11, v.tensor_tensor(before, before, both_sum, ALU.add))
                spaced_wait(dve, slots_stored[half], 32 * G * s)
                v.tensor_copy(ids_s[:, half, :, :], ids_t[:, ds(G * g, G), :]).then_inc(route_step, 1)
                step(g, 13, v.tensor_tensor(slot_s[:, half, :, :].rearrange("p t k -> p (t k)"), slotf, overf,
                                            ALU.add))
                dve.sem_inc(slots_ready, 1)

            def route(s, groups):
                n = G * len(groups)
                for q in range(0, n, 2):
                    make_x2([2 * G * s + t for t in (q, q + 1) if t < n])
                    if not (isinstance(s, int) and s == 0):
                        if q == 0:
                            choose(2 * s - 1, 1)
                        if q == 2:
                            mark(2 * s - 1)
                        if q == 4:
                            place(s - 1, 2 * s - 1, 1)
                    if q == G + 1:
                        choose(2 * s, 0)
                    if q == G + 3:
                        mark(2 * s)
                    if q == G + 5:
                        place(s, 2 * s, 0)
                if len(groups) == 1:
                    choose(2 * s, 0)
                    mark(2 * s)
                    place(s, 2 * s, 0)
            in_pairs(dve, NG7, route)
            dve.sem_inc(blk_step, 1)

            link(v.tensor_tensor(vals_t[:, :, 1:2], vals_t[:, :, 1:2], vals_t[:, :, 0:1], ALU.subtract))
            dve.sem_inc(rsqrt_asked, 1)
            dve.wait_ge(blk_mm, 1)
            link(v.tensor_scalar(cnt[0:NE, 0:1], banks[4][0:NE, 0:1], float(CAP), float(P - 1), ALU.min, ALU.add))
            link(v.tensor_copy(cnt[0:NE, 1:2].bitcast(I32), cnt[0:NE, 0:1]))
            link(v.tensor_scalar(cnt[0:NE, 1:2].bitcast(I32), cnt[0:NE, 1:2].bitcast(I32), 7, None,
                                 ALU.arith_shift_right))
            link(v.tensor_copy(cnt[0:NE, 2:3], cnt[0:NE, 1:2].bitcast(I32)))
            dve.sem_inc(blk_step, 1)
            dve.wait_ge(blk_mm, 2)
            link(v.tensor_copy(cnt[0:NE, 3:4], banks[5][0:NE, 0:1]))
            link(v.tensor_scalar(reached[0:NE, :], iota_b[0:NE, :], cnt[0:NE, 3:4], None, ALU.is_ge))
            dve.sem_inc(blk_step, 1)
            dve.wait_ge(blk_mm, 3)
            ex, pre = banks[4][0:1, 0:BL], banks[5][0:1, 0:BL]
            v.tensor_scalar(blk_e[:, :], ex, float(NE - 1), None, ALU.min)
            link(v.tensor_scalar(blk_row[0:1, 0, :], ex, float(CAP), None, ALU.mult))
            link(v.tensor_tensor(blk_row[0:1, 1, :], iota_b[0:1, :], pre, ALU.subtract))
            link(v.scalar_tensor_tensor(blk_row[0:1, 2, :], blk_row[0:1, 1, :], float(P), blk_row[0:1, 0, :],
                                        ALU.mult, ALU.add))
            link(v.tensor_scalar(blk_s[:, :], blk_row[0:1, 2, :], float(SLOTS), None, ALU.min))
            v.tensor_copy(blk_row[0:1, 3, :], ex)
            link(v.tensor_copy(cnt[0:1, 6:7], banks[2][0:1, 0:1]))
            link(v.tensor_tensor(blk_row[0:1, 1, 2:BL], blk_row[0:1, 3, 2:BL], blk_row[0:1, 3, 0:BL - 2],
                                 ALU.not_equal))
            link(v.tensor_scalar(blk_row[0:1, 0, :], iota_b[0:1, :], cnt[0:1, 6:7], None, ALU.is_lt))
            link(v.tensor_tensor(blk_new[:, 2:BL], blk_row[0:1, 1, 2:BL], blk_row[0:1, 0, 2:BL], ALU.mult))
            link(v.tensor_scalar(cnt[0:1, 4:5], banks[2][0:1, 0:1], 3.0, 1.0, ALU.max, ALU.add))
            link(v.tensor_copy(cnt[0:1, 5:6].bitcast(I32), cnt[0:1, 4:5]))
            link(v.tensor_scalar(blk_n[:, :], cnt[0:1, 5:6].bitcast(I32), 1, None, ALU.arith_shift_right))
            dve.sem_inc(blocks_ready, 1)
            dve.wait_ge(sqrt_done, 3)
            link(v.tensor_scalar(vals_t[:, :, 0:1], vals_t[:, :, 1:2], 1.0, None, ALU.add))
            link(v.reciprocal(vals_t[:, :, 0:1], vals_t[:, :, 0:1]))
            link(v.tensor_tensor(vals_t[:, :, 1:2], vals_t[:, :, 1:2], vals_t[:, :, 0:1], ALU.mult))

            pairs = dve.value_load(blk_n[0:1, 0:1], min_val=2, max_val=(BL - 8) // 2)

            def row_ids(blk, n_before, b):
                dve.wait_ge(bid_full[b], 16 * (n_before + 1))
                spaced_wait(dve, xg_turned, blk - 1)
                v.tensor_scalar(tmp_s[:, 0:1], bids_all[:, ds(blk, 1)], float(N), float(-N), ALU.is_ge, ALU.mult
                                ).then_inc(gid_step, 1)
                spaced_wait(dve, gid_step, 3 * blk + 1)
                v.tensor_tensor(tmp_s[:, 1:2], bids_all[:, ds(blk, 1)], tmp_s[:, 0:1], ALU.add).then_inc(gid_step, 1)
                dve.wait_ge(gid_step, 3 * blk + 2)
                v.tensor_scalar(gid_s[:, b:b + 1], tmp_s[:, 1:2], float(N - 1), None, ALU.min).then_inc(gid_step, 1)

            def copy_xT(blk, b):
                dve.wait_ge(xg_turned, blk + 1)
                wait_count(dve, mm1_done, HC * (blk - 1) if not isinstance(blk, int) or blk > 1 else 0)
                v.tensor_copy(xgT[:, b, :, :], banks[b][:, 0:D].rearrange("p (c n) -> p c n", c=DC)
                              ).then_inc(xgT_ready, 1)

            def copy_b1(blk, b):
                dve.wait_ge(b1_turned, blk + 1)
                wait_count(dve, gelu_done, HC * (blk - 1) if not isinstance(blk, int) or blk > 1 else 0)
                v.tensor_copy(b1T[:, b, :], banks[b][:, D:D + HC]).then_inc(b1T_ready, 1)

            def blocks(j):
                for b in range(2):
                    blk = 2 * j + b
                    row_ids(blk + 3, j + 1 + b, 1 - b)
                    copy_b1(blk + 1, 1 - b)
                    copy_xT(blk + 2, b)
                    spaced_wait(dve, yo_stored[b], 16 * j)
                    v.tensor_copy(bids_s[:, b:b + 1], bids_all[:, ds(blk, 1)])
                    dve.wait_ge(mm2_done, blk + 1)
                    v.tensor_tensor(yo_s[:, b, :], banks[6 + b][:, 0:D], b2_s[:, b, :], ALU.add
                                    ).then_inc(yo_ready, 1)

            row_ids(0, 0, 0)
            row_ids(1, 0, 1)
            copy_xT(0, 0)
            copy_xT(1, 1)
            row_ids(2, 1, 0)
            copy_b1(0, 0)
            blocks(0)
            with dve.Fori(1, pairs) as j:
                blocks(j)

            def add_experts(group, tiles):
                for first, n, _, k in parts(tiles):
                    dve.wait_ge(y_full[k], 32 * (group + 1 if k < 3 else 1))
                    for which, y_s, before_it, done in ((0, ya_s, None, ya_added), (1, yb_s, ya_added, yb_added)):
                        for b in range(first, first + n):
                            i = tiles[b]
                            yi = Y[:, ds(i, 1), :].rearrange("p a d -> p (a d)")
                            if before_it:
                                dve.wait_ge(before_it, i + 1)
                            v.scalar_tensor_tensor(yi, y_s[:, b, :],
                                                   vals_t[:, ds(i, 1), which:which + 1].rearrange("p a b -> p (a b)"),
                                                   yi, ALU.mult, ALU.add).then_inc(done, 1)
            in_sevens(dve, NT, add_experts)

            dve.wait_ge(mean_mm, NT)
            link(v.tensor_scalar(mean_s, banks[0][:, 0:D], 1.0 / N, None, ALU.mult))

            def centre(_, tiles):
                for b, i in enumerate(tiles):
                    v.tensor_tensor(Y[:, ds(i, 1), :], Y[:, ds(i, 1), :], mean_s.unsqueeze(1), ALU.subtract
                                    ).then_inc(centred, 1)
            in_sevens(dve, NT, centre)
            dve.wait_ge(var_mm, NT)
            link(v.tensor_scalar(bn_s[:, 0, :], banks[1][:, 0:D], 1.0 / N, BN_EPS, ALU.mult, ALU.add))
            dve.sem_inc(rsqrt_asked, 1)
            dve.wait_ge(sqrt_done, 4)
            link(v.reciprocal(bn_s[:, 1, :], bn_s[:, 1, :]))
            dve.wait_ge(last_in, 32)
            link(v.tensor_tensor(scale_s, bn_s[:, 1, :], bias2_s[:, :], ALU.mult))
            dve.sem_inc(scale_ready, 1)

            def final_sum(group, tiles):
                own = SEVEN - BY_POOL
                for i in tiles[BY_POOL:]:
                    v.tensor_tensor(Y[:, ds(i, 1), :], Y[:, ds(i, 1), :], scale_s.unsqueeze(1), ALU.mult
                                    ).then_inc(own_scaled, 1)
                for b, i in enumerate(tiles):
                    dve.wait_ge(beta_added, i + 1)
                    if b < BY_POOL:
                        dve.wait_ge(scaled, BY_POOL * group + b + 1)
                    else:
                        dve.wait_ge(own_scaled, own * group + b - BY_POOL + 1)
                    v.tensor_tensor(X[:, ds(i, 1), :], X[:, ds(i, 1), :], Y[:, ds(i, 1), :], ALU.add
                                    ).then_inc(summed, 1)
                for b, i in enumerate(tiles):
                    spaced_wait(dve, summed, i + 1)
                    v.bn_stats(stats[:, ds(i, 1), :].rearrange("p a s -> p (a s)"),
                               X[:, ds(i, 1), :].rearrange("p a d -> p (a d)")).then_inc(stats2, 1)
            in_sevens(dve, NT, final_sum)
            dve.wait_ge(stats2, NT)
            row_norm(5)

            def norm_out(p, tiles):
                for b, i in enumerate(tiles):
                    xi = X[:, ds(i, 1), :].rearrange("p a d -> p (a d)")
                    v.tensor_scalar(xi, xi,
                                    row_t[:, RSTD, ds(i, 1)], row_t[:, NMR, ds(i, 1)], ALU.mult, ALU.add
                                    ).then_inc(out_ready, 1)
            in_sevens(dve, NT, norm_out)


_INS = ['x', 'src', 'dst', 'L0_gnn_weight', 'L0_gnn_bias', 'L1_gnn_W_gc', 'L1_gnn_b_gc', 'L1_gnn_W_res',
        'L1_gnn_b_res', 'L1_gnn_Wg', 'L1_gnn_bg', 'L1_gnn_w1', 'L1_gnn_b1', 'L1_gnn_w2', 'L1_gnn_b2',
        'L1_gnn_gamma', 'L1_gnn_beta']
_OUTS = [((6250, 256), 'float32')]


def kernel(**inputs):
    import numpy as _np
    import concourse.bacc as _bacc
    from concourse import mybir as _mybir
    from concourse.bass_utils import run_bass_kernel_spmd as _run

    nc = _bacc.Bacc("TRN2", target_bir_lowering=False, num_devices=1)
    arrays, args = {}, []
    for name in _INS:
        a = _np.ascontiguousarray(inputs[name])
        arrays[f"in_{name}_dram"] = a
        args.append(nc.dram_tensor(f"in_{name}_dram", a.shape, _mybir.dt.from_np(a.dtype), kind="ExternalInput").ap())
    for i, (shape, dtype) in enumerate(_OUTS):
        dt = _mybir.dt.from_np(_np.dtype(dtype))
        args.append(nc.dram_tensor(f"out_{i}_dram", shape, dt, kind="ExternalOutput").ap())
    gnn_kernel(nc, *args)
    r = _run(nc, [arrays], core_ids=[0])
    got = tuple(r.results[0][f"out_{i}_dram"] for i in range(len(_OUTS)))
    return got[0]
```
